# Optimizing a Trainium2 kernel written in Bass

```python
import numpy as np
import jax
import jax.numpy as jnp

def _softmax(x, axis=-1):
    return jax.nn.softmax(x, axis=axis)

def _gelu(x):
    return jax.nn.gelu(x, approximate=True)

def _silu(x):
    return jax.nn.silu(x)

def _sigmoid(x):
    return jax.nn.sigmoid(x)

def _layernorm(x, axis=-1, eps=1e-05):
    m = jnp.mean(x, axis=axis, keepdims=True)
    v = jnp.var(x, axis=axis, keepdims=True)
    return (x - m) / jnp.sqrt(v + eps)

def _scatter_add(tgt, idx, src, axis=0):
    return tgt.at[idx].add(src)

def _segment_sum(src, seg, n):
    return jax.ops.segment_sum(src, seg, n)
kernel_name = 'mk_adj_resnorm_d2_adj_r2_5c8205'

def setup_inputs(seed: int=0):
    np.random.seed(seed)
    _w = jnp.asarray

    def _rec_inputs():
        import jax
        import jax.numpy as jnp
        _gk = jax.random.key(seed)
        x = -0.0005207 + 1.001 * jax.random.normal(jax.random.fold_in(_gk, 1), (2048, 256), jnp.float32)
        _w = (1.0 + jnp.arange(2048, dtype=jnp.float32)) ** (-0.5)
        _w = _w / _w.mean()
        _pij = jnp.clip(0.000976562 * _w[:, None] * _w[None, :], 0.0, 1.0)
        _a = jax.random.uniform(jax.random.fold_in(_gk, 2), (2048, 2048)) < _pij
        adj = _a.astype(jnp.int32)
        _nm = jnp.ones((2048,), dtype=bool)
        nodemask = jnp.where(_nm, 1.0, 0.0).astype(jnp.int32)
        return (x, adj, nodemask)
    x, adj, nodemask = _rec_inputs()

    def _L0_gnn_setup():
        import jax, jax.numpy as jnp
        import numpy as np
        D = 256
        H = 8
        HD = D // H
        EPS = 1e-05
        NEG = -1e+30

        def layer_norm(x, scale, bias):
            mu = jnp.mean(x, axis=-1, keepdims=True)
            var = jnp.mean(jnp.square(x - mu), axis=-1, keepdims=True)
            return (x - mu) * jax.lax.rsqrt(var + EPS) * scale + bias
        key = jax.random.key(seed)
        ks = jax.random.split(key, 16)
        S = T = 2048
        inp = {'h_source': jax.random.normal(ks[0], (S, D), jnp.float32), 'h_target': jax.random.normal(ks[1], (T, D), jnp.float32), 'edge_mask': jax.random.randint(ks[2], (T, S), 0, 2, jnp.int32), 'source_mask': jnp.ones((S,), jnp.int32), 'target_mask': jnp.ones((T,), jnp.int32), 'ln1_scale': jnp.ones((D,), jnp.float32), 'ln1_bias': jnp.zeros((D,), jnp.float32), 'Wq': jax.random.normal(ks[3], (D, D), jnp.float32) / np.sqrt(D), 'bq': jnp.zeros((D,), jnp.float32), 'Wk': jax.random.normal(ks[4], (D, D), jnp.float32) / np.sqrt(D), 'bk': jnp.zeros((D,), jnp.float32), 'Wv': jax.random.normal(ks[5], (D, D), jnp.float32) / np.sqrt(D), 'bv': jnp.zeros((D,), jnp.float32), 'Wo': jax.random.normal(ks[6], (D, D), jnp.float32) / np.sqrt(D), 'bo': jnp.zeros((D,), jnp.float32), 'ln2_scale': jnp.ones((D,), jnp.float32), 'ln2_bias': jnp.zeros((D,), jnp.float32), 'W1': jax.random.normal(ks[7], (D, 4 * D), jnp.float32) / np.sqrt(D), 'W2': jax.random.normal(ks[8], (4 * D, D), jnp.float32) / np.sqrt(4 * D)}
        return inp
    _L0_gnn_all = _L0_gnn_setup()
    _L0_gnn_in = {k: v for k, v in _L0_gnn_all.items() if k in ('h_target', 'ln1_scale', 'ln1_bias', 'Wq', 'bq', 'Wk', 'bk', 'Wv', 'bv', 'Wo', 'bo', 'ln2_scale', 'ln2_bias', 'W1', 'W2')}
    del _L0_gnn_all

    def _L1_gnn_setup():
        import jax, jax.numpy as jnp
        import numpy as np
        B, IN_F, OUT_F, H = (1024, 256, 256, 8)
        D = OUT_F // H
        key = jax.random.key(seed)
        ks = jax.random.split(key, 4)
        x = jax.random.normal(ks[0], (B, IN_F), dtype=jnp.float32)
        W_w = jax.random.normal(ks[1], (OUT_F, IN_F), dtype=jnp.float32) * (1.0 / np.sqrt(IN_F))
        W_b = jnp.zeros((OUT_F,), dtype=jnp.float32)
        a = jax.random.normal(ks[2], (2 * D, 1), dtype=jnp.float32) * 0.1
        adj = jax.random.randint(ks[3], (B, B), 0, 2, dtype=jnp.int32)
        return {'x': x, 'adj': adj, 'W_w': W_w, 'W_b': W_b, 'a': a}
    _L1_gnn_all = _L1_gnn_setup()
    _L1_gnn_in = {k: v for k, v in _L1_gnn_all.items() if k in ('W_w', 'W_b', 'a')}
    del _L1_gnn_all
    return {'x': x, 'adj': adj, 'nodemask': nodemask, 'L0_gnn_h_target': _L0_gnn_in['h_target'], 'L0_gnn_ln1_scale': _L0_gnn_in['ln1_scale'], 'L0_gnn_ln1_bias': _L0_gnn_in['ln1_bias'], 'L0_gnn_Wq': _L0_gnn_in['Wq'], 'L0_gnn_bq': _L0_gnn_in['bq'], 'L0_gnn_Wk': _L0_gnn_in['Wk'], 'L0_gnn_bk': _L0_gnn_in['bk'], 'L0_gnn_Wv': _L0_gnn_in['Wv'], 'L0_gnn_bv': _L0_gnn_in['bv'], 'L0_gnn_Wo': _L0_gnn_in['Wo'], 'L0_gnn_bo': _L0_gnn_in['bo'], 'L0_gnn_ln2_scale': _L0_gnn_in['ln2_scale'], 'L0_gnn_ln2_bias': _L0_gnn_in['ln2_bias'], 'L0_gnn_W1': _L0_gnn_in['W1'], 'L0_gnn_W2': _L0_gnn_in['W2'], 'L1_gnn_W_w': _L1_gnn_in['W_w'], 'L1_gnn_W_b': _L1_gnn_in['W_b'], 'L1_gnn_a': _L1_gnn_in['a']}

def reference(x, adj, nodemask, L0_gnn_h_target, L0_gnn_ln1_scale, L0_gnn_ln1_bias, L0_gnn_Wq, L0_gnn_bq, L0_gnn_Wk, L0_gnn_bk, L0_gnn_Wv, L0_gnn_bv, L0_gnn_Wo, L0_gnn_bo, L0_gnn_ln2_scale, L0_gnn_ln2_bias, L0_gnn_W1, L0_gnn_W2, L1_gnn_W_w, L1_gnn_W_b, L1_gnn_a):
    import jax
    import jax.numpy as jnp

    def _L0_gnn_ref(h_source, h_target, edge_mask, source_mask, target_mask, ln1_scale, ln1_bias, Wq, bq, Wk, bk, Wv, bv, Wo, bo, ln2_scale, ln2_bias, W1, W2):
        import jax, jax.numpy as jnp
        import numpy as np
        D = 256
        H = 8
        HD = D // H
        EPS = 1e-05
        NEG = -1e+30

        def layer_norm(x, scale, bias):
            mu = jnp.mean(x, axis=-1, keepdims=True)
            var = jnp.mean(jnp.square(x - mu), axis=-1, keepdims=True)
            return (x - mu) * jax.lax.rsqrt(var + EPS) * scale + bias
        smask = (source_mask == 1)[:, None]
        tmask = (target_mask == 1)[:, None]
        hs = layer_norm(h_source, ln1_scale, ln1_bias)
        ht = layer_norm(h_target, ln1_scale, ln1_bias)
        hs = jnp.where(smask, hs, 0.0)
        ht = jnp.where(tmask, ht, 0.0)
        T, S = (ht.shape[0], hs.shape[0])
        q = (ht @ Wq + bq).reshape(T, H, HD) / jnp.sqrt(jnp.float32(HD))
        k = (hs @ Wk + bk).reshape(S, H, HD)
        v = (hs @ Wv + bv).reshape(S, H, HD)
        logits = jnp.einsum('thd,shd->hts', q, k)
        logits = jnp.where(edge_mask[None] != 0, logits, NEG)
        probs = jax.nn.softmax(logits, axis=-1)
        ctx = jnp.einsum('hts,shd->thd', probs, v).reshape(T, D)
        attn = ctx @ Wo + bo
        attn = jnp.where(tmask, attn, 0.0)
        ht = ht + attn
        ht = layer_norm(ht, ln2_scale, ln2_bias)
        ht = jnp.where(tmask, ht, 0.0)
        ff = jax.nn.gelu(ht @ W1) @ W2
        return ht + ff

    def _L1_gnn_ref(x, adj, W_w, W_b, a):
        import jax, jax.numpy as jnp
        import numpy as np
        B, IN_F, OUT_F, H = (1024, 256, 256, 8)
        D = OUT_F // H
        Bn = x.shape[0]
        h = (x @ W_w.T + W_b).reshape(Bn, H, D)
        a_src, a_dst = (a[:D, 0], a[D:, 0])
        s_src = jnp.einsum('bhd,d->bh', h, a_src)
        s_dst = jnp.einsum('bhd,d->bh', h, a_dst)
        e = jax.nn.leaky_relu(s_src[:, None, :] + s_dst[None, :, :], negative_slope=0.2)
        e = jnp.where(adj[:, :, None] == 0, jnp.float32(-1000000000.0), e)
        attn = jax.nn.softmax(e, axis=1)
        h_prime = jnp.einsum('ijh,jhd->ihd', attn, h).reshape(Bn, H * D)
        return jax.nn.elu(h_prime)
    x = _layernorm(x + _L0_gnn_ref(x, L0_gnn_h_target, adj, nodemask, nodemask, L0_gnn_ln1_scale, L0_gnn_ln1_bias, L0_gnn_Wq, L0_gnn_bq, L0_gnn_Wk, L0_gnn_bk, L0_gnn_Wv, L0_gnn_bv, L0_gnn_Wo, L0_gnn_bo, L0_gnn_ln2_scale, L0_gnn_ln2_bias, L0_gnn_W1, L0_gnn_W2), axis=-1)
    x = _layernorm(x + _L1_gnn_ref(x, adj, L1_gnn_W_w, L1_gnn_W_b, L1_gnn_a), axis=-1)
    return x

_drawn_inputs = setup_inputs


def setup_inputs(seed=0):
    import zlib

    import numpy as np

    out = dict(_drawn_inputs(seed))
    spreads = {'L0_gnn_ln1_scale': (1.0, 0.2),
     'L0_gnn_ln1_bias': (0.0, 0.1),
     'L0_gnn_bq': (0.0, 0.595),
     'L0_gnn_bk': (0.0, 0.8),
     'L0_gnn_bv': (0.0, 0.1),
     'L0_gnn_bo': (0.0, 0.1),
     'L0_gnn_ln2_scale': (1.0, 0.2),
     'L0_gnn_ln2_bias': (0.0, 0.1),
     'L1_gnn_W_b': (0.0, 0.1)}
    factors = {}
    for name, (base, spread) in spreads.items():
        noise = np.random.default_rng([zlib.crc32(name.encode()), seed]).standard_normal(out[name].shape)
        drawn = base * np.exp(spread * noise) if base else spread * noise
        out[name] = jnp.asarray(drawn.astype(out[name].dtype))
    for name, factor in factors.items():
        out[name] = (out[name] * factor).astype(out[name].dtype)
    return out
```

```python
import concourse.bass as bass
from concourse import mybir
from contextlib import ExitStack

P = 128
N = 2048
D = 256
H = 8
HD = D // H
NT = N // P
NC = D // P
FF = 4 * D
NF = FF // P
VW = HD + 1
NU = NT * NT
NS = 2 * H
EPS = 1e-5
NEG = -1e30
EMPTY = -1e29
SLOPE = 0.2
AR = 4


def build(nc, ln1_sc, ln1_bc, bqc_d, Wbc, x, h_target, adj_s, nodemask, ln1_s, ln1_b, Wq, Wk, bk, Wv, bv, Wo, bo,
          ln2_s, ln2_b, W1, W2, Ww, WwT, Wb, att_a, out):
    f32, bf16, i32 = mybir.dt.float32, mybir.dt.bfloat16, mybir.dt.int32
    ALU, ACT, AX = mybir.AluOpType, mybir.ActivationFunctionType, mybir.AxisListType
    ds = bass.ds

    with ExitStack() as ctx:
        def sb(name, shape, dt=f32):
            return ctx.enter_context(nc.sbuf_tensor(name, shape, dt))

        def pb(name, shape):
            return ctx.enter_context(nc.psum_tensor(name, shape, f32))

        def sem(name):
            return ctx.enter_context(nc.semaphore(name))

        xs = sb("xs", [P, NT, D])
        ht = sb("ht", [P, NT, D])
        krows = sb("krows", [P, NT, D])
        vrows = sb("vrows", [P, NT, H * VW])
        qT = sb("qT", [P, NT, NC, P])
        macc = sb("macc", [P, NT, H])
        vmean = sb("vmean", [P, D])
        k_dram = [nc.dram_tensor(f"k_dram{l}", (N, D), f32).ap() for l in range(2)]
        v_dram = [nc.dram_tensor(f"v_dram{l}", (N, H * VW), f32).ap() for l in range(2)]

        wkv = sb("wkv", [P, NC, 2 * D])
        wq = sb("wq", [P, NC, D])
        wo = sb("wo", [P, NC, D])
        w1 = sb("w1", [P, NC, FF])
        w2 = sb("w2", [P, NF, D])
        wwT = sb("wwT", [P, NC, D + NS])
        ww = sb("ww", [P, NC, D])
        ablk = sb("ablk", [P, NC, NS])
        acol = sb("acol", [P, 2])
        bkv = sb("bkv", [P, 2 * D])
        s1bc = sb("s1bc", [P, D])
        b1bc = sb("b1bc", [P, D])
        bobc = sb("bobc", [P, D])
        s2bc = sb("s2bc", [P, D])
        b2bc = sb("b2bc", [P, D])
        bh = sb("bh", [P, D + NS])
        s1c = sb("s1c", [P, NC])
        b1c = sb("b1c", [P, NC])
        bqc = sb("bqc", [P, NC])
        bhc = sb("bhc", [P, NC])
        nmi = sb("nmi", [P, NT], i32)
        tm = sb("tm", [P, NT])
        identf = sb("identf", [P, P])
        identb = sb("identb", [P, P], bf16)
        negi = sb("negi", [P, 4, P], bf16)
        onesm = sb("onesm", [P, P])
        ones16 = sb("ones16", [P, P], bf16)
        before = sb("before", [P, P], bf16)
        nhalf = sb("nhalf", [P, 2 * NT])
        pvals = sb("pvals", [P, 1])
        ioc = sb("ioc", [P, P], bf16)
        iob = sb("iob", [P, NT], bf16)
        ioh = sb("ioh", [P, NU], bf16)
        iou = sb("iou", [P, NU + 2])

        srow = sb("srow", [P, NU + 1], i32)
        mrow = sb("mrow", [P, NU + 1], i32)
        invalid = sb("invalid", [P, NU + 1])
        ucol = sb("ucol", [1, NU + 2], i32)
        utile = sb("utile", [1, NU + 3], i32)
        npair = sb("npair", [1, 4], i32)
        stats = sb("stats", [P, 4, 6])
        mv = sb("mv", [P, 2 * NT, 2])
        mv4 = sb("mv4", [P, 4, 2])
        ve = sb("ve", [P, 2 * NT])
        rstd = sb("rstd", [P, 2 * NT])

        ctx, whole = ExitStack(), ctx
        adjb = [sb(f"adjb{r}", [P, N], i32) for r in range(AR)]
        anyf = sb("anyf", [P, NU])
        any16 = sb("any16", [P, NU], bf16)
        place = sb("place", [P, NU])
        placei = sb("placei", [P, NU], i32)
        loi = sb("loi", [P, NU], i32)
        lof = sb("lof", [P, NU])
        hif = sb("hif", [P, NU], bf16)
        pay = sb("pay", [P, NU, 2, NT], bf16)
        oneh = [sb(f"oneh{r}", [P, NT, P], bf16) for r in range(2)]
        ab = sb("ab", [P, NT, 2, NT])
        srcf = sb("srcf", [P, NU])
        nbi = sb("nbi", [P, NT], i32)
        nbf = sb("nbf", [P, NT])
        incl = sb("incl", [P, NT])
        tmp16 = sb("tmp16", [P, 2, NT])
        inclq = sb("inclq", [P, 3])
        done = sb("done", [NT, NU + 2])
        t0 = sb("t0", [1, NU + 2])
        t1 = sb("t1", [1, NU + 2])
        t2 = sb("t2", [1, NU + 2])
        t3 = sb("t3", [1, 1])
        xn = [sb(f"xn{r}", [P, 2, D]) for r in range(2)]
        hT = [sb(f"hT{r}", [P, 2, NC, P]) for r in range(2)]
        bhm = sb("bhm", [P, NC, P])
        ctx.close()

        ctx = whole
        Oacc = sb("Oacc", [P, NT, H * VW])
        ctx = ExitStack()
        urow = [sb(f"urow{r}", [P, 2], i32) for r in range(2)]
        vrow = [sb(f"vrow{r}", [P, 1], i32) for r in range(2)]
        uinv = [sb(f"uinv{r}", [P, 1]) for r in range(2)]
        Kg = [sb(f"Kg{r}", [P, D]) for r in range(2)]
        Vg = [sb(f"Vg{r}", [P, H * VW]) for r in range(2)]
        Mg = [sb(f"Mg{r}", [P, P], i32) for r in range(2)]
        Mb = [sb(f"Mb{r}", [P, P], bf16) for r in range(2)]
        qz = [sb(f"qz{r}", [P, H, P]) for r in range(2)]
        KTs = [sb(f"KTs{r}", [P, D]) for r in range(2)]
        Z = [sb(f"Z{r}", [P, H * P]) for r in range(2)]
        Y = sb("Y", [P, H * P])
        Pr = [sb(f"Pr{r}", [P, H * P]) for r in range(2)]
        PTs = [sb(f"PTs{r}", [P, H * P]) for r in range(2)]
        mu = sb("mu", [P, H])
        mnew = sb("mnew", [P, H])
        dm = [sb(f"dm{r}", [P, H]) for r in range(2)]
        ea = [sb(f"ea{r}", [P, H]) for r in range(2)]
        ctx.close()

        ctx = ExitStack()
        e8 = sb("e8", [P, 2, H])
        w8 = sb("w8", [P, 2, H])
        l8 = sb("l8", [P, 2, H])
        ctxr = sb("ctxr", [P, 2, D])
        tmpr = sb("tmpr", [P, 2, D])
        y = sb("y", [P, 2, D])
        ctxT = sb("ctxT", [P, 2, NC, P])
        yT = sb("yT", [P, NC, 2, P])
        h1 = sb("h1", [P, NF, 2 * P])
        x1s = sb("x1s", [P, 2, D])
        x1T = sb("x1T", [P, 2, NC, P])
        qrow = sb("qrow", [P, 2, D])
        ctx.close()
        ctx = whole

        pS = [pb(f"pS{r}", [P, H * P]) for r in range(2)]
        pPT = pb("pPT", [P, H * P])
        pKT = pb("pKT", [P, 512])
        pO = pb("pO", [P, 512])

        ld_x, ld_h, ld_w, ld_small = sem("ld_x"), sem("ld_h"), sem("ld_w"), sem("ld_small")
        ld_late = sem("ld_late")
        adj_ld = [sem(f"adj_ld{r}") for r in range(AR)]
        adj_used, consts, dconsts, waug = sem("adj_used"), sem("consts"), sem("dconsts"), sem("waug")
        ve_ready, rstd_ready = sem("ve_ready"), sem("rstd_ready")
        xn_ready, xn_used, ht_done = sem("xn_ready"), sem("xn_used"), sem("ht_done")
        tx_ready, hT_ready, hT_used = sem("tx_ready"), sem("hT_ready"), sem("hT_used")
        kvp_ready, kv_done = sem("kvp_ready"), sem("kv_done")
        qp_ready, q_done = sem("qp_ready"), sem("q_done")
        kv_stored = [sem("kv_stored0"), sem("kv_stored1")]
        any_ready, pos_ready, pay_ready = sem("any_ready"), sem("pos_ready"), sem("pay_ready")
        oh_ready, oh_used, idx_ready = sem("oh_ready"), sem("oh_used"), sem("idx_ready")
        done_ready, rows_ready = sem("done_ready"), sem("rows_ready")
        vm_ready, vm_done = sem("vm_ready"), sem("vm_done")
        phase = sem("phase")
        carrier = sem("carrier")
        out_done = sem("out_done")
        S = []
        for l in range(2):
            S.append({n: sem(f"{n}_{l}") for n in (
                "k_got0", "k_got1", "v_got0", "v_got1", "m_got0", "m_got1", "q_got0", "q_got1",
                "listed", "vlisted", "mask_ready", "kt_ready", "kt_done", "s_ready", "s_free",
                "y_ready", "z_ready", "exp_done", "ea_done", "pt_ready", "pt_done",
                "pv_done", "merged", "q_clear")})
        M = [{n: sem(f"{n}_m{l}") for n in (
            "ctx_ready", "ctxT_ready", "ctxT_done", "wo_ready", "z_done", "ve_ready", "rstd_ready",
            "y_ready", "yT_ready", "yT_done", "h1_ready", "h1_done", "ff_ready", "ff_done",
            "x1_ready", "x1_kept", "x1T_ready", "x1T_done", "h_ready", "h_done", "qrow_ready",
            "qrT_ready", "qT_done", "neg_ready", "exp_ready", "out_ready")} for l in range(2)]

        block = ctx.enter_context(nc.Block())

        def meet(e, k):
            e.drain().then_inc(phase, 1)
            e.wait_ge(phase, 5 * k)

        def wait_alone(e, semaphore, value):
            e.wait_ge(semaphore, value)
            e.sem_inc(carrier, 1)

        def heads(ap, w):
            return ap.rearrange("p (h w) -> p h w", w=w)

        def values(ap):
            return heads(ap, VW)[:, :, 0:HD]

        SMALL = 16 * 15

        def sync_attention(sp, l):
            s = S[l]
            np_ = sp.value_load(npair[0:1, 0:1], min_val=1, max_val=NU // 2)

            def bring(u, r):
                j = sp.value_load(utile[0:1, ds(u + 1, 1)], min_val=0, max_val=NT - 1)
                sp.wait_ge(s["s_ready"], u + 1)
                for a in range(4):
                    rows = slice(HD * a, HD * a + HD)
                    sp.dma_start(qz[r][rows, a:H:4, :],
                                 qT[rows, ds(j, 1), :, :].rearrange("p o c t -> p (o c) t")
                                 ).then_inc(s[f"q_got{r}"], 16)

            sp.wait_ge(s["q_clear"], 1)
            bring(0, 0)
            bring(1, 1)
            with sp.Fori(0, np_) as p:
                bring(p * 2 + 2, 0)
                bring(p * 2 + 3, 1)
            for r in range(2):
                wait_alone(sp, s[f"q_got{r}"], (np_ + 1) * 64)

        @block.sync
        def _(sp):
            sp.dma_start(xs[:, :, :], x.rearrange("(p a) d -> p a d", a=NT)).then_inc(ld_x, 16)
            sp.dma_start(ht[:, :, :], h_target.rearrange("(p a) d -> p a d", a=NT)).then_inc(ld_h, 16)
            adj_v = adj_s.rearrange("(p i j) a -> p i (j a)", i=NT, j=NT)
            for r in range(AR):
                sp.dma_start(adjb[r][:, :], adj_v[:, r, :]).then_inc(adj_ld[r], 16)
            with sp.Fori(1, NT // AR) as it:
                for r in range(AR):
                    sp.wait_ge(adj_used, it * AR + (r + 1 - AR))
                    sp.dma_start(adjb[r][:, :], adj_v[:, ds(it * AR + r, 1), :].rearrange(
                        "p i n -> p (i n)")).then_inc(adj_ld[r], 16)
            meet(sp, 1)
            sync_attention(sp, 0)
            meet(sp, 2)
            meet(sp, 3)
            sync_attention(sp, 1)
            meet(sp, 4)
            sp.wait_ge(out_done, 16 * NT // 2)

        def store_rows(g, l, j, n):
            g.dma_start(k_dram[l].rearrange("(p a) w -> p a w", a=NT)[:, ds(j, n), :],
                        krows[:, ds(j, n), :]).then_inc(kv_stored[l], 16)
            g.dma_start(v_dram[l].rearrange("(p a) w -> p a w", a=NT)[:, ds(j, n), :],
                        vrows[:, ds(j, n), :]).then_inc(kv_stored[l], 16)

        def pool_attention(g, l):
            s = S[l]
            np_ = g.value_load(npair[0:1, 0:1], min_val=1, max_val=NU // 2)

            def sources(u, r):
                c = g.value_load(ucol[0:1, ds(u, 1)], min_val=0, max_val=NU)
                wait_alone(g, s["mask_ready"], u + 1)
                wait_alone(g, s["kt_ready"], u + 1)
                g.tensor_copy(urow[r][:, 0:1], srow[:, ds(c, 1)])
                g.tensor_copy(uinv[r][:, :], invalid[:, ds(c, 1)])
                g.tensor_copy(urow[r][:, 1:2], mrow[:, ds(c, 1)]).then_inc(s["listed"], 1)
                wait_alone(g, s["listed"], u + 1)
                g.indirect_dma_start(Mg[r][:, :], None, adj_s,
                                     bass.IndirectOffsetOnAxis(ap=urow[r][:, 1:2], axis=0)
                                     ).then_inc(s[f"m_got{r}"], 16)
                g.indirect_dma_start(Kg[r][:, :], None, k_dram[l],
                                     bass.IndirectOffsetOnAxis(ap=urow[r][:, 0:1], axis=0)
                                     ).then_inc(s[f"k_got{r}"], 16)

            def source_values(u, r):
                c = g.value_load(ucol[0:1, ds(u, 1)], min_val=0, max_val=NU)
                wait_alone(g, s["pv_done"], u + 1)
                g.tensor_copy(vrow[r][:, 0:1], srow[:, ds(c, 1)]).then_inc(s["vlisted"], 1)
                wait_alone(g, s["vlisted"], u + 1)
                g.indirect_dma_start(Vg[r][:, :], None, v_dram[l],
                                     bass.IndirectOffsetOnAxis(ap=vrow[r][:, 0:1], axis=0)
                                     ).then_inc(s[f"v_got{r}"], 16)

            for r in range(2):
                last = g.memset(qz[r][:, :, :], 0.0)
            last.then_inc(s["q_clear"], 1)
            sources(0, 0)
            sources(1, 1)
            source_values(0, 0)
            with g.Fori(0, np_) as p:
                sources(p * 2 + 2, 0)
                source_values(p * 2 + 1, 1)
                sources(p * 2 + 3, 1)
                source_values(p * 2 + 2, 0)
            for r in range(2):
                for n in ("m_got", "k_got"):
                    wait_alone(g, s[f"{n}{r}"], (np_ + 1) * 16)
            wait_alone(g, s["v_got0"], (np_ + 1) * 16)
            wait_alone(g, s["v_got1"], np_ * 16)

        @block.gpsimd
        def _(g):
            g.memset(identf[:, :], 0.0)
            g.memset(before[:, :], 1.0)
            g.memset(onesm[:, :], 1.0 / N)
            g.memset(ones16[:, :], 1.0)
            g.memset(nhalf[:, :], -0.5)
            g.memset(ablk[:, :, :], 0.0)
            g.memset(vrows[:, :, :], 1.0)
            g.iota(ioc[:, :], [[1, P]], base=0, channel_multiplier=0,
                   allow_small_or_imprecise_dtypes=True)
            g.iota(iob[:, :], [[1, NT]], base=1, channel_multiplier=0,
                   allow_small_or_imprecise_dtypes=True)
            g.iota(ioh[:, :], [[1, NT], [0, NT]], base=0, channel_multiplier=0,
                   allow_small_or_imprecise_dtypes=True)
            g.iota(iou[:, :], [[1, NU + 2]], base=0, channel_multiplier=0,
                   allow_small_or_imprecise_dtypes=True)
            g.iota(pvals[:, :], [[0, 1]], base=1, channel_multiplier=1,
                   allow_small_or_imprecise_dtypes=True)
            g.drain()
            g.affine_select(out=identf[:, :], in_=identf[:, :], compare_op=ALU.not_equal, fill=1.0,
                            base=0, pattern=[[-1, P]], channel_multiplier=1)
            g.affine_select(out=before[:, :], in_=before[:, :], compare_op=ALU.is_ge, fill=0.0,
                            base=-1, pattern=[[1, P]], channel_multiplier=-1)
            g.drain().then_inc(consts, 1)

            g.wait_ge(ve_ready, 1)
            g.tensor_tensor(rstd[:, :], ve[:, :], nhalf[:, :], ALU.pow).then_inc(rstd_ready, 1)
            g.wait_ge(ld_small, SMALL)
            g.drain().then_inc(ht_done, 2)
            g.tensor_tensor(bobc[:, :], bobc[:, :], b1bc[:, :], ALU.add)
            g.drain()
            with g.Fori(0, NT // AR) as it:
                for k in range(AR):
                    j = it * AR + k
                    row = ht[:, ds(j, 1), :].rearrange("p o d -> p (o d)")
                    g.wait_ge(xn_ready, j + 1)
                    g.tensor_tensor(row, xn[k % 2][:, 1, :], s1bc[:, :], ALU.mult)
                    g.drain().then_inc(ht_done, 1)
                    g.tensor_tensor(row, row, bobc[:, :], ALU.add)
                wait_alone(g, kv_done, it * AR + (AR + 2))
                store_rows(g, 0, it * AR, AR)
            g.wait_ge(kv_stored[0], 32 * NT // AR)
            meet(g, 1)
            pool_attention(g, 0)
            meet(g, 2)

            g.memset(krows[:, :, :], 0.0)
            g.memset(qrow[:, :, :], 0.0)
            g.drain()
            g.memset(krows[:, :, 0:D:HD], 1.0)
            g.memset(qrow[:, :, 1:D:HD], 1.0)
            g.drain().then_inc(consts, 1)
            m = M[0]
            g.drain().then_inc(m["x1_kept"], 1)
            with g.Fori(0, NT // 2) as it:
                for half in range(2):
                    g.wait_ge(m["ve_ready"], it * 2 + (half + 1))
                    g.tensor_tensor(rstd[:, 0:2], ve[:, 0:2], nhalf[:, 0:2], ALU.pow
                                    ).then_inc(m["rstd_ready"], 1)
                wait_alone(g, m["x1_ready"], it + 1)
                g.tensor_copy(xs[:, ds(it * 2, 2), :], x1s[:, :, :]).then_inc(m["x1_kept"], 1)
                wait_alone(g, m["h_done"], it * 2 + 2)
                store_rows(g, 1, it * 2, 2)
            g.wait_ge(kv_stored[1], 32 * NT // 2)
            meet(g, 3)
            pool_attention(g, 1)
            meet(g, 4)
            m = M[1]
            with g.Fori(0, NT // 2) as it:
                g.wait_ge(m["ve_ready"], it + 1)
                g.tensor_tensor(rstd[:, 0:2], ve[:, 0:2], nhalf[:, 0:2], ALU.pow
                                ).then_inc(m["rstd_ready"], 1)
                wait_alone(g, m["out_ready"], it + 1)
                g.dma_start(out.rearrange("(p a) d -> p a d", a=NT)[:, ds(it * 2, 2), :],
                            ht[:, ds(it * 2, 2), :]).then_inc(out_done, 16)

        def bcast(ap):
            return ap.partition_broadcast(P)

        def act_attention(act, l):
            s = S[l]
            np_ = act.value_load(npair[0:1, 0:1], min_val=1, max_val=NU // 2)
            act.drain().then_inc(s["kt_done"], 1)
            act.drain().then_inc(s["exp_done"], 2)
            act.drain().then_inc(s["ea_done"], 1)
            act.drain().then_inc(s["pt_done"], 1)

            def keys(u, r):
                act.wait_ge(s["kt_ready"], u + 3)
                act.wait_ge(s["s_ready"], u + 1)
                act.activation(KTs[r][:, :], pKT[:, 0:D], ACT.Copy).then_inc(s["kt_done"], 1)

            def slope(u):
                act.wait_ge(s["s_ready"], u + 3)
                act.wait_ge(s["s_free"], u + 2)
                act.activation(Y[:, :], pS_of(u)[:, :], ACT.Copy, scale=SLOPE).then_inc(s["y_ready"], 1)

            def weights(u, r):
                act.wait_ge(s["z_ready"], u + 3)
                act.wait_ge(s["pt_ready"], u + 1)
                act.activation(Pr[r][:, :], Z[r][:, :], ACT.Exp).then_inc(s["exp_done"], 1)
                act.activation(ea[r][:, :], dm[r][:, :], ACT.Exp).then_inc(s["ea_done"], 1)

            def transposed(u, r):
                act.wait_ge(s["pt_ready"], u + 3)
                act.wait_ge(s["pv_done"], u + 1)
                act.activation(PTs[r][:, :], pPT[:, :], ACT.Copy).then_inc(s["pt_done"], 1)

            def pS_of(u):
                return pS[0] if u is None else pS[parity[0]]

            parity = [0]
            keys(0, 0)
            keys(1, 1)
            if l == 1:
                slope(0)
            with act.Fori(0, np_) as p:
                for r in range(2):
                    u = p * 2 + r
                    weights(u, r)
                    if l == 1:
                        parity[0] = 1 - r
                        slope(u + 1)
                    transposed(u, r)
                    keys(u + 2, r)

        @block.scalar
        def _(act):
            def small(dst, src):
                act.dma_start(dst, src).then_inc(ld_small, 16)

            for c in range(NC):
                rows = slice(P * c, P * c + P)
                act.dma_start(wkv[:, c, 0:D], Wk[rows, :]).then_inc(ld_w, 16)
                act.dma_start(wkv[:, c, D:2 * D], Wv[rows, :]).then_inc(ld_w, 16)
                act.dma_start(wq[:, c, :], Wq[rows, :]).then_inc(ld_w, 16)
            small(s1c[:, :], ln1_sc)
            small(b1c[:, :], ln1_bc)
            small(bqc[:, :], bqc_d)
            small(bhc[:, :], Wbc)
            small(nmi[:, :], nodemask.rearrange("(p a) -> p a", a=NT))
            small(bkv[:, 0:D], bcast(bk))
            small(bkv[:, D:2 * D], bcast(bv))
            small(s1bc[:, :], bcast(ln1_s))
            small(b1bc[:, :], bcast(ln1_b))
            small(bobc[:, :], bcast(bo))
            for q in range(4):
                small(acol[HD * q:HD * (q + 1), :], att_a)
            small(bh[:, 0:D], bcast(Wb))
            act.dma_start(wo[:, :, :], Wo.rearrange("(c p) n -> p c n", p=P)).then_inc(ld_late, 16)
            act.dma_start(w1[:, :, :], W1.rearrange("(c p) n -> p c n", p=P)).then_inc(ld_late, 16)
            act.dma_start(w2[:, :, :], W2.rearrange("(c p) n -> p c n", p=P)).then_inc(ld_late, 16)
            act.dma_start(ww[:, :, :], Ww.rearrange("(c p) n -> p c n", p=P)).then_inc(ld_late, 16)
            act.dma_start(wwT[:, :, 0:D], WwT.rearrange("(c p) n -> p c n", p=P)).then_inc(ld_late, 16)
            act.dma_start(s2bc[:, :], bcast(ln2_s)).then_inc(ld_late, 16)
            act.dma_start(b2bc[:, :], bcast(ln2_b)).then_inc(ld_late, 16)

            act.drain().then_inc(hT_ready, 2)
            act.drain().then_inc(q_done, 2)
            act.wait_ge(dconsts, 1)
            with act.Fori(0, NT // 2) as it:
                def scale(j, r):
                    act.wait_ge(tx_ready, j + 1)
                    act.wait_ge(hT_used, j + 1)
                    for i in range(2):
                        for c in range(NC):
                            last = act.activation(
                                hT[r][:, i, c, :], pS[r][:, (2 * i + c) * P:(2 * i + c + 1) * P],
                                ACT.Identity, bias=b1c[:, c:c + 1], scale=s1c[:, c:c + 1])
                    last.then_inc(hT_ready, 1)

                def queries(j, r):
                    act.wait_ge(qp_ready, j + 1)
                    for c in range(NC):
                        last = act.activation(
                            qT[:, ds(j, 1), c, :].rearrange("p o t -> p (o t)"),
                            (pKT, pO)[r][:, c * P:(c + 1) * P],
                            ACT.Identity, bias=bqc[:, c:c + 1], scale=float(HD) ** -0.5)
                    last.then_inc(q_done, 1)

                for r in range(2):
                    scale(it * 2 + r, r)
                for r in range(2):
                    queries(it * 2 + r, r)
            meet(act, 1)
            act_attention(act, 0)
            meet(act, 2)
            m = M[0]
            with act.Fori(0, NT // 2) as it:
                act.wait_ge(m["ctxT_ready"], it + 1)
                act.activation(ctxT[:, :, :, :].rearrange("p k c t -> p (k c t)"), pS[0][:, 0:512],
                               ACT.Copy).then_inc(m["ctxT_done"], 1)
                act.wait_ge(m["yT_ready"], it + 1)
                act.activation(yT[:, :, :, :].rearrange("p c k t -> p (c k t)"), pS[1][:, 0:512],
                               ACT.Copy).then_inc(m["yT_done"], 1)
                for f in range(NF // 2):
                    act.wait_ge(m["h1_ready"], it * (NF // 2) + (f + 1))
                    act.activation(h1[:, 2 * f:2 * f + 2, :].rearrange("p f t -> p (f t)"),
                                   (pS[1][:, 512:1024], pPT[:, 0:512])[f % 2],
                                   ACT.Gelu_apprx_tanh).then_inc(m["h1_done"], 1)
                act.wait_ge(m["x1T_ready"], it + 1)
                act.activation(x1T[:, :, :, :].rearrange("p k c t -> p (k c t)"), pKT[:, :],
                               ACT.Copy).then_inc(m["x1T_done"], 1)
                act.wait_ge(m["qrT_ready"], it + 1)
                act.activation(qT[:, ds(it * 2, 2), :, :].rearrange("p k c t -> p (k c t)"),
                               pKT[:, :], ACT.Copy).then_inc(m["qT_done"], 1)
            meet(act, 3)
            act_attention(act, 1)
            meet(act, 4)
            m = M[1]
            with act.Fori(0, NT // 2) as it:
                act.wait_ge(m["neg_ready"], it + 1)
                act.activation(tmpr[:, :, :], tmpr[:, :, :], ACT.Exp).then_inc(m["exp_ready"], 1)

        def vector_attention(v, l):
            s = S[l]
            np_ = v.value_load(npair[0:1, 0:1], min_val=1, max_val=NU // 2)
            v.memset(macc[:, :, :], NEG)
            v.memset(Oacc[:, :, :], 0.0)
            v.memset(ea[1][:, :], 1.0)
            v.memset(pO[:, 0:H * VW], 0.0)
            v.drain().then_inc(s["mask_ready"], 2)
            v.drain().then_inc(s["s_free"], 2)
            v.drain().then_inc(s["z_ready"], 2)

            def mask(u, r):
                v.wait_ge(s[f"m_got{r}"], (u // 2 if isinstance(u, int) else half_of[0]) * 16 + 16)
                v.wait_ge(s["s_ready"], u + 1)
                v.tensor_scalar(Mb[r][:, :], Mg[r][:, :], 0.0, uinv[r][:, 0:1], ALU.is_equal, ALU.max
                                ).then_inc(s["mask_ready"], 1)

            def running_maximum(j, scores):
                old = macc[:, ds(j, 1), :].rearrange("p o h -> p (o h)")
                v.tensor_reduce(mu[:, :], heads(scores, P), AX.X, ALU.max)
                v.drain()
                v.tensor_tensor(mnew[:, :], mu[:, :], old, ALU.max)
                v.drain()
                return old

            def softmax(u, r):
                j = v.value_load(utile[0:1, ds(u + 1, 1)], min_val=0, max_val=NT - 1)
                scores = pS[r][:, :]
                if l == 0:
                    v.wait_ge(s["s_ready"], u + 3)
                else:
                    v.wait_ge(s["y_ready"], u + 1)
                v.wait_ge(s["exp_done"], u + 1)
                if l == 1:
                    v.tensor_tensor(Z[r][:, :], scores, Y[:, :], ALU.max).then_inc(s["s_free"], 1)
                    v.drain()
                    scores = Z[r][:, :]
                old = running_maximum(j, scores)
                v.tensor_tensor(dm[r][:, :], old, mnew[:, :], ALU.subtract)
                v.tensor_tensor(heads(Z[r][:, :], P), heads(scores, P),
                                mnew[:, :].unsqueeze(2).broadcast_to([P, H, P]), ALU.subtract
                                ).then_inc(s["z_ready"], 1)
                v.drain()
                v.tensor_copy(old, mnew[:, :])

            def merge(u, r):
                j = v.value_load(utile[0:1, ds(u + 1, 1)], min_val=0, max_val=NT - 1)
                mine = Oacc[:, ds(j, 1), :].rearrange("p o w -> p (o w)")
                v.wait_ge(s["ea_done"], u + 2)
                v.tensor_tensor(heads(mine, VW), heads(mine, VW),
                                ea[r][:, :].unsqueeze(2).broadcast_to([P, H, VW]), ALU.mult)
                v.drain()
                v.wait_ge(s["pv_done"], u + 3)
                v.tensor_tensor(mine, mine, pO[:, 0:H * VW], ALU.add).then_inc(s["merged"], 1)

            half_of = [0]
            mask(0, 0)
            with v.Fori(0, np_) as p:
                half_of[0] = p
                mask(p * 2 + 1, 1)
                softmax(p * 2, 0)
                merge(p * 2 - 1, 1)
                half_of[0] = p + 1
                mask(p * 2 + 2, 0)
                softmax(p * 2 + 1, 1)
                merge(p * 2, 0)
            v.drain()
            merge(np_ * 2 - 1, 1)

        def averages(v, j0, dst):
            last = Oacc[:, ds(j0, 2), :].rearrange("p k (h w) -> p k h w", w=VW)
            v.tensor_scalar(e8[:, :, :], macc[:, ds(j0, 2), :], EMPTY, None, ALU.is_lt)
            v.drain()
            v.tensor_tensor(l8[:, :, :], e8[:, :, :], last[:, :, :, HD], ALU.add)
            v.tensor_scalar(w8[:, :, :], e8[:, :, :], -1.0, 1.0, ALU.mult, ALU.add)
            v.drain()
            v.reciprocal(l8[:, :, :], l8[:, :, :])
            v.drain()
            v.tensor_tensor(w8[:, :, :], w8[:, :, :], l8[:, :, :], ALU.mult)
            v.drain()
            for k in range(2):
                mine = Oacc[:, ds(j0 + k, 1), :].rearrange("p o w -> p (o w)")
                v.tensor_tensor(heads(dst[:, k, :], HD), values(mine),
                                w8[:, k, :].unsqueeze(2).broadcast_to([P, H, HD]), ALU.mult)
                v.tensor_tensor(heads(tmpr[:, k, :], HD), heads(vmean[:, :], HD),
                                e8[:, k, :].unsqueeze(2).broadcast_to([P, H, HD]), ALU.mult)
            v.drain()
            v.tensor_tensor(dst[:, :, :], dst[:, :, :], tmpr[:, :, :], ALU.add)
            v.drain()

        def statistics(v, rows, ready):
            v.drain()
            for k in range(2):
                v.bn_stats(stats[:, k, :], rows[:, k, :])
            v.drain()
            for k in range(2):
                v.bn_aggr(mv[:, k, :], stats[:, k, :])
            v.drain()
            v.tensor_scalar(ve[:, 0:2], mv[:, 0:2, 1], EPS, None, ALU.add).then_inc(ready, 1)

        def between(v):
            m = M[0]
            v.wait_ge(ld_late, 16 * 7)
            v.wait_ge(consts, 2)
            with v.Fori(0, NT // 2) as it:
                j0 = it * 2
                averages(v, j0, ctxr)
                v.drain().then_inc(m["ctx_ready"], 1)
                v.wait_ge(m["wo_ready"], it + 1)
                v.tensor_tensor(ctxr[:, :, :], pS[0][:, 512:1024].rearrange("p (k d) -> p k d", k=2),
                                ht[:, ds(j0, 2), :], ALU.add).then_inc(m["z_done"], 1)
                statistics(v, ctxr, m["ve_ready"])
                v.wait_ge(m["rstd_ready"], it * 2 + 1)
                for k in range(2):
                    v.tensor_scalar(y[:, k, :], ctxr[:, k, :], mv[:, k, 0:1], rstd[:, k:k + 1],
                                    ALU.subtract, ALU.mult)
                    v.tensor_scalar(tmpr[:, k, :], b2bc[:, :], tm[:, ds(j0 + k, 1)], None, ALU.mult)
                v.drain()
                for k in range(2):
                    v.scalar_tensor_tensor(y[:, k, :], y[:, k, :], tm[:, ds(j0 + k, 1)], s2bc[:, :],
                                           ALU.mult, ALU.mult)
                v.drain()
                v.tensor_tensor(y[:, :, :], y[:, :, :], tmpr[:, :, :], ALU.add)
                v.drain().then_inc(m["y_ready"], 1)
                v.wait_ge(m["ff_ready"], it + 1)
                v.tensor_tensor(ctxr[:, :, :], pPT[:, 512:1024].rearrange("p (k d) -> p k d", k=2),
                                y[:, :, :], ALU.add)
                v.drain().then_inc(m["ff_done"], 1)
                v.tensor_tensor(ctxr[:, :, :], ctxr[:, :, :], xs[:, ds(j0, 2), :], ALU.add)
                statistics(v, ctxr, m["ve_ready"])
                v.wait_ge(m["rstd_ready"], it * 2 + 2)
                v.wait_ge(m["x1_kept"], it + 1)
                for k in range(2):
                    v.tensor_scalar(x1s[:, k, :], ctxr[:, k, :], mv[:, k, 0:1], rstd[:, k:k + 1],
                                    ALU.subtract, ALU.mult)
                v.drain().then_inc(m["x1_ready"], 1)
                for k in range(2):
                    v.wait_ge(m["h_ready"], it * 2 + (k + 1))
                    j = j0 + k
                    v.tensor_tensor(values(vrows[:, ds(j, 1), :].rearrange("p o d -> p (o d)")),
                                    heads(pO[:, 0:D], HD), heads(bh[:, 0:D], HD), ALU.add)
                    v.tensor_tensor(qrow[:, k, 0:D:HD], pO[:, D:D + H], bh[:, D:D + H], ALU.add)
                    v.tensor_tensor(krows[:, ds(j, 1), 1:D:HD].rearrange("p o h -> p (o h)"),
                                    pO[:, D + H:D + NS], bh[:, D + H:D + NS], ALU.add)
                    v.drain().then_inc(m["h_done"], 1)
            v.wait_ge(vm_ready, 2)
            v.tensor_copy(vmean[:, :], pS[0][:, 0:D])

        def ending(v):
            m = M[1]
            with v.Fori(0, NT // 2) as it:
                j0 = it * 2
                averages(v, j0, ctxr)
                v.tensor_scalar(tmpr[:, :, :], ctxr[:, :, :], 0.0, None, ALU.min
                                ).then_inc(m["neg_ready"], 1)
                v.scalar_tensor_tensor(y[:, :, :].rearrange("p k d -> p (k d)"),
                                       ctxr[:, :, :].rearrange("p k d -> p (k d)"), 0.0,
                                       xs[:, ds(j0, 2), :].rearrange("p k d -> p (k d)"),
                                       ALU.max, ALU.add)
                v.drain()
                v.wait_ge(m["exp_ready"], it + 1)
                v.scalar_tensor_tensor(y[:, :, :].rearrange("p k d -> p (k d)"),
                                       tmpr[:, :, :].rearrange("p k d -> p (k d)"), -1.0,
                                       y[:, :, :].rearrange("p k d -> p (k d)"), ALU.add, ALU.add)
                statistics(v, y, m["ve_ready"])
                v.wait_ge(m["rstd_ready"], it + 1)
                for k in range(2):
                    v.tensor_scalar(ht[:, ds(j0 + k, 1), :].rearrange("p o d -> p (o d)"), y[:, k, :],
                                    mv[:, k, 0:1], rstd[:, k:k + 1], ALU.subtract, ALU.mult)
                v.drain().then_inc(m["out_ready"], 1)

        @block.vector
        def _(v):
            v.wait_ge(ld_x, 16)
            v.wait_ge(ld_h, 16)
            with v.Fori(0, NT // 2) as it:
                for k in range(2):
                    for i, src in enumerate((xs, ht)):
                        v.bn_stats(stats[:, 2 * k + i, :],
                                   src[:, ds(it * 2 + k, 1), :].rearrange("p o d -> p (o d)"))
                v.drain()
                for k in range(4):
                    v.bn_aggr(mv4[:, k, :], stats[:, k, :])
                v.drain()
                v.tensor_copy(mv[:, ds(it * 4, 4), :], mv4[:, :, :])
            v.drain()
            v.tensor_scalar(ve[:, :], mv[:, :, 1], EPS, None, ALU.add).then_inc(ve_ready, 1)
            v.wait_ge(ld_small, SMALL)
            v.tensor_scalar(tm[:, :], nmi[:, :], 1.0, None, ALU.is_equal)
            v.tensor_scalar(bqc[:, :], bqc[:, :], float(HD) ** -0.5, None, ALU.mult)
            v.wait_ge(consts, 1)
            v.tensor_copy(identb[:, :], identf[:, :])
            v.tensor_scalar(negi[:, :, :], identf[:, :].unsqueeze(1).broadcast_to([P, 4, P]), NEG,
                            None, ALU.mult)
            for c in range(NC):
                for q in range(4):
                    rows = slice(HD * q, HD * q + HD)
                    for i in range(2):
                        h = i * H + 4 * c + q
                        v.tensor_copy(ablk[rows, c, h:h + 1], acol[rows, i:i + 1])
            v.tensor_copy(bhm[:, :, :], bhc[:, :].unsqueeze(2).broadcast_to([P, NC, P]))
            v.drain().then_inc(dconsts, 1)

            v.drain().then_inc(kv_done, 2)
            v.wait_ge(rstd_ready, 1)
            with v.Fori(0, NT // AR) as it:
                def normalise(j, r):
                    v.wait_ge(xn_used, j + 1)
                    v.wait_ge(ht_done, j + 1)
                    for i, src in enumerate((xs, ht)):
                        last = v.tensor_scalar(
                            xn[r][:, i, :], src[:, ds(j, 1), :].rearrange("p o d -> p (o d)"),
                            mv[:, ds(j * 2 + i, 1), 0:1].rearrange("p o d -> p (o d)"),
                            rstd[:, ds(j * 2 + i, 1)], ALU.subtract, ALU.mult)
                    last.then_inc(xn_ready, 1)

                def edges(j, k):
                    v.wait_ge(adj_ld[k], it * 16 + 16)
                    v.tensor_reduce(anyf[:, ds(j * NT, NT)],
                                    adjb[k][:, :].rearrange("p (j a) -> p j a", a=P), AX.X, ALU.max,
                                    apply_absolute_value=True).then_inc(adj_used, 1)

                def keys_values(j, r):
                    v.wait_ge(kvp_ready, j + 1)
                    kvp = pPT[:, 512 * r:512 * r + 512]
                    v.scalar_tensor_tensor(krows[:, ds(j, 1), :].rearrange("p o d -> p (o d)"),
                                           kvp[:, 0:D], tm[:, ds(j, 1)], bkv[:, 0:D],
                                           ALU.mult, ALU.add)
                    v.scalar_tensor_tensor(values(vrows[:, ds(j, 1), :].rearrange("p o d -> p (o d)")),
                                           heads(kvp[:, D:2 * D], HD), tm[:, ds(j, 1)],
                                           heads(bkv[:, D:2 * D], HD),
                                           ALU.mult, ALU.add).then_inc(kv_done, 1)

                for half in range(AR // 2):
                    pair = [(it * AR + (2 * half + r), r) for r in range(2)]
                    for j, r in pair:
                        normalise(j, r)
                    for j, r in pair:
                        edges(j, 2 * half + r)
                    for j, r in pair:
                        keys_values(j, r)
            v.drain()
            v.tensor_scalar(any16[:, :], anyf[:, :], 0.0, None, ALU.is_gt).then_inc(any_ready, 1)

            v.wait_ge(pos_ready, 1)
            v.scalar_tensor_tensor(place[:, :], pS[0][:, 512:512 + NU], 1.0, any16[:, :],
                                   ALU.add, ALU.mult)
            v.drain()
            v.tensor_scalar(placei[:, :], place[:, :], float(P - 1), None, ALU.add)
            v.drain()
            v.tensor_scalar(loi[:, :], placei[:, :], P - 1, None, ALU.bitwise_and)
            v.tensor_scalar(placei[:, :], placei[:, :], 7, None, ALU.logical_shift_right)
            v.drain()
            v.tensor_copy(lof[:, :], loi[:, :])
            v.tensor_copy(hif[:, :], placei[:, :])
            v.drain()
            v.tensor_tensor(pay[:, :, 1, :], hif[:, :].unsqueeze(2).broadcast_to([P, NU, NT]),
                            iob[:, :].unsqueeze(1).broadcast_to([P, NU, NT]), ALU.is_equal)
            v.drain()
            v.tensor_scalar(pay[:, :, 0, :], pay[:, :, 1, :], pvals[:, 0:1], None, ALU.mult)
            v.drain()
            v.tensor_tensor(pay[:, :, 1, :], pay[:, :, 1, :],
                            ioh[:, :].unsqueeze(2).broadcast_to([P, NU, NT]), ALU.mult)
            v.drain().then_inc(pay_ready, 1)
            with v.Fori(0, NT // 2) as it:
                for r in range(2):
                    j = it * 2 + r
                    v.wait_ge(oh_used, j + 1)
                    for i in range(NT):
                        last = v.tensor_scalar(oneh[r][:, i, :], ioc[:, :], lof[:, ds(j + i * NT, 1)],
                                               None, ALU.is_equal)
                    last.then_inc(oh_ready, 1)
            v.wait_ge(idx_ready, 1)
            v.tensor_copy(ab[:, :, :, :].rearrange("p j w b -> p (j w b)"), pPT[:, 0:512])
            v.memset(srow[:, 0:1], 0)
            v.memset(mrow[:, 0:1], 0)
            v.memset(invalid[:, 0:1], 1.0)
            v.drain()
            tiles = srcf[:, :].rearrange("p (j b) -> p j b", b=NT)
            v.scalar_tensor_tensor(tiles, ab[:, :, 0, :], float(NT), ab[:, :, 1, :],
                                   ALU.mult, ALU.add)
            v.tensor_scalar(invalid[:, 1:].rearrange("p (j b) -> p j b", b=NT), ab[:, :, 0, :], 0.0,
                            None, ALU.is_equal)
            v.drain()
            v.tensor_scalar(srcf[:, :], srcf[:, :], float(-NT), 0.0, ALU.add, ALU.max)
            v.drain()
            v.tensor_copy(srow[:, 1:], srcf[:, :])
            v.scalar_tensor_tensor(mrow[:, 1:], srcf[:, :], float(NT), ioh[:, :], ALU.mult, ALU.add)

            v.tensor_scalar(nbf[:, :], pS[1][:, 512:512 + NT], float(P - 1), None, ALU.add)
            v.drain()
            v.tensor_copy(nbi[:, :], nbf[:, :])
            v.drain()
            v.tensor_scalar(nbi[:, :], nbi[:, :], 7, None, ALU.logical_shift_right)
            v.drain()
            v.tensor_copy(nbf[:, :], nbi[:, :])
            v.memset(tmp16[:, 0, :], 1.0)
            v.drain()
            v.tensor_tensor_scan(incl[:, :], tmp16[:, 0, :], nbf[:, :], 0.0, ALU.mult, ALU.add)
            v.drain()
            v.tensor_tensor(tmp16[:, 0, :], incl[:, :], identf[:, 0:NT], ALU.mult)
            v.tensor_tensor(tmp16[:, 1, :], nbf[:, :], identf[:, 0:NT], ALU.mult)
            v.drain()
            v.tensor_reduce(inclq[:, 0:2], tmp16[:, :, :], AX.X, ALU.add)
            v.memset(inclq[:, 2:3], 1.0)
            v.drain()
            v.tensor_scalar(done[:, :], iou[0:NT, :], inclq[0:NT, 0:1], None, ALU.is_ge
                            ).then_inc(done_ready, 1)
            v.wait_ge(rows_ready, 1)
            tile_of, units_before = pKT[0:1, 0:NU + 2], pO[0:1, 0:NU + 2]
            v.scalar_tensor_tensor(t0[:, :], tile_of, float(NT), iou[0:1, :], ALU.mult, ALU.add)
            v.tensor_scalar(t1[:, :], iou[0:1, :], incl[0:1, NT - 1:NT], None, ALU.is_lt)
            v.tensor_scalar(t2[:, :], tile_of, float(NT - 1), None, ALU.min)
            v.drain()
            v.scalar_tensor_tensor(t0[:, :], t0[:, :], 1.0, units_before, ALU.add, ALU.subtract)
            v.memset(utile[:, 0:1], 0)
            v.tensor_copy(utile[:, 1:], t2[:, :])
            v.tensor_scalar(t3[:, :], incl[0:1, NT - 1:NT], 1.0, None, ALU.add)
            v.drain()
            v.tensor_tensor(ucol[:, :], t0[:, :], t1[:, :], ALU.mult)
            v.tensor_copy(npair[:, 1:2], t3[:, :])
            v.drain()
            v.tensor_scalar(npair[:, 2:3], npair[:, 1:2], 1, None, ALU.logical_shift_right)
            v.drain()
            v.tensor_scalar(npair[:, 0:1], npair[:, 2:3], 1.0, None, ALU.max)

            v.wait_ge(waug, 1)
            for c in range(NC):
                v.tensor_copy(wwT[:, c, D:D + NS], pPT[:, 512 + NS * c:512 + NS * (c + 1)])
            v.tensor_copy(bh[:, D:D + NS], pPT[:, 512 + 2 * NS:512 + 3 * NS])
            v.wait_ge(vm_ready, 1)
            v.tensor_copy(vmean[:, :], pS[0][:, 0:D])
            meet(v, 1)
            vector_attention(v, 0)
            meet(v, 2)
            between(v)
            meet(v, 3)
            vector_attention(v, 1)
            meet(v, 4)
            ending(v)

        def mean_values(pe):
            for j in range(NT):
                last = pe.matmul(heads(pS[0][:, 0:D], HD), onesm[:, :], values(vrows[:, j, :]),
                                 start=(j == 0), stop=(j == NT - 1))
            last.then_inc(vm_ready, 1)

        def tensor_attention(pe, l):
            s = S[l]
            np_ = pe.value_load(npair[0:1, 0:1], min_val=1, max_val=NU // 2)
            pe.drain().then_inc(s["kt_ready"], 2)
            pe.drain().then_inc(s["s_ready"], 2)
            pe.drain().then_inc(s["pt_ready"], 2)
            pe.drain().then_inc(s["pv_done"], 2)

            def turn_keys(u, r, half):
                pe.wait_ge(s[f"k_got{r}"], half * 16 + 16)
                pe.wait_ge(s["kt_done"], u + 1)
                for c in range(NC):
                    last = pe.transpose(pKT[:, c * P:(c + 1) * P], Kg[r][:, c * P:(c + 1) * P],
                                        identf[:, :])
                last.then_inc(s["kt_ready"], 1)

            def scores(u, r, half):
                pe.wait_ge(s["mask_ready"], u + 3)
                pe.wait_ge(s["s_free" if l else "z_ready"], u + 1)
                pe.wait_ge(s[f"q_got{r}"], half * 64 + 64)
                for b in range(2):
                    pe.matmul(pS[r][:, 512 * b:512 * (b + 1)], Mb[r][:, :],
                              negi[:, :, :].rearrange("p f t -> p (f t)"), start=True, stop=False,
                              skip_group_check=True)
                pe.wait_ge(s["kt_done"], u + 2)
                for h in range(H):
                    last = pe.matmul(pS[r][:, h * P:(h + 1) * P], qz[r][:, h, :],
                                     KTs[r][:, (h // 4) * P:(h // 4 + 1) * P], start=False,
                                     stop=(h % 4 == 3), skip_group_check=True)
                last.then_inc(s["s_ready"], 1)

            def turn_weights(u, r):
                pe.wait_ge(s["exp_done"], u + 3)
                pe.wait_ge(s["pt_done"], u + 1)
                for h in range(H):
                    last = pe.transpose(pPT[:, h * P:(h + 1) * P], Pr[r][:, h * P:(h + 1) * P],
                                        identf[:, :])
                last.then_inc(s["pt_ready"], 1)

            def weigh(u, r, half):
                pe.wait_ge(s["pt_done"], u + 2)
                pe.wait_ge(s[f"v_got{r}"], half * 16 + 16)
                pe.wait_ge(s["merged"], u + 1)
                for h in range(H):
                    last = pe.matmul(pO[:, h * VW:(h + 1) * VW], PTs[r][:, h * P:(h + 1) * P],
                                     Vg[r][:, h * VW:(h + 1) * VW], start=True, stop=True)
                last.then_inc(s["pv_done"], 1)

            turn_keys(0, 0, 0)
            scores(0, 0, 0)
            turn_keys(1, 1, 0)
            with pe.Fori(0, np_) as p:
                for r in range(2):
                    u = p * 2 + r
                    scores(u + 1, 1 - r, p + r)
                    turn_weights(u, r)
                    turn_keys(u + 2, r, p + 1)
                    weigh(u, r, p)

        def dense(pe):
            m = M[0]
            with pe.Fori(0, NT // 2) as it:
                pe.wait_ge(m["ctx_ready"], it + 1)
                for k in range(2):
                    for c in range(NC):
                        last = pe.transpose(pS[0][:, (2 * k + c) * P:(2 * k + c + 1) * P],
                                            ctxr[:, k, c * P:(c + 1) * P], identf[:, :])
                last.then_inc(m["ctxT_ready"], 1)
                pe.wait_ge(m["ctxT_done"], it + 1)
                for k in range(2):
                    for c in range(NC):
                        last = pe.matmul(pS[0][:, 512 + D * k:512 + D * (k + 1)], ctxT[:, k, c, :],
                                         wo[:, c, :], start=(c == 0), stop=(c == NC - 1))
                last.then_inc(m["wo_ready"], 1)
                pe.wait_ge(m["y_ready"], it + 1)
                for c in range(NC):
                    for k in range(2):
                        last = pe.transpose(pS[1][:, (2 * c + k) * P:(2 * c + k + 1) * P],
                                            y[:, k, c * P:(c + 1) * P], identf[:, :])
                last.then_inc(m["yT_ready"], 1)
                pe.wait_ge(m["yT_done"], it + 1)
                for f in range(NF):
                    if f % 2 == 0 and f >= 4:
                        pe.wait_ge(m["h1_done"], it * (NF // 2) + (f // 2 - 1))
                    bank = (pS[1][:, 512:1024], pPT[:, 0:512])[(f // 2) % 2]
                    for c in range(NC):
                        last = pe.matmul(bank[:, (f % 2) * 2 * P:(f % 2 + 1) * 2 * P],
                                         w1[:, c, f * P:(f + 1) * P],
                                         yT[:, c, :, :].rearrange("p k t -> p (k t)"),
                                         start=(c == 0), stop=(c == NC - 1))
                    if f % 2:
                        last.then_inc(m["h1_ready"], 1)
                pe.wait_ge(m["h1_done"], it * (NF // 2) + NF // 2)
                for k in range(2):
                    for f in range(NF):
                        last = pe.matmul(pPT[:, 512 + D * k:512 + D * (k + 1)],
                                         h1[:, f, k * P:(k + 1) * P], w2[:, f, :],
                                         start=(f == 0), stop=(f == NF - 1))
                last.then_inc(m["ff_ready"], 1)
                pe.wait_ge(m["x1_ready"], it + 1)
                for k in range(2):
                    for c in range(NC):
                        last = pe.transpose(pKT[:, (2 * k + c) * P:(2 * k + c + 1) * P],
                                            x1s[:, k, c * P:(c + 1) * P], identf[:, :])
                last.then_inc(m["x1T_ready"], 1)
                pe.wait_ge(m["x1T_done"], it + 1)
                for k in range(2):
                    if k:
                        pe.wait_ge(m["h_done"], it * 2 + 1)
                    for c in range(NC):
                        last = pe.matmul(pO[:, 0:D + NS], x1T[:, k, c, :], wwT[:, c, :],
                                         start=(c == 0), stop=(c == NC - 1))
                    last.then_inc(m["h_ready"], 1)
                pe.wait_ge(m["h_done"], it * 2 + 2)
                for k in range(2):
                    for c in range(NC):
                        last = pe.transpose(pKT[:, (2 * k + c) * P:(2 * k + c + 1) * P],
                                            qrow[:, k, c * P:(c + 1) * P], identf[:, :])
                last.then_inc(m["qrT_ready"], 1)
                pe.wait_ge(m["qT_done"], it + 1)
            mean_values(pe)



        @block.tensor
        def _(pe):
            pe.drain().then_inc(xn_used, 2)
            pe.drain().then_inc(hT_used, 2)
            pe.wait_ge(consts, 1)
            pe.wait_ge(ld_w, 16 * 6)
            with pe.Fori(0, NT // 2) as it:
                def turn(j, r):
                    pe.wait_ge(xn_ready, j + 1)
                    pe.wait_ge(hT_ready, j + 1)
                    for i in range(2):
                        for c in range(NC):
                            last = pe.transpose(pS[r][:, (2 * i + c) * P:(2 * i + c + 1) * P],
                                                xn[r][:, i, c * P:(c + 1) * P], identf[:, :])
                    last.then_inc(tx_ready, 1)
                    pe.drain().then_inc(xn_used, 1)

                def project(j, r):
                    pe.wait_ge(hT_ready, j + 3)
                    pe.wait_ge(kv_done, j + 1)
                    for c in range(NC):
                        last = pe.matmul(pPT[:, 512 * r:512 * r + 512], hT[r][:, 0, c, :],
                                         wkv[:, c, :], start=(c == 0), stop=(c == NC - 1))
                    last.then_inc(kvp_ready, 1)
                    pe.wait_ge(q_done, j + 1)
                    for f in range(NC):
                        for c in range(NC):
                            last = pe.matmul((pKT, pO)[r][:, f * P:(f + 1) * P],
                                             wq[:, c, f * P:(f + 1) * P], hT[r][:, 1, c, :],
                                             start=(c == 0), stop=(c == NC - 1))
                    last.then_inc(qp_ready, 1)
                    pe.drain().then_inc(hT_used, 1)

                for r in range(2):
                    turn(it * 2 + r, r)
                for r in range(2):
                    project(it * 2 + r, r)

            pe.wait_ge(any_ready, 1)
            pe.wait_ge(hT_ready, NT + 2)
            pe.wait_ge(q_done, NT + 2)
            pe.wait_ge(kv_done, NT + 2)
            pe.matmul(pS[0][:, 512:512 + NU], before[:, :], any16[:, :], start=True, stop=False,
                      skip_group_check=True)
            for i in range(NT - 1):
                mine = any16[:, NT * i:NT * (i + 1)]
                last = pe.matmul(pS[0][:, 512 + NT * (i + 1):512 + NU].rearrange("p (n j) -> p n j", j=NT),
                                 ones16[:, :], mine.unsqueeze(1).broadcast_to([P, NT - 1 - i, NT]),
                                 start=False, stop=(i == NT - 2), skip_group_check=True)
            for i in range(NT):
                last = pe.matmul(pS[1][:, 512:512 + NT], ones16[:, :], any16[:, NT * i:NT * (i + 1)],
                                 start=(i == 0), stop=(i == NT - 1))
            last.then_inc(pos_ready, 1)
            pe.drain().then_inc(oh_used, 2)
            pe.wait_ge(pay_ready, 1)
            with pe.Fori(0, NT // 2) as it:
                for r in range(2):
                    j = it * 2 + r
                    pe.wait_ge(oh_ready, j + 1)
                    for i in range(NT):
                        last = pe.matmul(pPT[:, ds(j * 2 * NT, 2 * NT)], oneh[r][:, i, :],
                                         pay[:, ds(j + i * NT, 1), :, :].rearrange("p o w b -> p (o w b)"),
                                         start=(i == 0), stop=(i == NT - 1))
                    pe.drain().then_inc(oh_used, 1)
            pe.drain().then_inc(idx_ready, 1)
            pe.wait_ge(done_ready, 1)
            pe.matmul(pKT[0:1, 0:NU + 2], inclq[0:NT, 2:3], done[:, :], start=True, stop=True)
            pe.matmul(pO[0:1, 0:NU + 2], inclq[0:NT, 1:2], done[:, :], start=True, stop=True
                      ).then_inc(rows_ready, 1)
            pe.wait_ge(ld_late, 16 * 7)
            for c in range(NC):
                for o in range(NC):
                    pe.matmul(pPT[:, 512 + NS * c:512 + NS * (c + 1)], ww[:, o, c * P:(c + 1) * P],
                              ablk[:, o, :], start=(o == 0), stop=(o == NC - 1))
            for o in range(NC):
                last = pe.matmul(pPT[:, 512 + 2 * NS:512 + 3 * NS], bhm[:, o, :], ablk[:, o, :],
                                 start=(o == 0), stop=(o == NC - 1))
            last.then_inc(waug, 1)
            mean_values(pe)
            meet(pe, 1)
            tensor_attention(pe, 0)
            meet(pe, 2)
            dense(pe)
            meet(pe, 3)
            tensor_attention(pe, 1)
            meet(pe, 4)


def kernel(x, adj, nodemask, L0_gnn_h_target, L0_gnn_ln1_scale, L0_gnn_ln1_bias, L0_gnn_Wq,
           L0_gnn_bq, L0_gnn_Wk, L0_gnn_bk, L0_gnn_Wv, L0_gnn_bv, L0_gnn_Wo, L0_gnn_bo,
           L0_gnn_ln2_scale, L0_gnn_ln2_bias, L0_gnn_W1, L0_gnn_W2, L1_gnn_W_w, L1_gnn_W_b,
           L1_gnn_a):
    import numpy as np
    import concourse.bacc as bacc
    from concourse.bass_utils import run_bass_kernel_spmd

    def by_chunk(a, width):
        return np.asarray(a).reshape(-1, width).T

    adj_s = np.ascontiguousarray(
        np.asarray(adj).T.reshape(N, P, NT).transpose(0, 2, 1)).reshape(N * NT, P)
    host = dict(x=x, h_target=L0_gnn_h_target, adj_s=adj_s, nodemask=nodemask,
                ln1_s=L0_gnn_ln1_scale, ln1_b=L0_gnn_ln1_bias, Wq=L0_gnn_Wq,
                Wk=L0_gnn_Wk, bk=L0_gnn_bk, Wv=L0_gnn_Wv, bv=L0_gnn_bv, Wo=L0_gnn_Wo,
                bo=L0_gnn_bo, ln2_s=L0_gnn_ln2_scale, ln2_b=L0_gnn_ln2_bias, W1=L0_gnn_W1,
                W2=L0_gnn_W2, Ww=L1_gnn_W_w, WwT=np.asarray(L1_gnn_W_w).T, Wb=L1_gnn_W_b,
                ln1_sc=by_chunk(L0_gnn_ln1_scale, P), ln1_bc=by_chunk(L0_gnn_ln1_bias, P),
                bqc_d=by_chunk(L0_gnn_bq, P), Wbc=by_chunk(L1_gnn_W_b, P),
                att_a=by_chunk(L1_gnn_a, HD))
    host = {k: np.ascontiguousarray(a) for k, a in host.items()}
    nc = bacc.Bacc("TRN2", target_bir_lowering=False, num_devices=1)
    args = {k: nc.dram_tensor(f"in_{k}", a.shape, mybir.dt.from_np(a.dtype),
                              kind="ExternalInput").ap() for k, a in host.items()}
    args["out"] = nc.dram_tensor("out_0", (N, D), mybir.dt.float32, kind="ExternalOutput").ap()
    build(nc, **args)
    r = run_bass_kernel_spmd(nc, [{f"in_{k}": a for k, a in host.items()}], core_ids=[0])
    return r.results[0]["out_0"]
```

```python
import concourse.bass as bass
from concourse import mybir
from contextlib import ExitStack

P = 128
N = 2048
D = 256
H = 8
HD = D // H
NT = N // P
NC = D // P
FF = 4 * D
NF = FF // P
VW = HD + 1
PAIRS = NT // 2
NU = NT * NT
NV = NU + 6
NS = 2 * H
EPS = 1e-5
NEG = -1e30
EMPTY = -1e29
SLOPE = 0.2
AR = 4


def build(nc, ln1_sc, ln1_bc, bqc_d, Wbc, x, h_target, adj_s, nodemask, ln1_s, ln1_b, Wq, Wk, bk, Wv, bv, Wo, bo,
          ln2_s, ln2_b, W1, W2, Ww, WwT, Wb, att_a, out):
    f32, bf16, i32 = mybir.dt.float32, mybir.dt.bfloat16, mybir.dt.int32
    ALU, ACT, AX = mybir.AluOpType, mybir.ActivationFunctionType, mybir.AxisListType
    ds = bass.ds

    with ExitStack() as ctx:
        def sb(name, shape, dt=f32):
            return ctx.enter_context(nc.sbuf_tensor(name, shape, dt))

        def pb(name, shape):
            return ctx.enter_context(nc.psum_tensor(name, shape, f32))

        def sem(name):
            return ctx.enter_context(nc.semaphore(name))

        xs = sb("xs", [P, NT, D])
        ht = sb("ht", [P, NT, D])
        krows = sb("krows", [P, NT, D])
        vrows = sb("vrows", [P, NT, H * VW])
        qT = sb("qT", [P, NT, NC, P])
        macc = sb("macc", [P, NT, H])
        vmean = sb("vmean", [P, D])
        k_dram = [nc.dram_tensor(f"k_dram{l}", (N, D), f32).ap() for l in range(2)]
        v_dram = [nc.dram_tensor(f"v_dram{l}", (N, H * VW), f32).ap() for l in range(2)]

        wkv = sb("wkv", [P, NC, 2 * D])
        wq = sb("wq", [P, NC, D])
        wo = sb("wo", [P, NC, D])
        w1 = sb("w1", [P, NC, FF])
        w2 = sb("w2", [P, NF, D])
        wwT = sb("wwT", [P, NC, D + NS])
        ww = sb("ww", [P, NC, D])
        ablk = sb("ablk", [P, NC, NS])
        acol = sb("acol", [P, 2])
        bkv = sb("bkv", [P, 2 * D])
        s1bc = sb("s1bc", [P, D])
        b1bc = sb("b1bc", [P, D])
        bobc = sb("bobc", [P, D])
        s2bc = sb("s2bc", [P, D])
        b2bc = sb("b2bc", [P, D])
        bh = sb("bh", [P, D + NS])
        s1c = sb("s1c", [P, NC])
        b1c = sb("b1c", [P, NC])
        bqc = sb("bqc", [P, NC])
        bhc = sb("bhc", [P, NC])
        nmi = sb("nmi", [P, NT], i32)
        tm = sb("tm", [P, NT])
        identf = sb("identf", [P, P])
        identb = sb("identb", [P, P], bf16)
        negi = sb("negi", [P, 4, P], bf16)
        onesm = sb("onesm", [P, P])
        ones16 = sb("ones16", [P, P], bf16)
        before = sb("before", [P, P], bf16)
        nhalf = sb("nhalf", [P, 2 * NT])
        pvals = sb("pvals", [P, 1])
        ioc = sb("ioc", [P, P], bf16)
        iob = sb("iob", [P, NT], bf16)
        ioh = sb("ioh", [P, NU], bf16)
        iou = sb("iou", [P, NV])

        srow = sb("srow", [P, NU + 1], i32)
        mrow = sb("mrow", [P, NU + 1], i32)
        invalid = sb("invalid", [P, NU + 1])
        tile4 = sb("tile4", [1, NU // 2 + 1, 4], i32)
        col4 = sb("col4", [1, NU // 2, 4], i32)
        npair = sb("npair", [1, 4], i32)
        stats = sb("stats", [P, 4, 6])
        mv = sb("mv", [P, 2 * NT, 2])
        mv4 = sb("mv4", [P, 4, 2])
        ve = sb("ve", [P, 2 * NT])
        rstd = sb("rstd", [P, 2 * NT])

        ctx, whole = ExitStack(), ctx
        anyf = sb("anyf", [P, NU])
        any16 = sb("any16", [P, NU], bf16)
        place = sb("place", [P, NU])
        placei = sb("placei", [P, NU], i32)
        loi = sb("loi", [P, NU], i32)
        lof = sb("lof", [P, NU])
        hif = sb("hif", [P, NU], bf16)
        srcf = sb("srcf", [P, NU])
        nbi = sb("nbi", [P, NT], i32)
        nbf = sb("nbf", [P, NT])
        incl = sb("incl", [P, NT])
        tmp16 = sb("tmp16", [P, 2, NT])
        inclq = sb("inclq", [P, 3])
        t3 = sb("t3", [1, 1])
        xn = [sb(f"xn{r}", [P, 2, D]) for r in range(2)]
        hT = [sb(f"hT{r}", [P, 2, NC, P]) for r in range(2)]
        bhm = sb("bhm", [P, NC, P])
        ctx, group = ExitStack(), ctx
        adjb = [sb(f"adjb{r}", [P, N], i32) for r in range(AR)]
        ctx.close()
        ctx = ExitStack()
        pay = sb("pay", [P, NU, 2, NT], bf16)
        oneh = [sb(f"oneh{r}", [P, NT, P], bf16) for r in range(2)]
        ab = sb("ab", [P, NT, 2, NT])
        ucol = sb("ucol", [1, NV], i32)
        utile = sb("utile", [1, NV + 2], i32)
        done = sb("done", [NT, NV])
        t0 = sb("t0", [1, NV])
        t1 = sb("t1", [1, NV])
        t2 = sb("t2", [1, NV])
        ctx.close()
        ctx = group
        ctx.close()

        ctx = whole
        Oacc = sb("Oacc", [P, NT, H * VW])
        ctx = ExitStack()
        urow = [sb(f"urow{r}", [P, 2], i32) for r in range(2)]
        vrow = [sb(f"vrow{r}", [P, 1], i32) for r in range(2)]
        uinv = [sb(f"uinv{r}", [P, 1]) for r in range(2)]
        Kg = [sb(f"Kg{r}", [P, D]) for r in range(2)]
        Vg = [sb(f"Vg{r}", [P, H * VW]) for r in range(2)]
        Mg = [sb(f"Mg{r}", [P, P], i32) for r in range(2)]
        Mb = [sb(f"Mb{r}", [P, P], bf16) for r in range(2)]
        qz = [sb(f"qz{r}", [P, H, P]) for r in range(2)]
        KTs = [sb(f"KTs{r}", [P, D]) for r in range(2)]
        Z = [sb(f"Z{r}", [P, H * P]) for r in range(2)]
        Y = sb("Y", [P, H * P])
        Pr = [sb(f"Pr{r}", [P, H * P]) for r in range(2)]
        PTs = [sb(f"PTs{r}", [P, H * P]) for r in range(2)]
        mu = sb("mu", [P, H])
        old = [sb(f"old{r}", [P, H]) for r in range(2)]
        dm = [sb(f"dm{r}", [P, H]) for r in range(2)]
        ea = [sb(f"ea{r}", [P, H]) for r in range(2)]
        ctx.close()

        ctx = ExitStack()
        e8 = sb("e8", [P, NT, H])
        w8 = sb("w8", [P, NT, H])
        l8 = sb("l8", [P, NT, H])
        negmean = sb("negmean", [P, NT])
        shift = sb("shift", [P, NT])
        ctxr = sb("ctxr", [P, 2, D])
        tmpr = sb("tmpr", [P, 2, D])
        z = sb("z", [P, 2, D])
        y = sb("y", [P, 2, D])
        yx = sb("yx", [P, 2, D])
        ctxT = sb("ctxT", [P, 2, NC, P])
        yT = sb("yT", [P, NC, 2, P])
        h1 = sb("h1", [P, NF, 2 * P])
        x1s = sb("x1s", [P, 2, D])
        x1T = sb("x1T", [P, 2, NC, P])
        qrow = sb("qrow", [P, 2, D])
        ctx.close()
        ctx = whole

        pS = [pb(f"pS{r}", [P, H * P]) for r in range(2)]
        pPT = pb("pPT", [P, H * P])
        pKT = pb("pKT", [P, 512])
        pO = pb("pO", [P, 512])

        ld_x, ld_h, ld_w, ld_small = sem("ld_x"), sem("ld_h"), sem("ld_w"), sem("ld_small")
        ld_late = sem("ld_late")
        adj_ld = [sem(f"adj_ld{r}") for r in range(AR)]
        adj_used, consts, dconsts, waug = sem("adj_used"), sem("consts"), sem("dconsts"), sem("waug")
        ve_ready, rstd_ready = sem("ve_ready"), sem("rstd_ready")
        xn_ready, xn_used, ht_done = sem("xn_ready"), sem("xn_used"), sem("ht_done")
        tx_ready, hT_ready, hT_used = sem("tx_ready"), sem("hT_ready"), sem("hT_used")
        kvp_ready, kv_done = sem("kvp_ready"), sem("kv_done")
        qp_ready, q_done = sem("qp_ready"), sem("q_done")
        kv_stored = [sem("kv_stored0"), sem("kv_stored1")]
        any_ready, pos_ready, pay_ready = sem("any_ready"), sem("pos_ready"), sem("pay_ready")
        oh_ready, oh_used, idx_ready = sem("oh_ready"), sem("oh_used"), sem("idx_ready")
        done_ready, rows_ready = sem("done_ready"), sem("rows_ready")
        vm_ready, vm_done = sem("vm_ready"), sem("vm_done")
        phase = sem("phase")
        carrier = sem("carrier")
        out_done = sem("out_done")
        S = []
        for l in range(2):
            S.append({n: sem(f"{n}_{l}") for n in (
                "k_got0", "k_got1", "v_got0", "v_got1", "m_got0", "m_got1", "q_got0", "q_got1",
                "listed", "vlisted", "mask_ready", "kt_ready", "kt_done", "s_ready", "s_free",
                "y_ready", "z_ready", "exp_done", "ea_done", "pt_ready", "pt_done",
                "pv_done", "merged", "q_clear")})
        M = [{n: sem(f"{n}_m{l}") for n in (
            "w8_ready", "ctx_ready", "ctxT_ready", "ctxT_done", "wo_ready", "ve_ready",
            "rstd_ready", "y_ready", "yT_ready", "yT_done", "h1_ready", "h1_done", "ff_ready",
            "yx_ready", "x1_ready", "x1T_ready", "x1T_done", "h_ready", "h_done",
            "qrT_ready", "qT_done", "mean_ready", "c_ready", "relu_done", "exp_ready", "out_ready")} for l in range(2)]

        block = ctx.enter_context(nc.Block())

        def meet(e, k):
            e.drain().then_inc(phase, 1)
            e.wait_ge(phase, 5 * k)

        def load4(engine, table, p, top):
            return nc.values_load_multi_w_load_instructions(
                table[0:1, ds(p, 1), :].rearrange("o p f -> o (p f)"), engines=[engine], min_val=0,
                max_val=top)[1]

        def wait_alone(e, semaphore, value):
            e.wait_ge(semaphore, value)
            e.sem_inc(carrier, 1)

        def heads(ap, w):
            return ap.rearrange("p (h w) -> p h w", w=w)

        def values(ap):
            return heads(ap, VW)[:, :, 0:HD]

        def store_rows(g, l, j, n):
            g.dma_start(k_dram[l].rearrange("(p a) w -> p a w", a=NT)[:, ds(j, n), :],
                        krows[:, ds(j, n), :]).then_inc(kv_stored[l], 16)
            g.dma_start(v_dram[l].rearrange("(p a) w -> p a w", a=NT)[:, ds(j, n), :],
                        vrows[:, ds(j, n), :]).then_inc(kv_stored[l], 16)

        def mean_part(j):
            return qT[:, ds(j, 1), :, :].rearrange("p o c t -> p (o c t)")

        SMALL = 16 * 15

        def sync_attention(sp, l):
            s = S[l]
            np_ = sp.value_load(npair[0:1, 0:1], min_val=1, max_val=NU // 2)

            def bring(u, r, j):
                sp.wait_ge(s["s_ready"], u + 1)
                for a in range(4):
                    rows = slice(HD * a, HD * a + HD)
                    sp.dma_start(qz[r][rows, a:H:4, :],
                                 qT[rows, ds(j, 1), :, :].rearrange("p o c t -> p (o c) t")
                                 ).then_inc(s[f"q_got{r}"], 16)

            sp.wait_ge(s["q_clear"], 1)
            tiles = load4(mybir.EngineType.SP, tile4, 0, NT - 1)
            bring(0, 0, tiles[2])
            bring(1, 1, tiles[3])
            with sp.Fori(0, np_) as p:
                tiles = load4(mybir.EngineType.SP, tile4, p + 1, NT - 1)
                bring(p * 2 + 2, 0, tiles[2])
                bring(p * 2 + 3, 1, tiles[3])
            for r in range(2):
                wait_alone(sp, s[f"q_got{r}"], (np_ + 1) * 64)

        @block.sync
        def _(sp):
            sp.dma_start(xs[:, :, :], x.rearrange("(p a) d -> p a d", a=NT)).then_inc(ld_x, 16)
            sp.dma_start(ht[:, :, :], h_target.rearrange("(p a) d -> p a d", a=NT)).then_inc(ld_h, 16)
            adj_v = adj_s.rearrange("(p i j) a -> p i (j a)", i=NT, j=NT)
            for r in range(AR):
                sp.dma_start(adjb[r][:, :], adj_v[:, r, :]).then_inc(adj_ld[r], 16)
            with sp.Fori(1, NT // AR) as it:
                for r in range(AR):
                    sp.wait_ge(adj_used, it * AR + (r + 1 - AR))
                    sp.dma_start(adjb[r][:, :], adj_v[:, ds(it * AR + r, 1), :].rearrange(
                        "p i n -> p (i n)")).then_inc(adj_ld[r], 16)
            meet(sp, 1)
            sync_attention(sp, 0)
            meet(sp, 2)
            with sp.Fori(0, PAIRS) as i:
                sp.wait_ge(M[0]["h_done"], i * 2 + 2)
                store_rows(sp, 1, i * 2, 2)
            sp.wait_ge(kv_stored[1], 32 * PAIRS)
            meet(sp, 3)
            sync_attention(sp, 1)
            meet(sp, 4)
            with sp.Fori(0, PAIRS) as i:
                sp.wait_ge(M[1]["out_ready"], i + 1)
                sp.dma_start(out.rearrange("(p a) d -> p a d", a=NT)[:, ds(i * 2, 2), :],
                             krows[:, ds(i * 2, 2), :]).then_inc(out_done, 16)
            sp.wait_ge(out_done, 16 * PAIRS)

        def pool_attention(g, l):
            s = S[l]
            np_ = g.value_load(npair[0:1, 0:1], min_val=1, max_val=NU // 2)

            def sources(u, r, c):
                wait_alone(g, s["mask_ready"], u + 1)
                wait_alone(g, s["kt_ready"], u + 1)
                g.tensor_copy(urow[r][:, 0:1], srow[:, ds(c, 1)])
                g.tensor_copy(uinv[r][:, :], invalid[:, ds(c, 1)])
                g.tensor_copy(urow[r][:, 1:2], mrow[:, ds(c, 1)]).then_inc(s["listed"], 1)
                wait_alone(g, s["listed"], u + 1)
                g.indirect_dma_start(Mg[r][:, :], None, adj_s,
                                     bass.IndirectOffsetOnAxis(ap=urow[r][:, 1:2], axis=0)
                                     ).then_inc(s[f"m_got{r}"], 16)
                g.indirect_dma_start(Kg[r][:, :], None, k_dram[l],
                                     bass.IndirectOffsetOnAxis(ap=urow[r][:, 0:1], axis=0)
                                     ).then_inc(s[f"k_got{r}"], 16)

            def gather_values(r):
                g.indirect_dma_start(Vg[r][:, :], None, v_dram[l],
                                     bass.IndirectOffsetOnAxis(ap=vrow[r][:, 0:1], axis=0)
                                     ).then_inc(s[f"v_got{r}"], 16)

            def source_values(u, r, c):
                wait_alone(g, s["pv_done"], u + 1)
                g.tensor_copy(vrow[r][:, 0:1], srow[:, ds(c, 1)]).then_inc(s["vlisted"], 1)
                wait_alone(g, s["vlisted"], u + 2)
                gather_values(r)

            for r in range(2):
                last = g.memset(qz[r][:, :, :], 0.0)
            last.then_inc(s["q_clear"], 1)
            g.memset(PTs[1][:, :], 0.0)
            g.memset(vrow[1][:, :], 0).then_inc(s["vlisted"], 1)
            wait_alone(g, s["vlisted"], 1)
            gather_values(1)
            first = g.value_load(npair[0:1, 3:4], min_val=0, max_val=NU)
            sources(0, 0, first)
            columns = load4(mybir.EngineType.Pool, col4, 0, NU)
            sources(1, 1, columns[0])
            source_values(0, 0, first)
            sources(2, 0, columns[1])
            third = g.value_load(npair[0:1, 1:2], min_val=0, max_val=NU)
            sources(3, 1, third)
            with g.Fori(0, np_) as p:
                columns = load4(mybir.EngineType.Pool, col4, p, NU)
                sources(p * 2 + 4, 0, columns[2])
                source_values(p * 2 + 1, 1, columns[0])
                sources(p * 2 + 5, 1, columns[3])
                source_values(p * 2 + 2, 0, columns[1])
            for n in ("m_got", "k_got"):
                for r in range(2):
                    wait_alone(g, s[f"{n}{r}"], (np_ + 2) * 16)
            for r in range(2):
                wait_alone(g, s[f"v_got{r}"], (np_ + 1) * 16)

        @block.gpsimd
        def _(g):
            g.memset(identf[:, :], 0.0)
            g.memset(before[:, :], 1.0)
            g.memset(onesm[:, :], 1.0 / N)
            g.memset(ones16[:, :], 1.0)
            g.memset(nhalf[:, :], -0.5)
            g.memset(ablk[:, :, :], 0.0)
            g.memset(vrows[:, :, :], 1.0)
            g.iota(ioc[:, :], [[1, P]], base=0, channel_multiplier=0,
                   allow_small_or_imprecise_dtypes=True)
            g.iota(iob[:, :], [[1, NT]], base=1, channel_multiplier=0,
                   allow_small_or_imprecise_dtypes=True)
            g.iota(ioh[:, :], [[1, NT], [0, NT]], base=0, channel_multiplier=0,
                   allow_small_or_imprecise_dtypes=True)
            g.iota(iou[:, :], [[1, NV]], base=0, channel_multiplier=0,
                   allow_small_or_imprecise_dtypes=True)
            g.iota(pvals[:, :], [[0, 1]], base=1, channel_multiplier=1,
                   allow_small_or_imprecise_dtypes=True)
            g.drain()
            g.affine_select(out=identf[:, :], in_=identf[:, :], compare_op=ALU.not_equal, fill=1.0,
                            base=0, pattern=[[-1, P]], channel_multiplier=1)
            g.affine_select(out=before[:, :], in_=before[:, :], compare_op=ALU.is_ge, fill=0.0,
                            base=-1, pattern=[[1, P]], channel_multiplier=-1)
            g.drain().then_inc(consts, 1)

            g.wait_ge(ve_ready, 1)
            g.tensor_tensor(rstd[:, :], ve[:, :], nhalf[:, :], ALU.pow).then_inc(rstd_ready, 1)
            g.wait_ge(ld_small, SMALL)
            g.drain().then_inc(ht_done, 2)
            g.tensor_tensor(bobc[:, :], bobc[:, :], b1bc[:, :], ALU.add)
            g.drain()
            with g.Fori(0, NT // AR) as it:
                for k in range(AR):
                    j = it * AR + k
                    row = ht[:, ds(j, 1), :].rearrange("p o d -> p (o d)")
                    g.wait_ge(xn_ready, j + 1)
                    g.tensor_tensor(row, xn[k % 2][:, 1, :], s1bc[:, :], ALU.mult)
                    g.drain().then_inc(ht_done, 1)
                    g.tensor_tensor(row, row, bobc[:, :], ALU.add)
                wait_alone(g, kv_done, it * AR + (AR + 2))
                store_rows(g, 0, it * AR, AR)
            g.wait_ge(kv_stored[0], 32 * NT // AR)
            meet(g, 1)
            pool_attention(g, 0)
            meet(g, 2)

            m = M[0]

            def average(i):
                for k in range(2):
                    mine = Oacc[:, ds(i * 2 + k, 1), :].rearrange("p o w -> p (o w)")
                    g.tensor_tensor(heads(ctxr[:, k, :], HD), values(mine),
                                    w8[:, ds(i * 2 + k, 1), :].rearrange("p o h -> p (o h)")
                                    .unsqueeze(2).broadcast_to([P, H, HD]), ALU.mult)
                    g.tensor_tensor(heads(tmpr[:, k, :], HD), heads(vmean[:, :], HD),
                                    e8[:, ds(i * 2 + k, 1), :].rearrange("p o h -> p (o h)")
                                    .unsqueeze(2).broadcast_to([P, H, HD]), ALU.mult)
                g.drain()
                g.tensor_tensor(ctxr[:, :, :], ctxr[:, :, :], tmpr[:, :, :], ALU.add
                                ).then_inc(m["ctx_ready"], 1)

            def rsqrt(count):
                g.wait_ge(m["ve_ready"], count)
                g.tensor_tensor(rstd[:, 0:2], ve[:, 0:2], nhalf[:, 0:2], ALU.pow
                                ).then_inc(m["rstd_ready"], 1)

            def residual(i):
                g.wait_ge(m["y_ready"], i + 1)
                g.tensor_tensor(yx[:, :, :], y[:, :, :], xs[:, ds(i * 2, 2), :], ALU.add
                                ).then_inc(m["yx_ready"], 1)

            g.wait_ge(m["w8_ready"], 1)
            average(0)
            g.wait_ge(m["ctxT_ready"], 1)
            average(1)
            g.memset(qrow[:, :, :], 0.0)
            g.drain()
            g.memset(qrow[:, :, 1:D:HD], 1.0)
            rsqrt(1)
            g.memset(krows[:, :, :], 0.0)
            g.drain()
            g.memset(krows[:, :, 0:D:HD], 1.0).then_inc(consts, 1)
            residual(0)
            rsqrt(2)
            with g.Fori(1, PAIRS - 1) as i:
                rsqrt(i * 2 + 1)
                average(i + 1)
                residual(i)
                rsqrt(i * 2 + 2)
            rsqrt(PAIRS * 2 - 1)
            residual(PAIRS - 1)
            rsqrt(PAIRS * 2)
            meet(g, 3)
            pool_attention(g, 1)
            meet(g, 4)
            m = M[1]
            g.wait_ge(m["w8_ready"], 1)
            with g.Fori(0, PAIRS) as i:
                for k in range(2):
                    last = g.tensor_tensor(heads(mean_part(i * 2 + k), HD), heads(vmean[:, :], HD),
                                           e8[:, ds(i * 2 + k, 1), :].rearrange("p o h -> p (o h)")
                                           .unsqueeze(2).broadcast_to([P, H, HD]), ALU.mult)
                last.then_inc(m["mean_ready"], 1)
            with g.Fori(0, PAIRS) as i:
                pair = ds(i * 2, 2)
                wait_alone(g, m["ve_ready"], i + 1)
                g.tensor_tensor(rstd[:, pair], ve[:, pair], nhalf[:, 0:2], ALU.pow)
                g.drain()
                g.tensor_tensor(shift[:, pair], negmean[:, pair], rstd[:, pair], ALU.mult
                                ).then_inc(m["rstd_ready"], 1)

        def bcast(ap):
            return ap.partition_broadcast(P)

        def act_attention(act, l):
            s = S[l]
            np_ = act.value_load(npair[0:1, 0:1], min_val=1, max_val=NU // 2)
            act.drain().then_inc(s["kt_done"], 1)
            act.drain().then_inc(s["exp_done"], 2)
            act.drain().then_inc(s["ea_done"], 1)
            act.drain().then_inc(s["pt_done"], 1)

            act.preload_act_table(ACT.Exp)

            def keys(u, r):
                act.wait_ge(s["kt_ready"], u + 3)
                act.wait_ge(s["s_ready"], u + 1)
                act.activation(KTs[r][:, :], pKT[:, 0:D], ACT.Copy).then_inc(s["kt_done"], 1)

            def slope(u, r):
                act.wait_ge(s["s_ready"], u + 3)
                act.wait_ge(s["s_free"], u + 2)
                act.activation(Y[:, :], pS[r][:, :], ACT.Copy, scale=SLOPE).then_inc(s["y_ready"], 1)

            def weights(u, r):
                act.wait_ge(s["z_ready"], u + 3)
                act.wait_ge(s["pt_ready"], u + 1)
                act.activation(Pr[r][:, :], Z[r][:, :], ACT.Exp).then_inc(s["exp_done"], 1)
                act.activation(ea[r][:, :], dm[r][:, :], ACT.Exp).then_inc(s["ea_done"], 1)

            def transposed(u, r):
                act.wait_ge(s["pt_ready"], u + 3)
                act.wait_ge(s["pv_done"], u + 1)
                act.activation(PTs[r][:, :], pPT[:, :], ACT.Copy).then_inc(s["pt_done"], 1)

            keys(0, 0)
            keys(1, 1)
            if l == 1:
                slope(0, 0)
                slope(1, 1)
            keys(2, 0)
            with act.Fori(0, np_) as p:
                for r in range(2):
                    u = p * 2 + r
                    weights(u, r)
                    if l == 1:
                        slope(u + 2, r)
                    transposed(u, r)
                    keys(u + 3, 1 - r)

        @block.scalar
        def _(act):
            def small(dst, src):
                act.dma_start(dst, src).then_inc(ld_small, 16)

            for c in range(NC):
                rows = slice(P * c, P * c + P)
                act.dma_start(wkv[:, c, 0:D], Wk[rows, :]).then_inc(ld_w, 16)
                act.dma_start(wkv[:, c, D:2 * D], Wv[rows, :]).then_inc(ld_w, 16)
                act.dma_start(wq[:, c, :], Wq[rows, :]).then_inc(ld_w, 16)
            small(s1c[:, :], ln1_sc)
            small(b1c[:, :], ln1_bc)
            small(bqc[:, :], bqc_d)
            small(bhc[:, :], Wbc)
            small(nmi[:, :], nodemask.rearrange("(p a) -> p a", a=NT))
            small(bkv[:, 0:D], bcast(bk))
            small(bkv[:, D:2 * D], bcast(bv))
            small(s1bc[:, :], bcast(ln1_s))
            small(b1bc[:, :], bcast(ln1_b))
            small(bobc[:, :], bcast(bo))
            for q in range(4):
                small(acol[HD * q:HD * (q + 1), :], att_a)
            small(bh[:, 0:D], bcast(Wb))
            act.dma_start(wo[:, :, :], Wo.rearrange("(c p) n -> p c n", p=P)).then_inc(ld_late, 16)
            act.dma_start(w1[:, :, :], W1.rearrange("(c p) n -> p c n", p=P)).then_inc(ld_late, 16)
            act.dma_start(w2[:, :, :], W2.rearrange("(c p) n -> p c n", p=P)).then_inc(ld_late, 16)
            act.dma_start(ww[:, :, :], Ww.rearrange("(c p) n -> p c n", p=P)).then_inc(ld_late, 16)
            act.dma_start(wwT[:, :, 0:D], WwT.rearrange("(c p) n -> p c n", p=P)).then_inc(ld_late, 16)
            act.dma_start(s2bc[:, :], bcast(ln2_s)).then_inc(ld_late, 16)
            act.dma_start(b2bc[:, :], bcast(ln2_b)).then_inc(ld_late, 16)

            act.drain().then_inc(hT_ready, 2)
            act.drain().then_inc(q_done, 2)
            act.preload_act_table(ACT.Identity)
            act.wait_ge(dconsts, 1)
            with act.Fori(0, NT // 2) as it:
                def scale(j, r):
                    act.wait_ge(tx_ready, j + 1)
                    act.wait_ge(hT_used, j + 1)
                    for i in range(2):
                        for c in range(NC):
                            last = act.activation(
                                hT[r][:, i, c, :], pS[r][:, (2 * i + c) * P:(2 * i + c + 1) * P],
                                ACT.Identity, bias=b1c[:, c:c + 1], scale=s1c[:, c:c + 1])
                    last.then_inc(hT_ready, 1)

                def queries(j, r):
                    act.wait_ge(qp_ready, j + 1)
                    for c in range(NC):
                        last = act.activation(
                            qT[:, ds(j, 1), c, :].rearrange("p o t -> p (o t)"),
                            (pKT, pO)[r][:, c * P:(c + 1) * P],
                            ACT.Identity, bias=bqc[:, c:c + 1], scale=float(HD) ** -0.5)
                    last.then_inc(q_done, 1)

                for r in range(2):
                    scale(it * 2 + r, r)
                for r in range(2):
                    queries(it * 2 + r, r)
            meet(act, 1)
            act_attention(act, 0)
            meet(act, 2)
            m = M[0]
            act.preload_act_table(ACT.Gelu_apprx_tanh)

            def turned(i, src, dst, ready, done):
                act.wait_ge(m[ready], i + 1)
                act.activation(dst, src, ACT.Copy).then_inc(m[done], 1)

            def turned_ctx(i):
                turned(i, pS[0][:, 0:512], ctxT[:, :, :, :].rearrange("p k c t -> p (k c t)"),
                       "ctxT_ready", "ctxT_done")

            def turned_y(i):
                turned(i, pS[1][:, 0:512], yT[:, :, :, :].rearrange("p c k t -> p (c k t)"),
                       "yT_ready", "yT_done")

            def turned_x1(i):
                act.wait_ge(m["x1_ready"], i + 1)
                act.activation(xs[:, ds(i * 2, 2), :], x1s[:, :, :], ACT.Copy)
                turned(i, pKT[:, :], x1T[:, :, :, :].rearrange("p k c t -> p (k c t)"),
                       "x1T_ready", "x1T_done")

            def turned_q(i):
                turned(i, pKT[:, :], qT[:, ds(i * 2, 2), :, :].rearrange("p k c t -> p (k c t)"),
                       "qrT_ready", "qT_done")

            def gelu(i):
                for f in range(NF // 2):
                    act.wait_ge(m["h1_ready"], i * (NF // 2) + (f + 1))
                    act.activation(h1[:, 2 * f:2 * f + 2, :].rearrange("p f t -> p (f t)"),
                                   (pS[1][:, 512:1024], pPT[:, 0:512])[f % 2],
                                   ACT.Gelu_apprx_tanh).then_inc(m["h1_done"], 1)

            act.drain().then_inc(m["qT_done"], 1)
            turned_ctx(0)
            turned_ctx(1)
            turned_y(0)
            gelu(0)
            turned_y(1)
            with act.Fori(1, PAIRS - 1) as i:
                gelu(i)
                turned_x1(i - 1)
                turned_ctx(i + 1)
                turned_y(i + 1)
                turned_q(i - 1)
            gelu(PAIRS - 1)
            turned_x1(PAIRS - 2)
            turned_q(PAIRS - 2)
            turned_x1(PAIRS - 1)
            turned_q(PAIRS - 1)
            meet(act, 3)
            act_attention(act, 1)
            meet(act, 4)
            m = M[1]

            def exponentials(i):
                e = vrows[:, ds(i * 2, 2), 0:D]
                wait_alone(act, m["c_ready"], i + 1)
                act.activation(e, krows[:, ds(i * 2, 2), :], ACT.Relu, scale=-1.0
                               ).then_inc(m["relu_done"], 1)
                wait_alone(act, m["relu_done"], i + 1)
                act.activation(e, e, ACT.Exp, scale=-1.0).then_inc(m["exp_ready"], 1)

            def normalised(i):
                wait_alone(act, m["rstd_ready"], i + 1)
                for k in range(2):
                    j = i * 2 + k
                    last = act.activation(krows[:, ds(j, 1), :], ht[:, ds(j, 1), :], ACT.Identity,
                                          bias=shift[:, ds(j, 1)], scale=rstd[:, ds(j, 1)])
                last.then_inc(m["out_ready"], 1)

            exponentials(0)
            with act.Fori(0, PAIRS - 1) as i:
                exponentials(i + 1)
                normalised(i)
            normalised(PAIRS - 1)

        def vector_attention(v, l):
            s = S[l]
            np_ = v.value_load(npair[0:1, 0:1], min_val=1, max_val=NU // 2)
            v.memset(macc[:, :, :], NEG)
            v.memset(Oacc[:, :, :], 0.0)
            for r in range(2):
                v.memset(ea[r][:, :], 1.0)
            v.memset(pO[:, 0:H * VW], 0.0)
            v.drain().then_inc(s["mask_ready"], 2)
            v.drain().then_inc(s["s_free"], 2)
            v.drain().then_inc(s["z_ready"], 2)

            def per_tile(a, j):
                return a[:, ds(j, 1), :].rearrange("p o w -> p (o w)")

            def mask(u, r, half):
                v.wait_ge(s[f"m_got{r}"], half * 16 + 16)
                v.wait_ge(s["s_ready"], u + 1)
                v.tensor_scalar(Mb[r][:, :], Mg[r][:, :], 0.0, uinv[r][:, 0:1], ALU.is_equal, ALU.max
                                ).then_inc(s["mask_ready"], 1)

            def leak(u, r):
                v.wait_ge(s["y_ready"], u + 1)
                v.wait_ge(s["exp_done"], u + 1)
                v.tensor_tensor(Z[r][:, :], pS[r][:, :], Y[:, :], ALU.max).then_inc(s["s_free"], 1)

            def add(u, j):
                mine = per_tile(Oacc, j)
                v.wait_ge(s["pv_done"], u + 3)
                v.tensor_tensor(mine, mine, pO[:, 0:H * VW], ALU.add).then_inc(s["merged"], 1)

            def rescale(u, r, j):
                mine = per_tile(Oacc, j)
                v.wait_ge(s["ea_done"], u + 2)
                v.tensor_tensor(heads(mine, VW), heads(mine, VW),
                                ea[r][:, :].unsqueeze(2).broadcast_to([P, H, VW]), ALU.mult)

            def step(u, r, tiles):
                scores = Z[r] if l else pS[r]
                v.wait_ge(s["s_free" if l else "s_ready"], u + 3)
                v.tensor_reduce(mu[:, :], heads(scores[:, :], P), AX.X, ALU.max)
                kept = per_tile(macc, tiles[2])
                v.tensor_copy(old[r][:, :], kept)
                v.drain()
                v.tensor_tensor(kept, mu[:, :], old[r][:, :], ALU.max)
                rescale(u - 2, r, tiles[0])
                v.drain()
                v.wait_ge(s["exp_done"], u + 1)
                v.tensor_tensor(dm[r][:, :], old[r][:, :], kept, ALU.subtract)
                v.tensor_tensor(heads(Z[r][:, :], P), heads(scores[:, :], P),
                                kept.unsqueeze(2).broadcast_to([P, H, P]), ALU.subtract
                                ).then_inc(s["z_ready"], 1)
                add(u - 2, tiles[0])
                if l == 1:
                    leak(u + 1, 1 - r)

            mask(0, 0, 0)
            mask(1, 1, 0)
            if l == 1:
                leak(0, 0)
            with v.Fori(0, np_) as p:
                tiles = load4(mybir.EngineType.DVE, tile4, p, NT - 1)
                for r in range(2):
                    mask(p * 2 + (r + 2), r, p + 1)
                    step(p * 2 + r, r, tiles[r:r + 3])
            tiles = load4(mybir.EngineType.DVE, tile4, np_, NT - 1)
            for r in range(2):
                v.drain()
                rescale(np_ * 2 + (r - 2), r, tiles[r])
                v.drain()
                add(np_ * 2 + (r - 2), tiles[r])

        def averaging_weights(v, ready):
            sums = Oacc[:, :, :].rearrange("p j (h w) -> p j h w", w=VW)[:, :, :, HD]
            v.tensor_scalar(e8[:, :, :], macc[:, :, :], EMPTY, None, ALU.is_lt)
            v.drain()
            v.tensor_tensor(l8[:, :, :], e8[:, :, :], sums, ALU.add)
            v.tensor_scalar(w8[:, :, :], e8[:, :, :], -1.0, 1.0, ALU.mult, ALU.add)
            v.drain()
            v.reciprocal(l8[:, :, :], l8[:, :, :])
            v.drain()
            v.tensor_tensor(w8[:, :, :], w8[:, :, :], l8[:, :, :], ALU.mult).then_inc(ready, 1)

        def statistics(v, rows, ready):
            v.drain()
            for k in range(2):
                v.bn_stats(stats[:, k, :], rows[:, k, :])
            v.drain()
            for k in range(2):
                v.bn_aggr(mv[:, k, :], stats[:, k, :])
            v.drain()
            v.tensor_scalar(ve[:, 0:2], mv[:, 0:2, 1], EPS, None, ALU.add).then_inc(ready, 1)

        def between(v):
            m = M[0]

            def norm2(i, count):
                v.wait_ge(m["wo_ready"], i + 1)
                v.tensor_tensor(z[:, :, :], pS[0][:, 512:1024].rearrange("p (k d) -> p k d", k=2),
                                ht[:, ds(i * 2, 2), :], ALU.add)
                statistics(v, z, m["ve_ready"])
                v.wait_ge(m["rstd_ready"], count)
                for k in range(2):
                    v.tensor_scalar(y[:, k, :], z[:, k, :], mv[:, k, 0:1], rstd[:, k:k + 1],
                                    ALU.subtract, ALU.mult)
                v.drain()
                for k in range(2):
                    v.scalar_tensor_tensor(y[:, k, :], y[:, k, :], tm[:, ds(i * 2 + k, 1)],
                                           s2bc[:, :], ALU.mult, ALU.mult)
                v.drain()
                for k in range(2):
                    v.scalar_tensor_tensor(y[:, k, :], b2bc[:, :], tm[:, ds(i * 2 + k, 1)],
                                           y[:, k, :], ALU.mult, ALU.add)
                v.drain().then_inc(m["y_ready"], 1)

            def norm3(i, count):
                v.wait_ge(m["yx_ready"], i + 1)
                v.wait_ge(m["ff_ready"], i + 1)
                v.tensor_tensor(z[:, :, :], pPT[:, 512:1024].rearrange("p (k d) -> p k d", k=2),
                                yx[:, :, :], ALU.add)
                statistics(v, z, m["ve_ready"])
                v.wait_ge(m["rstd_ready"], count)
                for k in range(2):
                    v.tensor_scalar(x1s[:, k, :], z[:, k, :], mv[:, k, 0:1], rstd[:, k:k + 1],
                                    ALU.subtract, ALU.mult)
                v.drain().then_inc(m["x1_ready"], 1)

            def values_scores(i):
                for k in range(2):
                    v.wait_ge(m["h_ready"], i * 2 + (k + 1))
                    j, h = i * 2 + k, (pO, pS[1])[k]
                    v.tensor_tensor(values(vrows[:, ds(j, 1), :].rearrange("p o d -> p (o d)")),
                                    heads(h[:, 0:D], HD), heads(bh[:, 0:D], HD), ALU.add)
                    v.tensor_tensor(qrow[:, k, 0:D:HD], h[:, D:D + H], bh[:, D:D + H], ALU.add)
                    v.tensor_tensor(krows[:, ds(j, 1), 1:D:HD].rearrange("p o h -> p (o h)"),
                                    h[:, D + H:D + NS], bh[:, D + H:D + NS], ALU.add)
                    v.drain().then_inc(m["h_done"], 1)

            averaging_weights(v, m["w8_ready"])
            v.wait_ge(ld_late, 16 * 7)
            norm2(0, 1)
            v.wait_ge(m["yT_ready"], 1)
            norm2(1, 2)
            v.wait_ge(consts, 2)
            with v.Fori(1, PAIRS - 1) as i:
                norm3(i - 1, i * 2 + 1)
                values_scores(i - 1)
                norm2(i + 1, i * 2 + 2)
            norm3(PAIRS - 2, PAIRS * 2 - 1)
            values_scores(PAIRS - 2)
            norm3(PAIRS - 1, PAIRS * 2)
            values_scores(PAIRS - 1)
            v.wait_ge(vm_ready, 2)
            v.tensor_copy(vmean[:, :], pS[0][:, 0:D])

        def ending(v):
            m = M[1]

            def average(i):
                for k in range(2):
                    j = ds(i * 2 + k, 1)
                    v.tensor_tensor(heads(krows[:, j, :].rearrange("p o d -> p (o d)"), HD),
                                    values(Oacc[:, j, :].rearrange("p o w -> p (o w)")),
                                    w8[:, j, :].rearrange("p o h -> p (o h)").unsqueeze(2)
                                    .broadcast_to([P, H, HD]), ALU.mult)

            def fill(i):
                pair = krows[:, ds(i * 2, 2), :].rearrange("p k d -> p (k d)")
                v.wait_ge(m["mean_ready"], i + 1)
                v.tensor_tensor(pair, pair, qT[:, ds(i * 2, 2), :, :].rearrange("p k c t -> p (k c t)"),
                                ALU.add).then_inc(m["c_ready"], 1)

            def positive(i):
                v.scalar_tensor_tensor(ht[:, ds(i * 2, 2), :], krows[:, ds(i * 2, 2), :], 0.0,
                                       xs[:, ds(i * 2, 2), :], ALU.max, ALU.add)

            def negative(i):
                v.wait_ge(m["exp_ready"], i + 1)
                v.scalar_tensor_tensor(ht[:, ds(i * 2, 2), :], vrows[:, ds(i * 2, 2), 0:D], -1.0,
                                       ht[:, ds(i * 2, 2), :], ALU.add, ALU.add)

            def moments(i):
                for k in range(2):
                    v.bn_stats(stats[:, k, :], ht[:, ds(i * 2 + k, 1), :].rearrange("p o d -> p (o d)"))

            def gather_moments():
                for k in range(2):
                    v.bn_aggr(mv[:, k, :], stats[:, k, :])

            def hand_over(i):
                v.tensor_scalar(negmean[:, ds(i * 2, 2)], mv[:, 0:2, 0], -1.0, None, ALU.mult)
                v.tensor_scalar(ve[:, ds(i * 2, 2)], mv[:, 0:2, 1], EPS, None, ALU.add
                                ).then_inc(m["ve_ready"], 1)

            averaging_weights(v, m["w8_ready"])
            v.drain()
            average(0)
            v.drain()
            fill(0)
            v.drain()
            positive(0)
            v.drain()
            with v.Fori(0, PAIRS - 1) as i:
                average(i + 1)
                negative(i)
                v.drain()
                fill(i + 1)
                moments(i)
                v.drain()
                positive(i + 1)
                gather_moments()
                v.drain()
                hand_over(i)
            negative(PAIRS - 1)
            v.drain()
            moments(PAIRS - 1)
            v.drain()
            gather_moments()
            v.drain()
            hand_over(PAIRS - 1)

        @block.vector
        def _(v):
            v.wait_ge(ld_x, 16)
            v.wait_ge(ld_h, 16)
            with v.Fori(0, NT // 2) as it:
                for k in range(2):
                    for i, src in enumerate((xs, ht)):
                        v.bn_stats(stats[:, 2 * k + i, :],
                                   src[:, ds(it * 2 + k, 1), :].rearrange("p o d -> p (o d)"))
                v.drain()
                for k in range(4):
                    v.bn_aggr(mv4[:, k, :], stats[:, k, :])
                v.drain()
                v.tensor_copy(mv[:, ds(it * 4, 4), :], mv4[:, :, :])
            v.drain()
            v.tensor_scalar(ve[:, :], mv[:, :, 1], EPS, None, ALU.add).then_inc(ve_ready, 1)
            v.wait_ge(ld_small, SMALL)
            v.tensor_scalar(tm[:, :], nmi[:, :], 1.0, None, ALU.is_equal)
            v.tensor_scalar(bqc[:, :], bqc[:, :], float(HD) ** -0.5, None, ALU.mult)
            v.wait_ge(consts, 1)
            v.tensor_copy(identb[:, :], identf[:, :])
            v.tensor_scalar(negi[:, :, :], identf[:, :].unsqueeze(1).broadcast_to([P, 4, P]), NEG,
                            None, ALU.mult)
            for c in range(NC):
                for q in range(4):
                    rows = slice(HD * q, HD * q + HD)
                    for i in range(2):
                        h = i * H + 4 * c + q
                        v.tensor_copy(ablk[rows, c, h:h + 1], acol[rows, i:i + 1])
            v.tensor_copy(bhm[:, :, :], bhc[:, :].unsqueeze(2).broadcast_to([P, NC, P]))
            v.drain().then_inc(dconsts, 1)

            v.drain().then_inc(kv_done, 2)
            v.wait_ge(rstd_ready, 1)
            with v.Fori(0, NT // AR) as it:
                def normalise(j, r):
                    v.wait_ge(xn_used, j + 1)
                    v.wait_ge(ht_done, j + 1)
                    for i, src in enumerate((xs, ht)):
                        last = v.tensor_scalar(
                            xn[r][:, i, :], src[:, ds(j, 1), :].rearrange("p o d -> p (o d)"),
                            mv[:, ds(j * 2 + i, 1), 0:1].rearrange("p o d -> p (o d)"),
                            rstd[:, ds(j * 2 + i, 1)], ALU.subtract, ALU.mult)
                    last.then_inc(xn_ready, 1)

                def edges(j, k):
                    v.wait_ge(adj_ld[k], it * 16 + 16)
                    v.tensor_reduce(anyf[:, ds(j * NT, NT)],
                                    adjb[k][:, :].rearrange("p (j a) -> p j a", a=P), AX.X, ALU.max,
                                    apply_absolute_value=True).then_inc(adj_used, 1)

                def keys_values(j, r):
                    v.wait_ge(kvp_ready, j + 1)
                    kvp = pPT[:, 512 * r:512 * r + 512]
                    v.scalar_tensor_tensor(krows[:, ds(j, 1), :].rearrange("p o d -> p (o d)"),
                                           kvp[:, 0:D], tm[:, ds(j, 1)], bkv[:, 0:D],
                                           ALU.mult, ALU.add)
                    v.scalar_tensor_tensor(values(vrows[:, ds(j, 1), :].rearrange("p o d -> p (o d)")),
                                           heads(kvp[:, D:2 * D], HD), tm[:, ds(j, 1)],
                                           heads(bkv[:, D:2 * D], HD),
                                           ALU.mult, ALU.add).then_inc(kv_done, 1)

                for half in range(AR // 2):
                    pair = [(it * AR + (2 * half + r), r) for r in range(2)]
                    for j, r in pair:
                        normalise(j, r)
                    for j, r in pair:
                        edges(j, 2 * half + r)
                    for j, r in pair:
                        keys_values(j, r)
            v.drain()
            v.tensor_scalar(any16[:, :], anyf[:, :], 0.0, None, ALU.is_gt).then_inc(any_ready, 1)

            v.wait_ge(pos_ready, 1)
            v.scalar_tensor_tensor(place[:, :], pS[0][:, 512:512 + NU], 1.0, any16[:, :],
                                   ALU.add, ALU.mult)
            v.drain()
            v.tensor_scalar(placei[:, :], place[:, :], float(P - 1), None, ALU.add)
            v.drain()
            v.tensor_scalar(loi[:, :], placei[:, :], P - 1, None, ALU.bitwise_and)
            v.tensor_scalar(placei[:, :], placei[:, :], 7, None, ALU.logical_shift_right)
            v.drain()
            v.tensor_copy(lof[:, :], loi[:, :])
            v.tensor_copy(hif[:, :], placei[:, :])
            v.drain()
            v.tensor_tensor(pay[:, :, 1, :], hif[:, :].unsqueeze(2).broadcast_to([P, NU, NT]),
                            iob[:, :].unsqueeze(1).broadcast_to([P, NU, NT]), ALU.is_equal)
            v.drain()
            v.tensor_scalar(pay[:, :, 0, :], pay[:, :, 1, :], pvals[:, 0:1], None, ALU.mult)
            v.drain()
            v.tensor_tensor(pay[:, :, 1, :], pay[:, :, 1, :],
                            ioh[:, :].unsqueeze(2).broadcast_to([P, NU, NT]), ALU.mult)
            v.drain().then_inc(pay_ready, 1)
            with v.Fori(0, NT // 2) as it:
                for r in range(2):
                    j = it * 2 + r
                    v.wait_ge(oh_used, j + 1)
                    for i in range(NT):
                        last = v.tensor_scalar(oneh[r][:, i, :], ioc[:, :], lof[:, ds(j + i * NT, 1)],
                                               None, ALU.is_equal)
                    last.then_inc(oh_ready, 1)
            v.wait_ge(idx_ready, 1)
            v.tensor_copy(ab[:, :, :, :].rearrange("p j w b -> p (j w b)"), pPT[:, 0:512])
            v.memset(srow[:, 0:1], 0)
            v.memset(mrow[:, 0:1], 0)
            v.memset(invalid[:, 0:1], 1.0)
            v.drain()
            tiles = srcf[:, :].rearrange("p (j b) -> p j b", b=NT)
            v.scalar_tensor_tensor(tiles, ab[:, :, 0, :], float(NT), ab[:, :, 1, :],
                                   ALU.mult, ALU.add)
            v.tensor_scalar(invalid[:, 1:].rearrange("p (j b) -> p j b", b=NT), ab[:, :, 0, :], 0.0,
                            None, ALU.is_equal)
            v.drain()
            v.tensor_scalar(srcf[:, :], srcf[:, :], float(-NT), 0.0, ALU.add, ALU.max)
            v.drain()
            v.tensor_copy(srow[:, 1:], srcf[:, :])
            v.scalar_tensor_tensor(mrow[:, 1:], srcf[:, :], float(NT), ioh[:, :], ALU.mult, ALU.add)

            v.tensor_scalar(nbf[:, :], pS[1][:, 512:512 + NT], float(P - 1), None, ALU.add)
            v.drain()
            v.tensor_copy(nbi[:, :], nbf[:, :])
            v.drain()
            v.tensor_scalar(nbi[:, :], nbi[:, :], 7, None, ALU.logical_shift_right)
            v.drain()
            v.tensor_copy(nbf[:, :], nbi[:, :])
            v.memset(tmp16[:, 0, :], 1.0)
            v.drain()
            v.tensor_tensor_scan(incl[:, :], tmp16[:, 0, :], nbf[:, :], 0.0, ALU.mult, ALU.add)
            v.drain()
            v.tensor_tensor(tmp16[:, 0, :], incl[:, :], identf[:, 0:NT], ALU.mult)
            v.tensor_tensor(tmp16[:, 1, :], nbf[:, :], identf[:, 0:NT], ALU.mult)
            v.drain()
            v.tensor_reduce(inclq[:, 0:2], tmp16[:, :, :], AX.X, ALU.add)
            v.memset(inclq[:, 2:3], 1.0)
            v.drain()
            v.tensor_scalar(done[:, :], iou[0:NT, :], inclq[0:NT, 0:1], None, ALU.is_ge
                            ).then_inc(done_ready, 1)
            v.wait_ge(rows_ready, 1)
            tile_of, units_before = pKT[0:1, 0:NV], pO[0:1, 0:NV]
            v.scalar_tensor_tensor(t0[:, :], tile_of, float(NT), iou[0:1, :], ALU.mult, ALU.add)
            v.tensor_scalar(t1[:, :], iou[0:1, :], incl[0:1, NT - 1:NT], None, ALU.is_lt)
            v.tensor_scalar(t2[:, :], tile_of, float(NT - 1), None, ALU.min)
            v.drain()
            v.scalar_tensor_tensor(t0[:, :], t0[:, :], 1.0, units_before, ALU.add, ALU.subtract)
            v.memset(utile[:, 0:2], 0)
            v.tensor_copy(utile[:, 2:], t2[:, :])
            v.tensor_scalar(t3[:, :], incl[0:1, NT - 1:NT], 1.0, None, ALU.add)
            v.drain()
            v.tensor_tensor(ucol[:, :], t0[:, :], t1[:, :], ALU.mult)
            v.tensor_copy(npair[:, 1:2], t3[:, :])
            v.drain()
            v.tensor_copy(tile4[:, :, 0:2], utile[:, 0:NU + 2].rearrange("o (p f) -> o p f", f=2))
            v.tensor_copy(tile4[:, :, 2:4], utile[:, 2:NU + 4].rearrange("o (p f) -> o p f", f=2))
            v.tensor_copy(npair[:, 3:4], ucol[:, 0:1])
            v.tensor_copy(col4[:, :, 0:2], ucol[:, 1:NU + 1].rearrange("o (p f) -> o p f", f=2))
            v.tensor_copy(col4[:, :, 2:4], ucol[:, 4:NU + 4].rearrange("o (p f) -> o p f", f=2))
            v.tensor_scalar(npair[:, 2:3], npair[:, 1:2], 1, None, ALU.logical_shift_right)
            v.drain()
            v.tensor_scalar(npair[:, 0:1], npair[:, 2:3], 1.0, None, ALU.max)
            v.tensor_copy(npair[:, 1:2], ucol[:, 3:4])

            v.wait_ge(waug, 1)
            for c in range(NC):
                v.tensor_copy(wwT[:, c, D:D + NS], pPT[:, 512 + NS * c:512 + NS * (c + 1)])
            v.tensor_copy(bh[:, D:D + NS], pPT[:, 512 + 2 * NS:512 + 3 * NS])
            v.wait_ge(vm_ready, 1)
            v.tensor_copy(vmean[:, :], pS[0][:, 0:D])
            meet(v, 1)
            vector_attention(v, 0)
            meet(v, 2)
            between(v)
            meet(v, 3)
            vector_attention(v, 1)
            meet(v, 4)
            ending(v)

        def mean_values(pe):
            for j in range(NT):
                last = pe.matmul(heads(pS[0][:, 0:D], HD), onesm[:, :], values(vrows[:, j, :]),
                                 start=(j == 0), stop=(j == NT - 1))
            last.then_inc(vm_ready, 1)

        def tensor_attention(pe, l):
            s = S[l]
            np_ = pe.value_load(npair[0:1, 0:1], min_val=1, max_val=NU // 2)
            pe.drain().then_inc(s["kt_ready"], 2)
            pe.drain().then_inc(s["s_ready"], 2)
            pe.drain().then_inc(s["pt_ready"], 2)
            pe.drain().then_inc(s["pv_done"], 1)

            def turn_keys(u, r, half):
                pe.wait_ge(s[f"k_got{r}"], half * 16 + 16)
                pe.wait_ge(s["kt_done"], u + 1)
                for c in range(NC):
                    last = pe.transpose(pKT[:, c * P:(c + 1) * P], Kg[r][:, c * P:(c + 1) * P],
                                        identf[:, :])
                last.then_inc(s["kt_ready"], 1)

            def scores(u, r, half):
                pe.wait_ge(s["mask_ready"], u + 3)
                pe.wait_ge(s["s_free" if l else "z_ready"], u + 1)
                pe.wait_ge(s[f"q_got{r}"], half * 64 + 64)
                for b in range(2):
                    pe.matmul(pS[r][:, 512 * b:512 * (b + 1)], Mb[r][:, :],
                              negi[:, :, :].rearrange("p f t -> p (f t)"), start=True, stop=False,
                              skip_group_check=True)
                pe.wait_ge(s["kt_done"], u + 2)
                for h in range(H):
                    last = pe.matmul(pS[r][:, h * P:(h + 1) * P], qz[r][:, h, :],
                                     KTs[r][:, (h // 4) * P:(h // 4 + 1) * P], start=False,
                                     stop=(h % 4 == 3), skip_group_check=True)
                last.then_inc(s["s_ready"], 1)

            def turn_weights(u, r):
                pe.wait_ge(s["exp_done"], u + 3)
                pe.wait_ge(s["pt_done"], u + 1)
                for h in range(H):
                    last = pe.transpose(pPT[:, h * P:(h + 1) * P], Pr[r][:, h * P:(h + 1) * P],
                                        identf[:, :])
                last.then_inc(s["pt_ready"], 1)

            def weigh(u, r, half):
                pe.wait_ge(s["pt_done"], u + 2)
                pe.wait_ge(s[f"v_got{r}"], half * 16 + 16)
                pe.wait_ge(s["merged"], u + 2)
                for h in range(H):
                    last = pe.matmul(pO[:, h * VW:(h + 1) * VW], PTs[r][:, h * P:(h + 1) * P],
                                     Vg[r][:, h * VW:(h + 1) * VW], start=True, stop=True)
                last.then_inc(s["pv_done"], 1)

            turn_keys(0, 0, 0)
            scores(0, 0, 0)
            turn_keys(1, 1, 0)
            scores(1, 1, 0)
            turn_keys(2, 0, 1)
            with pe.Fori(0, np_) as p:
                for r in range(2):
                    u = p * 2 + r
                    scores(u + 2, r, p + 1)
                    turn_weights(u, r)
                    weigh(u - 1, 1 - r, p)
                    turn_keys(u + 3, 1 - r, p + (r + 1))
            weigh(np_ * 2 - 1, 1, np_)

        def dense(pe):
            m = M[0]

            def turn(dst, rows, order, ready):
                for b, (k, c) in enumerate(order):
                    last = pe.transpose(dst[:, b * P:(b + 1) * P], rows[:, k, c * P:(c + 1) * P],
                                        identf[:, :])
                last.then_inc(ready, 1)

            by_tile = [(k, c) for k in range(2) for c in range(NC)]
            by_chunk = [(k, c) for c in range(NC) for k in range(2)]

            def project_out(i):
                pe.wait_ge(m["ctx_ready"], i + 1)
                turn(pS[0], ctxr, by_tile, m["ctxT_ready"])
                pe.wait_ge(m["ctxT_done"], i + 1)
                for k in range(2):
                    for c in range(NC):
                        last = pe.matmul(pS[0][:, 512 + D * k:512 + D * (k + 1)], ctxT[:, k, c, :],
                                         wo[:, c, :], start=(c == 0), stop=(c == NC - 1))
                last.then_inc(m["wo_ready"], 1)

            def turn_y(i):
                pe.wait_ge(m["y_ready"], i + 1)
                turn(pS[1], y, by_chunk, m["yT_ready"])

            def widen(i):
                pe.wait_ge(m["yT_done"], i + 1)
                for f in range(NF):
                    if f % 2 == 0 and f >= 4:
                        pe.wait_ge(m["h1_done"], i * (NF // 2) + (f // 2 - 1))
                    bank = (pS[1][:, 512:1024], pPT[:, 0:512])[(f // 2) % 2]
                    for c in range(NC):
                        last = pe.matmul(bank[:, (f % 2) * 2 * P:(f % 2 + 1) * 2 * P],
                                         w1[:, c, f * P:(f + 1) * P],
                                         yT[:, c, :, :].rearrange("p k t -> p (k t)"),
                                         start=(c == 0), stop=(c == NC - 1))
                    if f % 2:
                        last.then_inc(m["h1_ready"], 1)

            def narrow(i):
                pe.wait_ge(m["h1_done"], i * (NF // 2) + NF // 2)
                for k in range(2):
                    for f in range(NF):
                        last = pe.matmul(pPT[:, 512 + D * k:512 + D * (k + 1)],
                                         h1[:, f, k * P:(k + 1) * P], w2[:, f, :],
                                         start=(f == 0), stop=(f == NF - 1))
                last.then_inc(m["ff_ready"], 1)

            def project_values(i):
                pe.wait_ge(m["x1_ready"], i + 1)
                pe.wait_ge(m["qT_done"], i + 1)
                turn(pKT, x1s, by_tile, m["x1T_ready"])
                pe.wait_ge(m["x1T_done"], i + 1)
                for k in range(2):
                    for c in range(NC):
                        last = pe.matmul((pO, pS[1])[k][:, 0:D + NS], x1T[:, k, c, :], wwT[:, c, :],
                                         start=(c == 0), stop=(c == NC - 1))
                    last.then_inc(m["h_ready"], 1)

            def turn_queries(i):
                pe.wait_ge(m["h_done"], i * 2 + 2)
                turn(pKT, qrow, by_tile, m["qrT_ready"])

            project_out(0)
            pe.wait_ge(m["ve_ready"], 1)
            project_out(1)
            turn_y(0)
            widen(0)
            narrow(0)
            turn_y(1)
            with pe.Fori(1, PAIRS - 1) as i:
                widen(i)
                project_values(i - 1)
                project_out(i + 1)
                narrow(i)
                pe.wait_ge(m["h_done"], i * 2)
                turn_y(i + 1)
                turn_queries(i - 1)
            widen(PAIRS - 1)
            project_values(PAIRS - 2)
            narrow(PAIRS - 1)
            turn_queries(PAIRS - 2)
            project_values(PAIRS - 1)
            turn_queries(PAIRS - 1)
            pe.wait_ge(m["qT_done"], PAIRS + 1)
            mean_values(pe)



        @block.tensor
        def _(pe):
            pe.drain().then_inc(xn_used, 2)
            pe.drain().then_inc(hT_used, 2)
            pe.wait_ge(consts, 1)
            pe.wait_ge(ld_w, 16 * 6)
            with pe.Fori(0, NT // 2) as it:
                def turn(j, r):
                    pe.wait_ge(xn_ready, j + 1)
                    pe.wait_ge(hT_ready, j + 1)
                    for i in range(2):
                        for c in range(NC):
                            last = pe.transpose(pS[r][:, (2 * i + c) * P:(2 * i + c + 1) * P],
                                                xn[r][:, i, c * P:(c + 1) * P], identf[:, :])
                    last.then_inc(tx_ready, 1)
                    pe.drain().then_inc(xn_used, 1)

                def project(j, r):
                    pe.wait_ge(hT_ready, j + 3)
                    pe.wait_ge(kv_done, j + 1)
                    for c in range(NC):
                        last = pe.matmul(pPT[:, 512 * r:512 * r + 512], hT[r][:, 0, c, :],
                                         wkv[:, c, :], start=(c == 0), stop=(c == NC - 1))
                    last.then_inc(kvp_ready, 1)
                    pe.wait_ge(q_done, j + 1)
                    for f in range(NC):
                        for c in range(NC):
                            last = pe.matmul((pKT, pO)[r][:, f * P:(f + 1) * P],
                                             wq[:, c, f * P:(f + 1) * P], hT[r][:, 1, c, :],
                                             start=(c == 0), stop=(c == NC - 1))
                    last.then_inc(qp_ready, 1)
                    pe.drain().then_inc(hT_used, 1)

                for r in range(2):
                    turn(it * 2 + r, r)
                for r in range(2):
                    project(it * 2 + r, r)

            pe.wait_ge(any_ready, 1)
            pe.wait_ge(hT_ready, NT + 2)
            pe.wait_ge(q_done, NT + 2)
            pe.wait_ge(kv_done, NT + 2)
            pe.matmul(pS[0][:, 512:512 + NU], before[:, :], any16[:, :], start=True, stop=False,
                      skip_group_check=True)
            for i in range(NT - 1):
                mine = any16[:, NT * i:NT * (i + 1)]
                last = pe.matmul(pS[0][:, 512 + NT * (i + 1):512 + NU].rearrange("p (n j) -> p n j", j=NT),
                                 ones16[:, :], mine.unsqueeze(1).broadcast_to([P, NT - 1 - i, NT]),
                                 start=False, stop=(i == NT - 2), skip_group_check=True)
            for i in range(NT):
                last = pe.matmul(pS[1][:, 512:512 + NT], ones16[:, :], any16[:, NT * i:NT * (i + 1)],
                                 start=(i == 0), stop=(i == NT - 1))
            last.then_inc(pos_ready, 1)
            pe.drain().then_inc(oh_used, 2)
            pe.wait_ge(pay_ready, 1)
            with pe.Fori(0, NT // 2) as it:
                for r in range(2):
                    j = it * 2 + r
                    pe.wait_ge(oh_ready, j + 1)
                    for i in range(NT):
                        last = pe.matmul(pPT[:, ds(j * 2 * NT, 2 * NT)], oneh[r][:, i, :],
                                         pay[:, ds(j + i * NT, 1), :, :].rearrange("p o w b -> p (o w b)"),
                                         start=(i == 0), stop=(i == NT - 1))
                    pe.drain().then_inc(oh_used, 1)
            pe.drain().then_inc(idx_ready, 1)
            pe.wait_ge(done_ready, 1)
            pe.matmul(pKT[0:1, 0:NV], inclq[0:NT, 2:3], done[:, :], start=True, stop=True)
            pe.matmul(pO[0:1, 0:NV], inclq[0:NT, 1:2], done[:, :], start=True, stop=True
                      ).then_inc(rows_ready, 1)
            pe.wait_ge(ld_late, 16 * 7)
            for c in range(NC):
                for o in range(NC):
                    pe.matmul(pPT[:, 512 + NS * c:512 + NS * (c + 1)], ww[:, o, c * P:(c + 1) * P],
                              ablk[:, o, :], start=(o == 0), stop=(o == NC - 1))
            for o in range(NC):
                last = pe.matmul(pPT[:, 512 + 2 * NS:512 + 3 * NS], bhm[:, o, :], ablk[:, o, :],
                                 start=(o == 0), stop=(o == NC - 1))
            last.then_inc(waug, 1)
            mean_values(pe)
            meet(pe, 1)
            tensor_attention(pe, 0)
            meet(pe, 2)
            dense(pe)
            meet(pe, 3)
            tensor_attention(pe, 1)
            meet(pe, 4)


def kernel(x, adj, nodemask, L0_gnn_h_target, L0_gnn_ln1_scale, L0_gnn_ln1_bias, L0_gnn_Wq,
           L0_gnn_bq, L0_gnn_Wk, L0_gnn_bk, L0_gnn_Wv, L0_gnn_bv, L0_gnn_Wo, L0_gnn_bo,
           L0_gnn_ln2_scale, L0_gnn_ln2_bias, L0_gnn_W1, L0_gnn_W2, L1_gnn_W_w, L1_gnn_W_b,
           L1_gnn_a):
    import numpy as np
    import concourse.bacc as bacc
    from concourse.bass_utils import run_bass_kernel_spmd

    def by_chunk(a, width):
        return np.asarray(a).reshape(-1, width).T

    adj_s = np.ascontiguousarray(
        np.asarray(adj).T.reshape(N, P, NT).transpose(0, 2, 1)).reshape(N * NT, P)
    host = dict(x=x, h_target=L0_gnn_h_target, adj_s=adj_s, nodemask=nodemask,
                ln1_s=L0_gnn_ln1_scale, ln1_b=L0_gnn_ln1_bias, Wq=L0_gnn_Wq,
                Wk=L0_gnn_Wk, bk=L0_gnn_bk, Wv=L0_gnn_Wv, bv=L0_gnn_bv, Wo=L0_gnn_Wo,
                bo=L0_gnn_bo, ln2_s=L0_gnn_ln2_scale, ln2_b=L0_gnn_ln2_bias, W1=L0_gnn_W1,
                W2=L0_gnn_W2, Ww=L1_gnn_W_w, WwT=np.asarray(L1_gnn_W_w).T, Wb=L1_gnn_W_b,
                ln1_sc=by_chunk(L0_gnn_ln1_scale, P), ln1_bc=by_chunk(L0_gnn_ln1_bias, P),
                bqc_d=by_chunk(L0_gnn_bq, P), Wbc=by_chunk(L1_gnn_W_b, P),
                att_a=by_chunk(L1_gnn_a, HD))
    host = {k: np.ascontiguousarray(a) for k, a in host.items()}
    nc = bacc.Bacc("TRN2", target_bir_lowering=False, num_devices=1)
    args = {k: nc.dram_tensor(f"in_{k}", a.shape, mybir.dt.from_np(a.dtype),
                              kind="ExternalInput").ap() for k, a in host.items()}
    args["out"] = nc.dram_tensor("out_0", (N, D), mybir.dt.float32, kind="ExternalOutput").ap()
    build(nc, **args)
    r = run_bass_kernel_spmd(nc, [{f"in_{k}": a for k, a in host.items()}], core_ids=[0])
    return r.results[0]["out_0"]
```

```python
import concourse.bass as bass
from concourse import mybir
from contextlib import ExitStack

P = 128
N = 2048
D = 256
H = 8
HD = D // H
NT = N // P
NC = D // P
FF = 4 * D
NF = FF // P
VW = HD + 1
PAIRS = NT // 2
NU = NT * NT
NV = NU + 6
NS = 2 * H
EPS = 1e-5
NEG = -1e30
EMPTY = -1e29
SLOPE = 0.2
AR = 4


def build(nc, x, h_target, adj_s, nodemask, ln1_s, ln1_b, ln1_sc, ln1_bc, Wq, bqc_d, Wk, bk, Wv, bv,
          Wo, bo, ln2_s, ln2_b, W1, W2, Ww, WwT, Wb, Wbc, att_a, out):
    f32, i32 = mybir.dt.float32, mybir.dt.int32
    bf16, f16 = mybir.dt.bfloat16, mybir.dt.float16
    ALU, ACT, AX = mybir.AluOpType, mybir.ActivationFunctionType, mybir.AxisListType
    ds = bass.ds

    with ExitStack() as ctx:
        def sb(name, shape, dt=f32):
            return ctx.enter_context(nc.sbuf_tensor(name, shape, dt))

        def pb(name, shape):
            return ctx.enter_context(nc.psum_tensor(name, shape, f32))

        def sem(name):
            return ctx.enter_context(nc.semaphore(name))

        xs = sb("xs", [P, NT, D])
        ht = sb("ht", [P, NT, D])
        krows = sb("krows", [P, NT, D])
        vrows = sb("vrows", [P, NT, H * VW])
        qT = sb("qT", [P, NT, NC, P])
        macc = sb("macc", [P, NT, H])
        vmean = sb("vmean", [P, D])
        k_dram = [nc.dram_tensor(f"k_dram{l}", (N, D), f32).ap() for l in range(2)]
        v_dram = [nc.dram_tensor(f"v_dram{l}", (N, H * VW), f32).ap() for l in range(2)]

        wkv = sb("wkv", [P, NC, 2 * D])
        wq = sb("wq", [P, NC, D])
        wo = sb("wo", [P, NC, D])
        w1 = sb("w1", [P, NC, FF])
        w2 = sb("w2", [P, NF, D])
        wwT = sb("wwT", [P, NC, D + NS])
        ww = sb("ww", [P, NC, D])
        ablk = sb("ablk", [P, NC, NS])
        acol = sb("acol", [P, 2])
        bkv = sb("bkv", [P, 2 * D])
        s1bc = sb("s1bc", [P, D])
        b1bc = sb("b1bc", [P, D])
        bobc = sb("bobc", [P, D])
        s2bc = sb("s2bc", [P, D])
        b2bc = sb("b2bc", [P, D])
        bh = sb("bh", [P, D + NS])
        s1c = sb("s1c", [P, NC])
        b1c = sb("b1c", [P, NC])
        bqc = sb("bqc", [P, NC])
        bhc = sb("bhc", [P, NC])
        nmi = sb("nmi", [P, NT], i32)
        tm = sb("tm", [P, NT])
        identf = sb("identf", [P, P])
        negi = sb("negi", [P, 4, P], bf16)
        onesm = sb("onesm", [P, P])
        ones16 = sb("ones16", [P, P], bf16)
        before = sb("before", [P, P], bf16)
        nhalf = sb("nhalf", [P, 2 * NT])
        ioc = sb("ioc", [P, P], f16)
        ioh = sb("ioh", [P, NU], bf16)
        iou = sb("iou", [P, NV])

        srow = sb("srow", [P, NU + 1], i32)
        mrow = sb("mrow", [P, NU + 1], i32)
        invalid = sb("invalid", [P, NU + 1])
        tile4 = sb("tile4", [1, NU // 2 + 1, 4], i32)
        col4 = sb("col4", [1, NU // 2, 4], i32)
        npair = sb("npair", [1, 4], i32)
        stats = sb("stats", [P, 4, 6])
        mv = sb("mv", [P, 2 * NT, 2])
        ve = sb("ve", [P, 2 * NT])
        rstd = sb("rstd", [P, 2 * NT])
        negmean = sb("negmean", [P, 2 * NT])
        shift = sb("shift", [P, 2 * NT])

        ctx, whole = ExitStack(), ctx
        xstats = sb("xstats", [P, 2 * NT, 6])
        idp1 = sb("idp1", [P, NU])
        anyf = sb("anyf", [P, NU])
        any16 = sb("any16", [P, NU], bf16)
        place = sb("place", [P, NU])
        placei = sb("placei", [P, NU], i32)
        loi = sb("loi", [P, NU], i32)
        lof = sb("lof", [P, NU])
        hif = sb("hif", [P, NU])
        srcf = sb("srcf", [P, NU])
        nbi = sb("nbi", [P, NT], i32)
        nbf = sb("nbf", [P, NT])
        incl = sb("incl", [P, NT])
        tmp16 = sb("tmp16", [P, 2, NT])
        inclq = sb("inclq", [P, 3])
        t3 = sb("t3", [1, 1])
        xn = [sb(f"xn{r}", [P, 2, D]) for r in range(2)]
        hT = [sb(f"hT{r}", [P, 2, NC, P]) for r in range(2)]
        bhm = sb("bhm", [P, NC, P])
        ctx, group = ExitStack(), ctx
        adjb = [sb(f"adjb{r}", [P, N], i32) for r in range(AR)]
        ctx.close()
        ctx = ExitStack()
        pay = sb("pay", [P, NU, NT], f16)
        oneh = [sb(f"oneh{r}", [P, NT, P], f16) for r in range(2)]
        node1 = sb("node1", [P, NU])
        ucol = sb("ucol", [1, NV], i32)
        utile = sb("utile", [1, NV + 2], i32)
        done = sb("done", [NT, NV])
        t0 = sb("t0", [1, NV])
        t1 = sb("t1", [1, NV])
        t2 = sb("t2", [1, NV])
        ctx.close()
        ctx = group
        ctx.close()

        ctx = whole
        Oacc = sb("Oacc", [P, NT, H * VW])
        ctx = ExitStack()
        urow = [sb(f"urow{r}", [P, 2], i32) for r in range(2)]
        vrow = [sb(f"vrow{r}", [P, 1], i32) for r in range(2)]
        uinv = [sb(f"uinv{r}", [P, 1]) for r in range(2)]
        Kg = [sb(f"Kg{r}", [P, D]) for r in range(2)]
        Vg = [sb(f"Vg{r}", [P, H * VW]) for r in range(2)]
        Mg = [sb(f"Mg{r}", [P, P], i32) for r in range(2)]
        Mb = [sb(f"Mb{r}", [P, P], bf16) for r in range(2)]
        qz = [sb(f"qz{r}", [P, H, P]) for r in range(2)]
        KTs = [sb(f"KTs{r}", [P, D]) for r in range(2)]
        Z = [sb(f"Z{r}", [P, H * P]) for r in range(2)]
        Y = sb("Y", [P, H * P])
        Pr = [sb(f"Pr{r}", [P, H * P]) for r in range(2)]
        PTs = [sb(f"PTs{r}", [P, H * P]) for r in range(2)]
        mu = sb("mu", [P, H])
        old = [sb(f"old{r}", [P, H]) for r in range(2)]
        dm = [sb(f"dm{r}", [P, H]) for r in range(2)]
        ea = [sb(f"ea{r}", [P, H]) for r in range(2)]
        ctx.close()

        ctx = ExitStack()
        e8 = sb("e8", [P, NT, H])
        w8 = sb("w8", [P, NT, H])
        l8 = sb("l8", [P, NT, H])
        ctxr = sb("ctxr", [P, 2, D])
        tmpr = sb("tmpr", [P, 2, D])
        z = sb("z", [P, 2, D])
        y = sb("y", [P, 2, D])
        yx = sb("yx", [P, 2, D])
        ctxT = sb("ctxT", [P, 2, NC, P])
        yT = sb("yT", [P, NC, 2, P])
        h1 = sb("h1", [P, NF, 2 * P])
        x1s = sb("x1s", [P, 2, D])
        x1T = sb("x1T", [P, 2, NC, P])
        qrow = sb("qrow", [P, 2, D])
        ctx.close()
        ctx = whole

        pS = [pb(f"pS{r}", [P, H * P]) for r in range(2)]
        pPT = pb("pPT", [P, H * P])
        pKT = pb("pKT", [P, 512])
        pO = pb("pO", [P, 512])

        ld_x, ld_h = [[sem(f"{n}{part}") for part in range(2)] for n in ("ld_x", "ld_h")]
        ld_w, ld_small = sem("ld_w"), sem("ld_small")
        ld_late, ld_mid = sem("ld_late"), sem("ld_mid")
        adj_ld = [sem(f"adj_ld{r}") for r in range(AR)]
        adj_used, consts, dconsts, waug = sem("adj_used"), sem("consts"), sem("dconsts"), sem("waug")
        ve_ready, rstd_ready = sem("ve_ready"), sem("rstd_ready")
        xn_ready, ht_done = sem("xn_ready"), sem("ht_done")
        tx_ready, hT_ready = sem("tx_ready"), sem("hT_ready")
        kvp_ready, kv_done = sem("kvp_ready"), sem("kv_done")
        qp_ready, q_done = sem("qp_ready"), sem("q_done")
        kv_stored = [sem("kv_stored0"), sem("kv_stored1")]
        any_ready, pos_ready, pay_ready = sem("any_ready"), sem("pos_ready"), sem("pay_ready")
        oh_ready, oh_used, idx_ready = sem("oh_ready"), sem("oh_used"), sem("idx_ready")
        done_ready, rows_ready = sem("done_ready"), sem("rows_ready")
        vm_ready = sem("vm_ready")
        phase = sem("phase")
        carrier = sem("carrier")
        out_done = sem("out_done")
        S = []
        for l in range(2):
            S.append({n: sem(f"{n}_{l}") for n in (
                "k_got0", "k_got1", "v_got0", "v_got1", "m_got0", "m_got1", "q_got0", "q_got1",
                "listed", "vlisted", "mask_ready", "kt_ready", "kt_done", "s_ready", "s_free",
                "y_ready", "z_ready", "exp_done", "ea_done", "pt_ready", "pt_done",
                "pv_done", "merged", "q_clear")})
        M = [{n: sem(f"{n}_m{l}") for n in (
            "w8_ready", "ctx_ready", "ctxT_ready", "ctxT_done", "wo_ready", "ve_ready",
            "rstd_ready", "y_ready", "yT_ready", "yT_done", "h1_ready", "h1_done", "ff_ready",
            "yx_ready", "x1_ready", "x1T_ready", "x1T_done", "h_ready", "h_done",
            "qrT_ready", "qT_done", "parts_ready", "c_ready", "relu_done", "exp_ready",
            "out_ready")} for l in range(2)]

        block = ctx.enter_context(nc.Block())

        def meet(e, k):
            e.drain().then_inc(phase, 1)
            e.wait_ge(phase, 5 * k)

        NORM_PARTS = [(0, 0, AR), (1, NT, NT + AR), (0, AR, NT), (1, NT + AR, 2 * NT)]

        def load4(engine, table, p, top):
            return nc.values_load_multi_w_load_instructions(
                table[0:1, ds(p, 1), :].rearrange("o p f -> o (p f)"), engines=[engine], min_val=0,
                max_val=top)[1]

        def wait_alone(e, semaphore, value):
            e.wait_ge(semaphore, value)
            e.sem_inc(carrier, 1)

        def heads(ap, w):
            return ap.rearrange("p (h w) -> p h w", w=w)

        def values(ap):
            return heads(ap, VW)[:, :, 0:HD]

        def store_rows(g, l, j, n):
            g.dma_start(k_dram[l].rearrange("(p a) w -> p a w", a=NT)[:, ds(j, n), :],
                        krows[:, ds(j, n), :]).then_inc(kv_stored[l], 16)
            g.dma_start(v_dram[l].rearrange("(p a) w -> p a w", a=NT)[:, ds(j, n), :],
                        vrows[:, ds(j, n), :]).then_inc(kv_stored[l], 16)

        def mean_part(j):
            return qT[:, ds(j, 1), :, :].rearrange("p o c t -> p (o c t)")

        def rows(w):
            return w.rearrange("(c p) n -> p c n", p=P)

        def bcast(ap):
            return ap.partition_broadcast(P)

        SMALL, LATE = 16 * 9, 16 * 8

        def sync_attention(sp, l):
            s = S[l]
            np_ = sp.value_load(npair[0:1, 0:1], min_val=1, max_val=NU // 2)

            def bring(u, r, j):
                sp.wait_ge(s["s_ready"], u + 1)
                for a in range(4):
                    rows = slice(HD * a, HD * a + HD)
                    sp.dma_start(qz[r][rows, a:H:4, :],
                                 qT[rows, ds(j, 1), :, :].rearrange("p o c t -> p (o c) t")
                                 ).then_inc(s[f"q_got{r}"], 16)

            sp.wait_ge(s["q_clear"], 1)
            tiles = load4(mybir.EngineType.SP, tile4, 0, NT - 1)
            bring(0, 0, tiles[2])
            bring(1, 1, tiles[3])
            with sp.Fori(0, np_) as p:
                tiles = load4(mybir.EngineType.SP, tile4, p + 1, NT - 1)
                bring(p * 2 + 2, 0, tiles[2])
                bring(p * 2 + 3, 1, tiles[3])
            for r in range(2):
                wait_alone(sp, s[f"q_got{r}"], (np_ + 1) * 64)

        @block.sync
        def _(sp):
            for part, (lo, hi) in enumerate(((0, AR), (AR, NT))):
                sp.dma_start(xs[:, lo:hi, :], x.rearrange("(p a) d -> p a d", a=NT)[:, lo:hi, :]
                             ).then_inc(ld_x[part], 16)
                sp.dma_start(ht[:, lo:hi, :], h_target.rearrange("(p a) d -> p a d", a=NT)[:, lo:hi, :]
                             ).then_inc(ld_h[part], 16)
            adj_v = adj_s.rearrange("(p i j) a -> p i (j a)", i=NT, j=NT)
            sp.wait_ge(ld_x[1], 16)
            for r in range(AR):
                sp.dma_start(adjb[r][:, :], adj_v[:, r, :]).then_inc(adj_ld[r], 16)
            with sp.Fori(1, NT // AR) as it:
                for r in range(AR):
                    sp.wait_ge(adj_used, it * AR + (r + 1 - AR))
                    sp.dma_start(adjb[r][:, :], adj_v[:, ds(it * AR + r, 1), :].rearrange(
                        "p i n -> p (i n)")).then_inc(adj_ld[r], 16)
            sp.dma_start(wo[:, :, :], rows(Wo)).then_inc(ld_mid, 16)
            sp.dma_start(w1[:, :, :], rows(W1)).then_inc(ld_mid, 16)
            sp.dma_start(w2[:, :, :], rows(W2)).then_inc(ld_mid, 16)
            sp.dma_start(s2bc[:, :], bcast(ln2_s)).then_inc(ld_mid, 16)
            sp.dma_start(b2bc[:, :], bcast(ln2_b)).then_inc(ld_mid, 16)
            with sp.Fori(0, NT // AR) as it:
                sp.wait_ge(kv_done, it * AR + (AR + 2))
                store_rows(sp, 0, it * AR, AR)
            sp.wait_ge(kv_stored[0], 32 * NT // AR)
            sp.wait_ge(ld_mid, 16 * 5)
            meet(sp, 1)
            sync_attention(sp, 0)
            meet(sp, 2)
            with sp.Fori(0, PAIRS) as i:
                sp.wait_ge(M[0]["h_done"], i * 2 + 2)
                store_rows(sp, 1, i * 2, 2)
            sp.wait_ge(kv_stored[1], 32 * PAIRS)
            meet(sp, 3)
            sync_attention(sp, 1)
            meet(sp, 4)
            with sp.Fori(0, PAIRS) as i:
                sp.wait_ge(M[1]["out_ready"], i + 1)
                sp.dma_start(out.rearrange("(p a) d -> p a d", a=NT)[:, ds(i * 2, 2), :],
                             krows[:, ds(i * 2, 2), :]).then_inc(out_done, 16)
            sp.wait_ge(out_done, 16 * PAIRS)

        def pool_attention(g, l):
            s = S[l]
            np_ = g.value_load(npair[0:1, 0:1], min_val=1, max_val=NU // 2)

            def sources(u, r, c):
                wait_alone(g, s["mask_ready"], u + 1)
                wait_alone(g, s["kt_ready"], u + 1)
                g.tensor_copy(urow[r][:, 0:1], srow[:, ds(c, 1)])
                g.tensor_copy(uinv[r][:, :], invalid[:, ds(c, 1)])
                g.tensor_copy(urow[r][:, 1:2], mrow[:, ds(c, 1)]).then_inc(s["listed"], 1)
                wait_alone(g, s["listed"], u + 1)
                g.indirect_dma_start(Mg[r][:, :], None, adj_s,
                                     bass.IndirectOffsetOnAxis(ap=urow[r][:, 1:2], axis=0)
                                     ).then_inc(s[f"m_got{r}"], 16)
                g.indirect_dma_start(Kg[r][:, :], None, k_dram[l],
                                     bass.IndirectOffsetOnAxis(ap=urow[r][:, 0:1], axis=0)
                                     ).then_inc(s[f"k_got{r}"], 16)

            def gather_values(r):
                g.indirect_dma_start(Vg[r][:, :], None, v_dram[l],
                                     bass.IndirectOffsetOnAxis(ap=vrow[r][:, 0:1], axis=0)
                                     ).then_inc(s[f"v_got{r}"], 16)

            def source_values(u, r, c):
                wait_alone(g, s["pv_done"], u + 1)
                g.tensor_copy(vrow[r][:, 0:1], srow[:, ds(c, 1)]).then_inc(s["vlisted"], 1)
                wait_alone(g, s["vlisted"], u + 2)
                gather_values(r)

            first = g.value_load(npair[0:1, 3:4], min_val=0, max_val=NU)
            sources(0, 0, first)
            columns = load4(mybir.EngineType.Pool, col4, 0, NU)
            sources(1, 1, columns[0])
            g.memset(PTs[1][:, :], 0.0)
            g.memset(vrow[1][:, :], 0).then_inc(s["vlisted"], 1)
            wait_alone(g, s["vlisted"], 1)
            gather_values(1)
            source_values(0, 0, first)
            sources(2, 0, columns[1])
            third = g.value_load(npair[0:1, 1:2], min_val=0, max_val=NU)
            sources(3, 1, third)
            with g.Fori(0, np_) as p:
                columns = load4(mybir.EngineType.Pool, col4, p, NU)
                sources(p * 2 + 4, 0, columns[2])
                source_values(p * 2 + 1, 1, columns[0])
                sources(p * 2 + 5, 1, columns[3])
                source_values(p * 2 + 2, 0, columns[1])
            for n in ("m_got", "k_got"):
                for r in range(2):
                    wait_alone(g, s[f"{n}{r}"], (np_ + 2) * 16)
            for r in range(2):
                wait_alone(g, s[f"v_got{r}"], (np_ + 1) * 16)

        @block.gpsimd
        def _(g):
            g.memset(identf[:, :], 0.0)
            g.memset(before[:, :], 1.0)
            g.memset(onesm[:, :], 1.0 / N)
            g.memset(ones16[:, :], 1.0)
            g.memset(nhalf[:, :], -0.5)
            g.memset(ablk[:, :, :], 0.0)
            g.iota(ioc[:, :], [[1, P]], base=0, channel_multiplier=0,
                   allow_small_or_imprecise_dtypes=True)
            g.iota(ioh[:, :], [[1, NT], [0, NT]], base=0, channel_multiplier=0,
                   allow_small_or_imprecise_dtypes=True)
            g.iota(iou[:, :], [[1, NV]], base=0, channel_multiplier=0,
                   allow_small_or_imprecise_dtypes=True)
            g.drain()
            g.affine_select(out=identf[:, :], in_=identf[:, :], compare_op=ALU.not_equal, fill=1.0,
                            base=0, pattern=[[-1, P]], channel_multiplier=1)
            g.affine_select(out=before[:, :], in_=before[:, :], compare_op=ALU.is_ge, fill=0.0,
                            base=-1, pattern=[[1, P]], channel_multiplier=-1)
            g.drain().then_inc(consts, 1)

            def rsqrt(n):
                _, lo, hi = NORM_PARTS[n]
                g.wait_ge(ve_ready, n + 1)
                g.tensor_tensor(rstd[:, lo:hi], ve[:, lo:hi], nhalf[:, lo:hi], ALU.pow)
                g.drain()
                g.tensor_tensor(shift[:, lo:hi], negmean[:, lo:hi], rstd[:, lo:hi], ALU.mult
                                ).then_inc(rstd_ready, 1)

            def residual(j, r):
                row = ht[:, ds(j, 1), :].rearrange("p o d -> p (o d)")
                g.wait_ge(xn_ready, j + 1)
                g.tensor_tensor(row, xn[r][:, 1, :], s1bc[:, :], ALU.mult)
                g.drain().then_inc(ht_done, 1)
                g.tensor_tensor(row, row, bobc[:, :], ALU.add)

            rsqrt(0)
            rsqrt(1)
            g.drain().then_inc(ht_done, 2)
            g.memset(vrows[:, :, HD:H * VW:VW], 1.0)
            g.iota(idp1[:, :], [[1, NT], [0, NT]], base=1, channel_multiplier=NT,
                   allow_small_or_imprecise_dtypes=True).then_inc(consts, 1)
            g.wait_ge(ld_small, SMALL)
            g.tensor_tensor(bobc[:, :], bobc[:, :], b1bc[:, :], ALU.add)
            g.drain()
            for j in range(2):
                residual(j, j)
            rsqrt(2)
            rsqrt(3)
            with g.Fori(1, NT // 2) as it:
                for r in range(2):
                    residual(it * 2 + r, r)
            meet(g, 1)
            pool_attention(g, 0)
            meet(g, 2)

            m = M[0]

            def average(i):
                for k in range(2):
                    mine = Oacc[:, ds(i * 2 + k, 1), :].rearrange("p o w -> p (o w)")
                    g.tensor_tensor(heads(ctxr[:, k, :], HD), values(mine),
                                    w8[:, ds(i * 2 + k, 1), :].rearrange("p o h -> p (o h)")
                                    .unsqueeze(2).broadcast_to([P, H, HD]), ALU.mult)
                    g.tensor_tensor(heads(tmpr[:, k, :], HD), heads(vmean[:, :], HD),
                                    e8[:, ds(i * 2 + k, 1), :].rearrange("p o h -> p (o h)")
                                    .unsqueeze(2).broadcast_to([P, H, HD]), ALU.mult)
                g.drain()
                g.tensor_tensor(ctxr[:, :, :], ctxr[:, :, :], tmpr[:, :, :], ALU.add
                                ).then_inc(m["ctx_ready"], 1)

            def rsqrt(count):
                g.wait_ge(m["ve_ready"], count)
                g.tensor_tensor(rstd[:, 0:2], ve[:, 0:2], nhalf[:, 0:2], ALU.pow
                                ).then_inc(m["rstd_ready"], 1)

            def residual(i):
                g.wait_ge(m["y_ready"], i + 1)
                g.tensor_tensor(yx[:, :, :], y[:, :, :], xs[:, ds(i * 2, 2), :], ALU.add
                                ).then_inc(m["yx_ready"], 1)

            g.wait_ge(m["w8_ready"], 1)
            average(0)
            g.wait_ge(m["ctxT_ready"], 1)
            average(1)
            g.memset(qrow[:, :, :], 0.0)
            g.drain()
            g.memset(qrow[:, :, 1:D:HD], 1.0)
            rsqrt(1)
            g.memset(krows[:, :, :], 0.0)
            g.drain()
            g.memset(krows[:, :, 0:D:HD], 1.0).then_inc(consts, 1)
            residual(0)
            rsqrt(2)
            with g.Fori(1, PAIRS - 1) as i:
                rsqrt(i * 2 + 1)
                average(i + 1)
                residual(i)
                rsqrt(i * 2 + 2)
            rsqrt(PAIRS * 2 - 1)
            residual(PAIRS - 1)
            rsqrt(PAIRS * 2)
            meet(g, 3)
            pool_attention(g, 1)
            meet(g, 4)
            m = M[1]
            g.wait_ge(m["w8_ready"], 1)

            def parts(i):
                for k in range(2):
                    j = ds(i * 2 + k, 1)
                    g.tensor_tensor(heads(krows[:, j, :].rearrange("p o d -> p (o d)"), HD),
                                    values(Oacc[:, j, :].rearrange("p o w -> p (o w)")),
                                    w8[:, j, :].rearrange("p o h -> p (o h)").unsqueeze(2)
                                    .broadcast_to([P, H, HD]), ALU.mult)
                    last = g.tensor_tensor(heads(mean_part(i * 2 + k), HD), heads(vmean[:, :], HD),
                                           e8[:, j, :].rearrange("p o h -> p (o h)")
                                           .unsqueeze(2).broadcast_to([P, H, HD]), ALU.mult)
                last.then_inc(m["parts_ready"], 1)

            def norm(i):
                pair = ds(i * 2, 2)
                wait_alone(g, m["ve_ready"], i + 1)
                g.tensor_tensor(rstd[:, pair], ve[:, pair], nhalf[:, 0:2], ALU.pow)
                g.drain()
                g.tensor_tensor(shift[:, pair], negmean[:, pair], rstd[:, pair], ALU.mult
                                ).then_inc(m["rstd_ready"], 1)

            for i in range(4):
                parts(i)
            with g.Fori(0, PAIRS - 4) as i:
                norm(i)
                parts(i + 4)
            for i in range(PAIRS - 4, PAIRS):
                norm(i)

        def act_attention(act, l):
            s = S[l]
            np_ = act.value_load(npair[0:1, 0:1], min_val=1, max_val=NU // 2)
            act.drain().then_inc(s["kt_done"], 1)
            act.drain().then_inc(s["exp_done"], 2)
            act.drain().then_inc(s["ea_done"], 1)
            act.drain().then_inc(s["pt_done"], 1)

            act.preload_act_table(ACT.Exp)

            def keys(u, r):
                act.wait_ge(s["kt_ready"], u + 3)
                act.wait_ge(s["s_ready"], u + 1)
                act.activation(KTs[r][:, :], pKT[:, 0:D], ACT.Copy).then_inc(s["kt_done"], 1)

            def slope(u, r):
                act.wait_ge(s["s_ready"], u + 3)
                act.wait_ge(s["s_free"], u + 2)
                act.activation(Y[:, :], pS[r][:, :], ACT.Copy, scale=SLOPE).then_inc(s["y_ready"], 1)

            def weights(u, r):
                act.wait_ge(s["z_ready"], u + 3)
                act.wait_ge(s["pt_ready"], u + 1)
                act.activation(Pr[r][:, :], Z[r][:, :], ACT.Exp).then_inc(s["exp_done"], 1)
                act.activation(ea[r][:, :], dm[r][:, :], ACT.Exp).then_inc(s["ea_done"], 1)

            def transposed(u, r):
                act.wait_ge(s["pt_ready"], u + 3)
                act.wait_ge(s["pv_done"], u + 1)
                act.activation(PTs[r][:, :], pPT[:, :], ACT.Copy).then_inc(s["pt_done"], 1)

            keys(0, 0)
            keys(1, 1)
            if l == 1:
                slope(0, 0)
                slope(1, 1)
            keys(2, 0)
            with act.Fori(0, np_) as p:
                for r in range(2):
                    u = p * 2 + r
                    weights(u, r)
                    if l == 1:
                        slope(u + 2, r)
                    keys(u + 3, 1 - r)
                    transposed(u, r)

        @block.scalar
        def _(act):
            def small(dst, src):
                act.dma_start(dst, src).then_inc(ld_small, 16)

            def late(dst, src):
                act.dma_start(dst, src).then_inc(ld_late, 16)

            small(s1c[:, :], ln1_sc)
            small(b1c[:, :], ln1_bc)
            small(bqc[:, :], bqc_d)
            small(nmi[:, :], nodemask.rearrange("(p a) -> p a", a=NT))
            small(bkv[:, 0:D], bcast(bk))
            small(bkv[:, D:2 * D], bcast(bv))
            small(s1bc[:, :], bcast(ln1_s))
            small(b1bc[:, :], bcast(ln1_b))
            small(bobc[:, :], bcast(bo))
            act.dma_start(wkv[:, :, 0:D], rows(Wk)).then_inc(ld_w, 16)
            act.dma_start(wkv[:, :, D:2 * D], rows(Wv)).then_inc(ld_w, 16)
            act.dma_start(wq[:, :, :], rows(Wq)).then_inc(ld_w, 16)
            late(bhc[:, :], Wbc)
            for q in range(4):
                late(acol[HD * q:HD * (q + 1), :], att_a)
            late(bh[:, 0:D], bcast(Wb))
            late(ww[:, :, :], rows(Ww))
            late(wwT[:, :, 0:D], rows(WwT))

            act.drain().then_inc(hT_ready, 2)
            act.drain().then_inc(q_done, 2)
            act.preload_act_table(ACT.Identity)

            def normalise(j, r):
                wait_alone(act, tx_ready, j + 1)
                wait_alone(act, ht_done, j + 1)
                for i, src in enumerate((xs, ht)):
                    last = act.activation(xn[r][:, i, :], src[:, ds(j, 1), :].rearrange("p o d -> p (o d)"),
                                          ACT.Identity, bias=shift[:, ds(j + i * NT, 1)],
                                          scale=rstd[:, ds(j + i * NT, 1)])
                last.then_inc(xn_ready, 1)

            def scale(j, r):
                act.wait_ge(tx_ready, j + 3)
                act.wait_ge(qp_ready, j + 1)
                for i in range(2):
                    for c in range(NC):
                        last = act.activation(
                            hT[r][:, i, c, :], pS[r][:, (2 * i + c) * P:(2 * i + c + 1) * P],
                            ACT.Identity, bias=b1c[:, c:c + 1], scale=s1c[:, c:c + 1])
                last.then_inc(hT_ready, 1)

            def queries(j, r):
                act.wait_ge(qp_ready, j + 3)
                for c in range(NC):
                    last = act.activation(
                        qT[:, ds(j, 1), c, :].rearrange("p o t -> p (o t)"),
                        (pKT, pO)[r][:, c * P:(c + 1) * P],
                        ACT.Identity, bias=bqc[:, c:c + 1], scale=float(HD) ** -0.5)
                last.then_inc(q_done, 1)

            act.wait_ge(rstd_ready, 2)
            for r in range(2):
                normalise(r, r)
            act.wait_ge(ld_small, SMALL)
            scale(0, 0)
            normalise(2, 0)
            act.wait_ge(dconsts, 1)

            def step(j, r):
                scale(j + 1, 1 - r)
                queries(j, r)

            with act.Fori(0, NT // 2 - 2) as it:
                for r in range(2):
                    step(it * 2 + r, r)
                    act.wait_ge(rstd_ready, len(NORM_PARTS))
                    normalise(it * 2 + (r + 3), 1 - r)
            step(NT - 4, 0)
            normalise(NT - 1, 1)
            step(NT - 3, 1)
            step(NT - 2, 0)
            queries(NT - 1, 1)
            meet(act, 1)
            act_attention(act, 0)
            meet(act, 2)
            m = M[0]
            act.preload_act_table(ACT.Gelu_apprx_tanh)

            def turned(i, src, dst, ready, done):
                act.wait_ge(m[ready], i + 1)
                act.activation(dst, src, ACT.Copy).then_inc(m[done], 1)

            def turned_ctx(i):
                turned(i, pS[0][:, 0:512], ctxT[:, :, :, :].rearrange("p k c t -> p (k c t)"),
                       "ctxT_ready", "ctxT_done")

            def turned_y(i):
                turned(i, pS[1][:, 0:512], yT[:, :, :, :].rearrange("p c k t -> p (c k t)"),
                       "yT_ready", "yT_done")

            def turned_x1(i):
                act.wait_ge(m["x1_ready"], i + 1)
                act.activation(xs[:, ds(i * 2, 2), :], x1s[:, :, :], ACT.Copy)
                turned(i, pKT[:, :], x1T[:, :, :, :].rearrange("p k c t -> p (k c t)"),
                       "x1T_ready", "x1T_done")

            def turned_q(i):
                turned(i, pKT[:, :], qT[:, ds(i * 2, 2), :, :].rearrange("p k c t -> p (k c t)"),
                       "qrT_ready", "qT_done")

            def gelu(i, part=range(NF // 2)):
                for f in part:
                    act.wait_ge(m["h1_ready"], i * (NF // 2) + (f + 1))
                    act.activation(h1[:, 2 * f:2 * f + 2, :].rearrange("p f t -> p (f t)"),
                                   (pS[1][:, 512:1024], pPT[:, 0:512])[f % 2],
                                   ACT.Gelu_apprx_tanh).then_inc(m["h1_done"], 1)

            act.drain().then_inc(m["qT_done"], 1)
            turned_ctx(0)
            turned_ctx(1)
            turned_y(0)
            gelu(0)
            turned_y(1)
            with act.Fori(1, PAIRS - 1) as i:
                gelu(i, range(NF // 2 - 1))
                turned_x1(i - 1)
                gelu(i, [NF // 2 - 1])
                turned_ctx(i + 1)
                turned_y(i + 1)
                turned_q(i - 1)
            gelu(PAIRS - 1, range(NF // 2 - 1))
            turned_x1(PAIRS - 2)
            gelu(PAIRS - 1, [NF // 2 - 1])
            turned_q(PAIRS - 2)
            turned_x1(PAIRS - 1)
            turned_q(PAIRS - 1)
            meet(act, 3)
            act_attention(act, 1)
            meet(act, 4)
            m = M[1]

            def exponentials(i):
                e = vrows[:, ds(i * 2, 2), 0:D]
                wait_alone(act, m["c_ready"], i + 1)
                act.activation(e, krows[:, ds(i * 2, 2), :], ACT.Relu, scale=-1.0
                               ).then_inc(m["relu_done"], 1)
                wait_alone(act, m["relu_done"], i + 1)
                act.activation(e, e, ACT.Exp, scale=-1.0).then_inc(m["exp_ready"], 1)

            def normalised(i):
                wait_alone(act, m["rstd_ready"], i + 1)
                for k in range(2):
                    j = i * 2 + k
                    last = act.activation(krows[:, ds(j, 1), :], ht[:, ds(j, 1), :], ACT.Identity,
                                          bias=shift[:, ds(j, 1)], scale=rstd[:, ds(j, 1)])
                last.then_inc(m["out_ready"], 1)

            exponentials(0)
            with act.Fori(0, PAIRS - 1) as i:
                exponentials(i + 1)
                normalised(i)
            normalised(PAIRS - 1)

        def vector_attention(v, l):
            s = S[l]
            np_ = v.value_load(npair[0:1, 0:1], min_val=1, max_val=NU // 2)
            v.drain().then_inc(s["mask_ready"], 2)
            v.drain().then_inc(s["s_free"], 2)
            v.drain().then_inc(s["z_ready"], 2)
            for r in range(2):
                last = v.memset(qz[r][:, :, :], 0.0)
            last.then_inc(s["q_clear"], 1)
            v.memset(macc[:, :, :], NEG)
            v.memset(Oacc[:, :, :], 0.0)
            for r in range(2):
                v.memset(ea[r][:, :], 1.0)
            v.memset(pO[:, 0:H * VW], 0.0)
            v.drain()

            def per_tile(a, j):
                return a[:, ds(j, 1), :].rearrange("p o w -> p (o w)")

            def mask(u, r, half):
                v.wait_ge(s[f"m_got{r}"], half * 16 + 16)
                v.wait_ge(s["s_ready"], u + 1)
                v.tensor_scalar(Mb[r][:, :], Mg[r][:, :], 0.0, uinv[r][:, 0:1], ALU.is_equal, ALU.max
                                ).then_inc(s["mask_ready"], 1)

            def leak(u, r):
                v.wait_ge(s["y_ready"], u + 1)
                v.wait_ge(s["exp_done"], u + 1)
                v.tensor_tensor(Z[r][:, :], pS[r][:, :], Y[:, :], ALU.max).then_inc(s["s_free"], 1)

            def add(u, j):
                mine = per_tile(Oacc, j)
                v.wait_ge(s["pv_done"], u + 3)
                v.tensor_tensor(mine, mine, pO[:, 0:H * VW], ALU.add).then_inc(s["merged"], 1)

            def rescale(u, r, j):
                mine = per_tile(Oacc, j)
                v.wait_ge(s["ea_done"], u + 2)
                v.tensor_tensor(heads(mine, VW), heads(mine, VW),
                                ea[r][:, :].unsqueeze(2).broadcast_to([P, H, VW]), ALU.mult)

            def step(p, r, tiles):
                u = p * 2 + r
                """Unit u's scores less the targets' running maximum, for the exponential."""
                scores = Z[r] if l else pS[r]
                v.wait_ge(s["s_free" if l else "s_ready"], u + 3)
                v.tensor_reduce(mu[:, :], heads(scores[:, :], P), AX.X, ALU.max)
                kept = per_tile(macc, tiles[2])
                v.tensor_copy(old[r][:, :], kept)
                v.drain()
                v.tensor_tensor(kept, mu[:, :], old[r][:, :], ALU.max)
                rescale(u - 2, r, tiles[0])
                v.drain()
                v.wait_ge(s["exp_done"], u + 1)
                v.tensor_tensor(dm[r][:, :], old[r][:, :], kept, ALU.subtract)
                v.tensor_tensor(heads(Z[r][:, :], P), heads(scores[:, :], P),
                                kept.unsqueeze(2).broadcast_to([P, H, P]), ALU.subtract
                                ).then_inc(s["z_ready"], 1)
                if r == 1:
                    v.load(ahead, tile4[0:1, ds(p + 1, 1), :].rearrange("o p f -> o (p f)"))
                add(u - 2, tiles[0])
                if l == 1:
                    leak(u + 1, 1 - r)

            mask(0, 0, 0)
            mask(1, 1, 0)
            if l == 1:
                leak(0, 0)
            ahead = [v.alloc_register(name=f"tile_ahead{l}{k}") for k in range(4)]
            v.load(ahead, tile4[0:1, 0, :])
            with v.Fori(0, np_) as p:
                tiles = [v.snap(a, min_val=0, max_val=NT - 1) for a in ahead]
                for r in range(2):
                    mask(p * 2 + (r + 2), r, p + 1)
                    step(p, r, tiles[r:r + 3])
            tiles = [v.snap(a, min_val=0, max_val=NT - 1) for a in ahead]
            for r in range(2):
                v.drain()
                rescale(np_ * 2 + (r - 2), r, tiles[r])
                v.drain()
                add(np_ * 2 + (r - 2), tiles[r])

        def averaging_weights(v, ready):
            sums = Oacc[:, :, :].rearrange("p j (h w) -> p j h w", w=VW)[:, :, :, HD]
            v.tensor_scalar(e8[:, :, :], macc[:, :, :], EMPTY, None, ALU.is_lt)
            v.drain()
            v.tensor_tensor(l8[:, :, :], e8[:, :, :], sums, ALU.add)
            v.tensor_scalar(w8[:, :, :], e8[:, :, :], -1.0, 1.0, ALU.mult, ALU.add)
            v.drain()
            v.reciprocal(l8[:, :, :], l8[:, :, :])
            v.drain()
            v.tensor_tensor(w8[:, :, :], w8[:, :, :], l8[:, :, :], ALU.mult).then_inc(ready, 1)

        def statistics(v, rows, ready):
            v.drain()
            for k in range(2):
                v.bn_stats(stats[:, k, :], rows[:, k, :])
            v.drain()
            for k in range(2):
                v.bn_aggr(mv[:, k, :], stats[:, k, :])
            v.drain()
            v.tensor_scalar(ve[:, 0:2], mv[:, 0:2, 1], EPS, None, ALU.add).then_inc(ready, 1)

        def between(v):
            m = M[0]

            def norm2(i, count):
                v.wait_ge(m["wo_ready"], i + 1)
                v.tensor_tensor(z[:, :, :], pS[0][:, 512:1024].rearrange("p (k d) -> p k d", k=2),
                                ht[:, ds(i * 2, 2), :], ALU.add)
                statistics(v, z, m["ve_ready"])
                v.wait_ge(m["rstd_ready"], count)
                for k in range(2):
                    v.tensor_scalar(y[:, k, :], z[:, k, :], mv[:, k, 0:1], rstd[:, k:k + 1],
                                    ALU.subtract, ALU.mult)
                v.drain()
                for k in range(2):
                    v.scalar_tensor_tensor(y[:, k, :], y[:, k, :], tm[:, ds(i * 2 + k, 1)],
                                           s2bc[:, :], ALU.mult, ALU.mult)
                v.drain()
                for k in range(2):
                    v.scalar_tensor_tensor(y[:, k, :], b2bc[:, :], tm[:, ds(i * 2 + k, 1)],
                                           y[:, k, :], ALU.mult, ALU.add)
                v.drain().then_inc(m["y_ready"], 1)

            def norm3(i, count):
                v.wait_ge(m["yx_ready"], i + 1)
                v.wait_ge(m["ff_ready"], i + 1)
                v.tensor_tensor(z[:, :, :], pPT[:, 512:1024].rearrange("p (k d) -> p k d", k=2),
                                yx[:, :, :], ALU.add)
                statistics(v, z, m["ve_ready"])
                v.wait_ge(m["rstd_ready"], count)
                for k in range(2):
                    v.tensor_scalar(x1s[:, k, :], z[:, k, :], mv[:, k, 0:1], rstd[:, k:k + 1],
                                    ALU.subtract, ALU.mult)
                v.drain().then_inc(m["x1_ready"], 1)

            def values_scores(i):
                for k in range(2):
                    v.wait_ge(m["h_ready"], i * 2 + (k + 1))
                    j, h = i * 2 + k, (pO, pS[1])[k]
                    v.tensor_tensor(values(vrows[:, ds(j, 1), :].rearrange("p o d -> p (o d)")),
                                    heads(h[:, 0:D], HD), heads(bh[:, 0:D], HD), ALU.add)
                    v.tensor_tensor(qrow[:, k, 0:D:HD], h[:, D:D + H], bh[:, D:D + H], ALU.add)
                    v.tensor_tensor(krows[:, ds(j, 1), 1:D:HD].rearrange("p o h -> p (o h)"),
                                    h[:, D + H:D + NS], bh[:, D + H:D + NS], ALU.add)
                    v.drain().then_inc(m["h_done"], 1)

            averaging_weights(v, m["w8_ready"])
            norm2(0, 1)
            v.wait_ge(m["yT_ready"], 1)
            norm2(1, 2)
            v.wait_ge(consts, 2)
            with v.Fori(1, PAIRS - 1) as i:
                norm3(i - 1, i * 2 + 1)
                values_scores(i - 1)
                norm2(i + 1, i * 2 + 2)
            norm3(PAIRS - 2, PAIRS * 2 - 1)
            values_scores(PAIRS - 2)
            norm3(PAIRS - 1, PAIRS * 2)
            values_scores(PAIRS - 1)
            v.wait_ge(vm_ready, 2)
            v.tensor_copy(vmean[:, :], pS[0][:, 0:D])

        def ending(v):
            m = M[1]

            def average(i):
                pair = krows[:, ds(i * 2, 2), :].rearrange("p k d -> p (k d)")
                v.wait_ge(m["parts_ready"], i + 1)
                v.tensor_tensor(pair, pair, qT[:, ds(i * 2, 2), :, :].rearrange("p k c t -> p (k c t)"),
                                ALU.add).then_inc(m["c_ready"], 1)

            def positive(i):
                v.scalar_tensor_tensor(ht[:, ds(i * 2, 2), :], krows[:, ds(i * 2, 2), :], 0.0,
                                       xs[:, ds(i * 2, 2), :], ALU.max, ALU.add)

            def negative(i):
                v.wait_ge(m["exp_ready"], i + 1)
                v.scalar_tensor_tensor(ht[:, ds(i * 2, 2), :], vrows[:, ds(i * 2, 2), 0:D], -1.0,
                                       ht[:, ds(i * 2, 2), :], ALU.add, ALU.add)

            def moments(i):
                for k in range(2):
                    v.bn_stats(stats[:, k, :], ht[:, ds(i * 2 + k, 1), :].rearrange("p o d -> p (o d)"))

            def gather_moments():
                for k in range(2):
                    v.bn_aggr(mv[:, k, :], stats[:, k, :])

            def hand_over(i):
                v.tensor_scalar(negmean[:, ds(i * 2, 2)], mv[:, 0:2, 0], -1.0, None, ALU.mult)
                v.tensor_scalar(ve[:, ds(i * 2, 2)], mv[:, 0:2, 1], EPS, None, ALU.add
                                ).then_inc(m["ve_ready"], 1)

            averaging_weights(v, m["w8_ready"])
            v.drain()
            average(0)
            v.drain()
            positive(0)
            average(1)
            v.drain()
            with v.Fori(0, PAIRS - 2) as i:
                negative(i)
                positive(i + 1)
                v.drain()
                moments(i)
                average(i + 2)
                v.drain()
                gather_moments()
                v.drain()
                hand_over(i)
            negative(PAIRS - 2)
            positive(PAIRS - 1)
            v.drain()
            moments(PAIRS - 2)
            v.drain()
            gather_moments()
            v.drain()
            hand_over(PAIRS - 2)
            negative(PAIRS - 1)
            v.drain()
            moments(PAIRS - 1)
            v.drain()
            gather_moments()
            v.drain()
            hand_over(PAIRS - 1)

        @block.vector
        def _(v):
            for n, (i, lo, hi) in enumerate(NORM_PARTS):
                v.wait_ge((ld_x, ld_h)[i][n // 2], 16)
                for n in range(lo, hi):
                    v.bn_stats(xstats[:, n, :], (xs, ht)[i][:, n % NT, :])
                v.drain()
                for n in range(lo, hi):
                    v.bn_aggr(mv[:, n, :], xstats[:, n, :])
                v.drain()
                v.tensor_scalar(negmean[:, lo:hi], mv[:, lo:hi, 0], -1.0, None, ALU.mult)
                v.tensor_scalar(ve[:, lo:hi], mv[:, lo:hi, 1], EPS, None, ALU.add
                                ).then_inc(ve_ready, 1)
            v.wait_ge(ld_small, SMALL)
            v.tensor_scalar(tm[:, :], nmi[:, :], 1.0, None, ALU.is_equal)
            v.tensor_scalar(bqc[:, :], bqc[:, :], float(HD) ** -0.5, None, ALU.mult)
            v.wait_ge(consts, 1)
            v.tensor_scalar(negi[:, :, :], identf[:, :].unsqueeze(1).broadcast_to([P, 4, P]), NEG,
                            None, ALU.mult)
            v.drain().then_inc(dconsts, 1)

            v.drain().then_inc(kv_done, 2)
            with v.Fori(0, NT // AR) as it:
                def edges(j, k):
                    v.wait_ge(adj_ld[k], it * 16 + 16)
                    v.tensor_reduce(anyf[:, ds(j * NT, NT)],
                                    adjb[k][:, :].rearrange("p (j a) -> p j a", a=P), AX.X, ALU.max,
                                    apply_absolute_value=True).then_inc(adj_used, 1)

                def keys_values(j, r):
                    v.wait_ge(kvp_ready, j + 1)
                    kvp = pPT[:, 512 * r:512 * r + 512]
                    v.scalar_tensor_tensor(krows[:, ds(j, 1), :].rearrange("p o d -> p (o d)"),
                                           kvp[:, 0:D], tm[:, ds(j, 1)], bkv[:, 0:D],
                                           ALU.mult, ALU.add)
                    v.scalar_tensor_tensor(values(vrows[:, ds(j, 1), :].rearrange("p o d -> p (o d)")),
                                           heads(kvp[:, D:2 * D], HD), tm[:, ds(j, 1)],
                                           heads(bkv[:, D:2 * D], HD),
                                           ALU.mult, ALU.add).then_inc(kv_done, 1)

                for k in range(AR):
                    edges(it * AR + k, k)
                    keys_values(it * AR + k, k % 2)
            v.drain()
            v.tensor_scalar(any16[:, :], anyf[:, :], 0.0, None, ALU.is_gt).then_inc(any_ready, 1)
            v.wait_ge(ld_late, LATE)
            for c in range(NC):
                for q in range(4):
                    rows = slice(HD * q, HD * q + HD)
                    for i in range(2):
                        h = i * H + 4 * c + q
                        v.tensor_copy(ablk[rows, c, h:h + 1], acol[rows, i:i + 1])
            v.tensor_copy(bhm[:, :, :], bhc[:, :].unsqueeze(2).broadcast_to([P, NC, P]))
            v.drain().then_inc(dconsts, 1)
            v.wait_ge(consts, 2)

            v.wait_ge(pos_ready, 1)
            v.scalar_tensor_tensor(place[:, :], pS[0][:, 512:512 + NU], 1.0, any16[:, :],
                                   ALU.add, ALU.mult)
            v.drain()
            v.tensor_scalar(placei[:, :], place[:, :], float(P - 1), None, ALU.add)
            v.drain()
            v.tensor_scalar(loi[:, :], placei[:, :], P - 1, None, ALU.bitwise_and)
            v.tensor_scalar(placei[:, :], placei[:, :], 7, None, ALU.logical_shift_right)
            v.drain()
            v.tensor_copy(lof[:, :], loi[:, :])
            v.tensor_copy(hif[:, :], placei[:, :])
            v.drain()
            for b in range(NT):
                last = v.scalar_tensor_tensor(pay[:, :, b], hif[:, :], float(b + 1), idp1[:, :],
                                              ALU.is_equal, ALU.mult)
            last.then_inc(pay_ready, 1)
            with v.Fori(0, NT // 2) as it:
                for r in range(2):
                    j = it * 2 + r
                    v.wait_ge(oh_used, j + 1)
                    v.tensor_tensor(oneh[r][:, :, :], ioc[:, :].unsqueeze(1).broadcast_to([P, NT, P]),
                                    lof[:, ds(j, NT, step=NT)].unsqueeze(2).broadcast_to([P, NT, P]),
                                    ALU.is_equal).then_inc(oh_ready, 1)
            v.tensor_scalar(nbf[:, :], pS[1][:, 512:512 + NT], float(P - 1), None, ALU.add)
            v.drain()
            v.tensor_copy(nbi[:, :], nbf[:, :])
            v.drain()
            v.tensor_scalar(nbi[:, :], nbi[:, :], 7, None, ALU.logical_shift_right)
            v.drain()
            v.tensor_copy(nbf[:, :], nbi[:, :])
            v.memset(tmp16[:, 0, :], 1.0)
            v.drain()
            v.tensor_tensor_scan(incl[:, :], tmp16[:, 0, :], nbf[:, :], 0.0, ALU.mult, ALU.add)
            v.drain()
            v.tensor_tensor(tmp16[:, 0, :], incl[:, :], identf[:, 0:NT], ALU.mult)
            v.tensor_tensor(tmp16[:, 1, :], nbf[:, :], identf[:, 0:NT], ALU.mult)
            v.drain()
            v.tensor_reduce(inclq[:, 0:2], tmp16[:, :, :], AX.X, ALU.add)
            v.memset(inclq[:, 2:3], 1.0)
            v.drain()
            v.tensor_scalar(done[:, :], iou[0:NT, :], inclq[0:NT, 0:1], None, ALU.is_ge
                            ).then_inc(done_ready, 1)

            v.wait_ge(idx_ready, 1)
            v.tensor_copy(node1[:, :], pPT[:, 0:NU])
            v.memset(srow[:, 0:1], 0)
            v.memset(mrow[:, 0:1], 0)
            v.memset(invalid[:, 0:1], 1.0)
            v.drain()
            v.tensor_scalar(invalid[:, 1:], node1[:, :], 0.0, None, ALU.is_equal)
            v.tensor_scalar(srcf[:, :], node1[:, :], -1.0, 0.0, ALU.add, ALU.max)
            v.drain()
            v.tensor_copy(srow[:, 1:], srcf[:, :])
            v.scalar_tensor_tensor(mrow[:, 1:], srcf[:, :], float(NT), ioh[:, :], ALU.mult, ALU.add)

            v.wait_ge(rows_ready, 1)
            tile_of, units_before = pKT[0:1, 0:NV], pO[0:1, 0:NV]
            v.scalar_tensor_tensor(t0[:, :], tile_of, float(NT), iou[0:1, :], ALU.mult, ALU.add)
            v.tensor_scalar(t1[:, :], iou[0:1, :], incl[0:1, NT - 1:NT], None, ALU.is_lt)
            v.tensor_scalar(t2[:, :], tile_of, float(NT - 1), None, ALU.min)
            v.drain()
            v.scalar_tensor_tensor(t0[:, :], t0[:, :], 1.0, units_before, ALU.add, ALU.subtract)
            v.memset(utile[:, 0:2], 0)
            v.tensor_copy(utile[:, 2:], t2[:, :])
            v.tensor_scalar(t3[:, :], incl[0:1, NT - 1:NT], 1.0, None, ALU.add)
            v.drain()
            v.tensor_tensor(ucol[:, :], t0[:, :], t1[:, :], ALU.mult)
            v.tensor_copy(npair[:, 1:2], t3[:, :])
            v.drain()
            v.tensor_copy(tile4[:, :, 0:2], utile[:, 0:NU + 2].rearrange("o (p f) -> o p f", f=2))
            v.tensor_copy(tile4[:, :, 2:4], utile[:, 2:NU + 4].rearrange("o (p f) -> o p f", f=2))
            v.tensor_copy(npair[:, 3:4], ucol[:, 0:1])
            v.tensor_copy(col4[:, :, 0:2], ucol[:, 1:NU + 1].rearrange("o (p f) -> o p f", f=2))
            v.tensor_copy(col4[:, :, 2:4], ucol[:, 4:NU + 4].rearrange("o (p f) -> o p f", f=2))
            v.tensor_scalar(npair[:, 2:3], npair[:, 1:2], 1, None, ALU.logical_shift_right)
            v.drain()
            v.tensor_scalar(npair[:, 0:1], npair[:, 2:3], 1.0, None, ALU.max)
            v.tensor_copy(npair[:, 1:2], ucol[:, 3:4])

            v.wait_ge(waug, 1)
            for c in range(NC):
                v.tensor_copy(wwT[:, c, D:D + NS], pPT[:, 512 + NS * c:512 + NS * (c + 1)])
            v.tensor_copy(bh[:, D:D + NS], pPT[:, 512 + 2 * NS:512 + 3 * NS])
            v.wait_ge(vm_ready, 1)
            v.tensor_copy(vmean[:, :], pS[0][:, 0:D])
            meet(v, 1)
            vector_attention(v, 0)
            meet(v, 2)
            between(v)
            meet(v, 3)
            vector_attention(v, 1)
            meet(v, 4)
            ending(v)

        def mean_values(pe, tiles=range(NT)):
            for j in tiles:
                last = pe.matmul(heads(pS[0][:, 0:D], HD), onesm[:, :], values(vrows[:, j, :]),
                                 start=(j == 0), stop=(j == NT - 1))
            if NT - 1 in tiles:
                last.then_inc(vm_ready, 1)

        def tensor_attention(pe, l):
            s = S[l]
            np_ = pe.value_load(npair[0:1, 0:1], min_val=1, max_val=NU // 2)
            pe.drain().then_inc(s["kt_ready"], 2)
            pe.drain().then_inc(s["s_ready"], 2)
            pe.drain().then_inc(s["pt_ready"], 2)
            pe.drain().then_inc(s["pv_done"], 1)

            def keys_there(u, r, half):
                pe.wait_ge(s[f"k_got{r}"], half * 16 + 16)
                pe.wait_ge(s["kt_done"], u + 1)

            def turn_keys(r):
                for c in range(NC):
                    last = pe.transpose(pKT[:, c * P:(c + 1) * P], Kg[r][:, c * P:(c + 1) * P],
                                        identf[:, :])
                last.then_inc(s["kt_ready"], 1)

            def scores(u, r, half):
                pe.wait_ge(s["kt_done"], u + 2)
                pe.wait_ge(s[f"q_got{r}"], half * 64 + 64)
                pe.wait_ge(s["mask_ready"], u + 3)
                pe.wait_ge(s["s_free" if l else "z_ready"], u + 1)
                for b in range(2):
                    pe.matmul(pS[r][:, 512 * b:512 * (b + 1)], Mb[r][:, :],
                              negi[:, :, :].rearrange("p f t -> p (f t)"), start=True, stop=False,
                              skip_group_check=True)
                for h in range(H):
                    last = pe.matmul(pS[r][:, h * P:(h + 1) * P], qz[r][:, h, :],
                                     KTs[r][:, (h // 4) * P:(h // 4 + 1) * P], start=False,
                                     stop=(h % 4 == 3), skip_group_check=True)
                last.then_inc(s["s_ready"], 1)

            def weights_there(u):
                pe.wait_ge(s["pt_done"], u + 1)
                pe.wait_ge(s["exp_done"], u + 3)

            def turn_weights(r):
                for h in range(H):
                    last = pe.transpose(pPT[:, h * P:(h + 1) * P], Pr[r][:, h * P:(h + 1) * P],
                                        identf[:, :])
                last.then_inc(s["pt_ready"], 1)

            def values_there(u, r, half):
                pe.wait_ge(s["pt_done"], u + 2)
                pe.wait_ge(s[f"v_got{r}"], half * 16 + 16)
                pe.wait_ge(s["merged"], u + 2)

            def weigh(r):
                for h in range(H):
                    last = pe.matmul(pO[:, h * VW:(h + 1) * VW], PTs[r][:, h * P:(h + 1) * P],
                                     Vg[r][:, h * VW:(h + 1) * VW], start=True, stop=True)
                last.then_inc(s["pv_done"], 1)

            for u in range(2):
                keys_there(u, u, 0)
                turn_keys(u)
                scores(u, u, 0)
            keys_there(2, 0, 1)
            turn_keys(0)
            with pe.Fori(0, np_) as p:
                for r in range(2):
                    u = p * 2 + r
                    scores(u + 2, r, p + 1)
                    keys_there(u + 3, 1 - r, p + (r + 1))
                    turn_keys(1 - r)
                    values_there(u - 1, 1 - r, p)
                    weights_there(u)
                    turn_weights(r)
                    weigh(1 - r)
            values_there(np_ * 2 - 1, 1, np_)
            weigh(1)

        def dense(pe):
            m = M[0]

            def turn(dst, rows, order, ready):
                for b, (k, c) in enumerate(order):
                    last = pe.transpose(dst[:, b * P:(b + 1) * P], rows[:, k, c * P:(c + 1) * P],
                                        identf[:, :])
                last.then_inc(ready, 1)

            by_tile = [(k, c) for k in range(2) for c in range(NC)]
            by_chunk = [(k, c) for c in range(NC) for k in range(2)]

            def turn_ctx(i):
                pe.wait_ge(m["ctx_ready"], i + 1)
                turn(pS[0], ctxr, by_tile, m["ctxT_ready"])

            def project_out(i):
                pe.wait_ge(m["ctxT_done"], i + 1)
                for k in range(2):
                    for c in range(NC):
                        last = pe.matmul(pS[0][:, 512 + D * k:512 + D * (k + 1)], ctxT[:, k, c, :],
                                         wo[:, c, :], start=(c == 0), stop=(c == NC - 1))
                last.then_inc(m["wo_ready"], 1)

            def turn_y(i):
                pe.wait_ge(m["y_ready"], i + 1)
                turn(pS[1], y, by_chunk, m["yT_ready"])

            def widen(i, part=range(NF)):
                pe.wait_ge(m["yT_done"], i + 1)
                for f in part:
                    if f % 2 == 0 and f >= 4:
                        pe.wait_ge(m["h1_done"], i * (NF // 2) + (f // 2 - 1))
                    bank = (pS[1][:, 512:1024], pPT[:, 0:512])[(f // 2) % 2]
                    for c in range(NC):
                        last = pe.matmul(bank[:, (f % 2) * 2 * P:(f % 2 + 1) * 2 * P],
                                         w1[:, c, f * P:(f + 1) * P],
                                         yT[:, c, :, :].rearrange("p k t -> p (k t)"),
                                         start=(c == 0), stop=(c == NC - 1))
                    if f % 2:
                        last.then_inc(m["h1_ready"], 1)

            def narrow(i, part=range(2 * NF)):
                pe.wait_ge(m["h1_done"], i * (NF // 2) + NF // 2)
                for k, f in [(n // NF, n % NF) for n in part]:
                    last = pe.matmul(pPT[:, 512 + D * k:512 + D * (k + 1)],
                                     h1[:, f, k * P:(k + 1) * P], w2[:, f, :],
                                     start=(f == 0), stop=(f == NF - 1))
                if 2 * NF - 1 in part:
                    last.then_inc(m["ff_ready"], 1)

            def turn_x1(i):
                pe.wait_ge(m["x1_ready"], i + 1)
                pe.wait_ge(m["qT_done"], i + 1)
                turn(pKT, x1s, by_tile, m["x1T_ready"])

            def project_values(i):
                pe.wait_ge(m["x1T_done"], i + 1)
                for k in range(2):
                    for c in range(NC):
                        last = pe.matmul((pO, pS[1])[k][:, 0:D + NS], x1T[:, k, c, :], wwT[:, c, :],
                                         start=(c == 0), stop=(c == NC - 1))
                    last.then_inc(m["h_ready"], 1)

            def turn_queries(i):
                pe.wait_ge(m["h_done"], i * 2 + 2)
                turn(pKT, qrow, by_tile, m["qrT_ready"])

            turn_ctx(0)
            project_out(0)
            turn_ctx(1)
            pe.wait_ge(m["ve_ready"], 1)
            project_out(1)
            turn_y(0)
            widen(0)
            narrow(0)
            turn_y(1)
            with pe.Fori(1, PAIRS - 1) as i:
                widen(i, range(NF - 2))
                turn_x1(i - 1)
                widen(i, range(NF - 2, NF))
                turn_ctx(i + 1)
                project_values(i - 1)
                project_out(i + 1)
                narrow(i, range(2 * NF - 2))
                pe.wait_ge(m["h_done"], i * 2)
                turn_y(i + 1)
                narrow(i, range(2 * NF - 2, 2 * NF))
                turn_queries(i - 1)
            widen(PAIRS - 1, range(NF - 2))
            turn_x1(PAIRS - 2)
            widen(PAIRS - 1, range(NF - 2, NF))
            project_values(PAIRS - 2)
            narrow(PAIRS - 1)
            turn_queries(PAIRS - 2)
            mean_values(pe, range(NT - 8))
            turn_x1(PAIRS - 1)
            mean_values(pe, range(NT - 8, NT - 6))
            project_values(PAIRS - 1)
            mean_values(pe, range(NT - 6, NT - 2))
            turn_queries(PAIRS - 1)
            mean_values(pe, range(NT - 2, NT))
            pe.wait_ge(m["qT_done"], PAIRS + 1)


        @block.tensor
        def _(pe):
            pe.drain().then_inc(tx_ready, 2)
            pe.drain().then_inc(qp_ready, 2)
            pe.wait_ge(consts, 1)
            pe.wait_ge(ld_w, 16 * 3)
            def turn(j, r):
                pe.wait_ge(xn_ready, j + 1)
                pe.wait_ge(hT_ready, j + 1)
                for i in range(2):
                    for c in range(NC):
                        last = pe.transpose(pS[r][:, (2 * i + c) * P:(2 * i + c + 1) * P],
                                            xn[r][:, i, c * P:(c + 1) * P], identf[:, :])
                last.then_inc(tx_ready, 1)

            def project(j, r):
                pe.wait_ge(hT_ready, j + 3)
                pe.wait_ge(kv_done, j + 1)
                for c in range(NC):
                    last = pe.matmul(pPT[:, 512 * r:512 * r + 512], hT[r][:, 0, c, :],
                                     wkv[:, c, :], start=(c == 0), stop=(c == NC - 1))
                last.then_inc(kvp_ready, 1)
                pe.wait_ge(q_done, j + 1)
                for f in range(NC):
                    for c in range(NC):
                        last = pe.matmul((pKT, pO)[r][:, f * P:(f + 1) * P],
                                         wq[:, c, f * P:(f + 1) * P], hT[r][:, 1, c, :],
                                         start=(c == 0), stop=(c == NC - 1))
                last.then_inc(qp_ready, 1)

            turn(0, 0)
            with pe.Fori(0, NT // 2 - 1) as it:
                for r in range(2):
                    turn(it * 2 + (r + 1), 1 - r)
                    project(it * 2 + r, r)
            turn(NT - 1, 1)
            project(NT - 2, 0)
            project(NT - 1, 1)

            pe.wait_ge(any_ready, 1)
            pe.wait_ge(hT_ready, NT + 2)
            pe.wait_ge(q_done, NT + 2)
            pe.wait_ge(kv_done, NT + 2)
            pe.matmul(pS[0][:, 512:512 + NU], before[:, :], any16[:, :], start=True, stop=False,
                      skip_group_check=True)
            for i in range(NT - 1):
                mine = any16[:, NT * i:NT * (i + 1)]
                last = pe.matmul(pS[0][:, 512 + NT * (i + 1):512 + NU].rearrange("p (n j) -> p n j", j=NT),
                                 ones16[:, :], mine.unsqueeze(1).broadcast_to([P, NT - 1 - i, NT]),
                                 start=False, stop=(i == NT - 2), skip_group_check=True)
            for i in range(NT):
                last = pe.matmul(pS[1][:, 512:512 + NT], ones16[:, :], any16[:, NT * i:NT * (i + 1)],
                                 start=(i == 0), stop=(i == NT - 1))
            last.then_inc(pos_ready, 1)
            pe.wait_ge(dconsts, 2)
            pe.wait_ge(ld_late, LATE)
            for c in range(NC):
                for o in range(NC):
                    pe.matmul(pPT[:, 512 + NS * c:512 + NS * (c + 1)], ww[:, o, c * P:(c + 1) * P],
                              ablk[:, o, :], start=(o == 0), stop=(o == NC - 1))
            for o in range(NC):
                last = pe.matmul(pPT[:, 512 + 2 * NS:512 + 3 * NS], bhm[:, o, :], ablk[:, o, :],
                                 start=(o == 0), stop=(o == NC - 1))
            last.then_inc(waug, 1)
            mean_values(pe)
            pe.drain().then_inc(oh_used, 2)
            pe.wait_ge(pay_ready, 1)
            with pe.Fori(0, NT // 2) as it:
                for r in range(2):
                    j = it * 2 + r
                    pe.wait_ge(oh_ready, j + 1)
                    for i in range(NT):
                        last = pe.matmul(pPT[:, ds(j * NT, NT)], oneh[r][:, i, :],
                                         pay[:, ds(j + i * NT, 1), :].rearrange("p o b -> p (o b)"),
                                         start=(i == 0), stop=(i == NT - 1))
                    last.then_inc(oh_used, 1)
            pe.drain().then_inc(idx_ready, 1)
            pe.wait_ge(done_ready, 1)
            pe.matmul(pKT[0:1, 0:NV], inclq[0:NT, 2:3], done[:, :], start=True, stop=True)
            pe.matmul(pO[0:1, 0:NV], inclq[0:NT, 1:2], done[:, :], start=True, stop=True
                      ).then_inc(rows_ready, 1)
            meet(pe, 1)
            tensor_attention(pe, 0)
            meet(pe, 2)
            dense(pe)
            meet(pe, 3)
            tensor_attention(pe, 1)
            meet(pe, 4)


def kernel(x, adj, nodemask, L0_gnn_h_target, L0_gnn_ln1_scale, L0_gnn_ln1_bias, L0_gnn_Wq,
           L0_gnn_bq, L0_gnn_Wk, L0_gnn_bk, L0_gnn_Wv, L0_gnn_bv, L0_gnn_Wo, L0_gnn_bo,
           L0_gnn_ln2_scale, L0_gnn_ln2_bias, L0_gnn_W1, L0_gnn_W2, L1_gnn_W_w, L1_gnn_W_b,
           L1_gnn_a):
    import numpy as np
    import concourse.bacc as bacc
    from concourse.bass_utils import run_bass_kernel_spmd

    def by_chunk(a, width):
        return np.asarray(a).reshape(-1, width).T

    adj_s = np.ascontiguousarray(
        np.asarray(adj).T.reshape(N, P, NT).transpose(0, 2, 1)).reshape(N * NT, P)
    host = dict(x=x, h_target=L0_gnn_h_target, adj_s=adj_s, nodemask=nodemask,
                ln1_s=L0_gnn_ln1_scale, ln1_b=L0_gnn_ln1_bias, Wq=L0_gnn_Wq,
                Wk=L0_gnn_Wk, bk=L0_gnn_bk, Wv=L0_gnn_Wv, bv=L0_gnn_bv, Wo=L0_gnn_Wo,
                bo=L0_gnn_bo, ln2_s=L0_gnn_ln2_scale, ln2_b=L0_gnn_ln2_bias, W1=L0_gnn_W1,
                W2=L0_gnn_W2, Ww=L1_gnn_W_w, WwT=np.asarray(L1_gnn_W_w).T, Wb=L1_gnn_W_b,
                ln1_sc=by_chunk(L0_gnn_ln1_scale, P), ln1_bc=by_chunk(L0_gnn_ln1_bias, P),
                bqc_d=by_chunk(L0_gnn_bq, P), Wbc=by_chunk(L1_gnn_W_b, P),
                att_a=by_chunk(L1_gnn_a, HD))
    host = {k: np.ascontiguousarray(a) for k, a in host.items()}
    nc = bacc.Bacc("TRN2", target_bir_lowering=False, num_devices=1)
    args = {k: nc.dram_tensor(f"in_{k}", a.shape, mybir.dt.from_np(a.dtype),
                              kind="ExternalInput").ap() for k, a in host.items()}
    args["out"] = nc.dram_tensor("out_0", (N, D), mybir.dt.float32, kind="ExternalOutput").ap()
    build(nc, **args)
    r = run_bass_kernel_spmd(nc, [{f"in_{k}": a for k, a in host.items()}], core_ids=[0])
    return r.results[0]["out_0"]
```
